# Optimizing a Trainium2 kernel written in Bass

```python
import numpy as np
import jax
import jax.numpy as jnp

def _softmax(x, axis=-1):
    return jax.nn.softmax(x, axis=axis)

def _gelu(x):
    return jax.nn.gelu(x, approximate=True)

def _silu(x):
    return jax.nn.silu(x)

def _sigmoid(x):
    return jax.nn.sigmoid(x)

def _layernorm(x, axis=-1, eps=1e-05):
    m = jnp.mean(x, axis=axis, keepdims=True)
    v = jnp.var(x, axis=axis, keepdims=True)
    return (x - m) / jnp.sqrt(v + eps)

def _scatter_add(tgt, idx, src, axis=0):
    return tgt.at[idx].add(src)

def _segment_sum(src, seg, n):
    return jax.ops.segment_sum(src, seg, n)
kernel_name = 'mk_seq_postln_d1_jaxref_r4_d1c03f'

def setup_inputs(seed: int=0):
    np.random.seed(seed)
    _w = jnp.asarray

    def _L0_attn_setup():
        import jax, jax.numpy as jnp
        import numpy as np
        B, S, HID = (2, 512, 512)
        NH, NG = (32, 8)
        HD = HID // NH
        KV = HD * NG
        key = jax.random.key(seed)
        ks = jax.random.split(key, 9)
        w = lambda k, shp: jax.random.normal(k, shp, dtype=jnp.float32) * 0.02
        return {'hidden_state': jax.random.normal(ks[0], (B, S, HID), dtype=jnp.float32), 'Wq': w(ks[1], (HID, HID)), 'bq': jnp.zeros((HID,), jnp.float32), 'Wk': w(ks[2], (HID, KV)), 'bk': jnp.zeros((KV,), jnp.float32), 'Wv': w(ks[3], (HID, KV)), 'bv': jnp.zeros((KV,), jnp.float32), 'Wo': w(ks[4], (HID, HID)), 'bo': jnp.zeros((HID,), jnp.float32)}
    _L0_attn_in = _L0_attn_setup()

    def _L0_ffn_setup():
        import jax, jax.numpy as jnp
        import numpy as np
        B, S, H = (1, 256, 512)
        I = 352
        E = 32
        K = 6
        G = 8
        TG = 3
        NSH = 2
        SCALE = 16.0
        C = 96

        def _moe_forward(x3, gate_w, w_gate_up, w_down, ws_gate_up, ws_down):
            b, s, h = x3.shape
            x = x3.reshape(-1, h)
            T = x.shape[0]
            logits = x @ gate_w.T
            grouped = logits.reshape(T, G, E // G)
            group_scores = jnp.max(grouped, axis=-1)
            _, group_idx = jax.lax.top_k(group_scores, TG)
            group_keep = jnp.zeros((T, G), bool).at[jnp.arange(T)[:, None], group_idx].set(True)
            masked = jnp.where(group_keep[..., None], grouped, 0.0)
            scores = masked.reshape(T, E)
            probs = jax.nn.softmax(scores.astype(jnp.float32), axis=-1)
            topk_w, topk_idx = jax.lax.top_k(probs, K)
            topk_w = topk_w * SCALE
            flat_e = topk_idx.reshape(-1)
            tok_idx = jnp.repeat(jnp.arange(T), K)
            oh = jax.nn.one_hot(flat_e, E, dtype=jnp.int32)
            pos = jnp.take_along_axis(jnp.cumsum(oh, axis=0) - 1, flat_e[:, None], axis=1)[:, 0]
            valid = pos < C
            slot = jnp.where(valid, flat_e * C + pos, E * C)
            buf = jnp.zeros((E * C + 1, h), x.dtype).at[slot].set(x[tok_idx])
            xb = buf[:E * C].reshape(E, C, h)
            gu = jnp.einsum('ech,ehf->ecf', xb, w_gate_up)
            g, u = jnp.split(gu, 2, axis=-1)
            act = jax.nn.silu(g) * u
            yb = jnp.einsum('eci,eih->ech', act, w_down)
            yflat = jnp.concatenate([yb.reshape(E * C, h), jnp.zeros((1, h), yb.dtype)], axis=0)
            y_pairs = yflat[slot].reshape(T, K, h)
            out = jnp.einsum('tk,tkh->th', topk_w.astype(x.dtype), y_pairs)
            gu_s = x @ ws_gate_up
            gs, us = jnp.split(gu_s, 2, axis=-1)
            out = out + jax.nn.silu(gs) * us @ ws_down
            return out.reshape(b, s, h)
        key = jax.random.key(seed)
        ks = jax.random.split(key, 6)
        s = 0.02
        return {'hidden_states': jax.random.normal(ks[0], (B, S, H), jnp.float32), 'gate_w': jax.random.normal(ks[1], (E, H), jnp.float32) * s, 'w_gate_up': jax.random.normal(ks[2], (E, H, 2 * I), jnp.float32) * s, 'w_down': jax.random.normal(ks[3], (E, I, H), jnp.float32) * s, 'ws_gate_up': jax.random.normal(ks[4], (H, 2 * I * NSH), jnp.float32) * s, 'ws_down': jax.random.normal(ks[5], (I * NSH, H), jnp.float32) * s}
    _L0_ffn_in = _L0_ffn_setup()
    _d = {'L0_attn_hidden_state': _L0_attn_in['hidden_state'], 'L0_attn_Wq': _L0_attn_in['Wq'], 'L0_attn_bq': _L0_attn_in['bq'], 'L0_attn_Wk': _L0_attn_in['Wk'], 'L0_attn_bk': _L0_attn_in['bk'], 'L0_attn_Wv': _L0_attn_in['Wv'], 'L0_attn_bv': _L0_attn_in['bv'], 'L0_attn_Wo': _L0_attn_in['Wo'], 'L0_attn_bo': _L0_attn_in['bo'], 'L0_ffn_gate_w': _L0_ffn_in['gate_w'], 'L0_ffn_w_gate_up': _L0_ffn_in['w_gate_up'], 'L0_ffn_w_down': _L0_ffn_in['w_down'], 'L0_ffn_ws_gate_up': _L0_ffn_in['ws_gate_up'], 'L0_ffn_ws_down': _L0_ffn_in['ws_down']}
    _x0 = _d['L0_attn_hidden_state']
    _d['L0_attn_hidden_state'] = jax.random.normal(jax.random.fold_in(jax.random.key(seed), 1), (2, 1024, 512), dtype=_x0.dtype)
    del _x0
    return _d

def reference(L0_attn_hidden_state, L0_attn_Wq, L0_attn_bq, L0_attn_Wk, L0_attn_bk, L0_attn_Wv, L0_attn_bv, L0_attn_Wo, L0_attn_bo, L0_ffn_gate_w, L0_ffn_w_gate_up, L0_ffn_w_down, L0_ffn_ws_gate_up, L0_ffn_ws_down):

    def _L0_attn_ref(hidden_state, Wq, bq, Wk, bk, Wv, bv, Wo, bo):
        import jax, jax.numpy as jnp
        import numpy as np
        B, S, HID = (2, 512, 512)
        NH, NG = (32, 8)
        HD = HID // NH
        KV = HD * NG
        bs, seq, _ = hidden_state.shape
        rep = NH // NG
        q = hidden_state @ Wq + bq
        k = hidden_state @ Wk + bk
        v = hidden_state @ Wv + bv
        q = q.reshape(bs, seq, NH, HD).transpose(0, 2, 1, 3)
        k = k.reshape(bs, seq, NG, HD).transpose(0, 2, 1, 3)
        v = v.reshape(bs, seq, NG, HD).transpose(0, 2, 1, 3)
        k = jnp.repeat(k, rep, axis=1)
        v = jnp.repeat(v, rep, axis=1)
        scores = jnp.einsum('bhqd,bhkd->bhqk', q, k) / jnp.sqrt(jnp.float32(HD))
        probs = jax.nn.softmax(scores, axis=-1)
        out = jnp.einsum('bhqk,bhkd->bhqd', probs, v)
        out = out.transpose(0, 2, 1, 3).reshape(bs, seq, HID)
        return out @ Wo + bo

    def _L0_ffn_ref(hidden_states, gate_w, w_gate_up, w_down, ws_gate_up, ws_down):
        import jax, jax.numpy as jnp
        import numpy as np
        B, S, H = (1, 256, 512)
        I = 352
        E = 32
        K = 6
        G = 8
        TG = 3
        NSH = 2
        SCALE = 16.0
        C = 96

        def _moe_forward(x3, gate_w, w_gate_up, w_down, ws_gate_up, ws_down):
            b, s, h = x3.shape
            x = x3.reshape(-1, h)
            T = x.shape[0]
            logits = x @ gate_w.T
            grouped = logits.reshape(T, G, E // G)
            group_scores = jnp.max(grouped, axis=-1)
            _, group_idx = jax.lax.top_k(group_scores, TG)
            group_keep = jnp.zeros((T, G), bool).at[jnp.arange(T)[:, None], group_idx].set(True)
            masked = jnp.where(group_keep[..., None], grouped, 0.0)
            scores = masked.reshape(T, E)
            probs = jax.nn.softmax(scores.astype(jnp.float32), axis=-1)
            topk_w, topk_idx = jax.lax.top_k(probs, K)
            topk_w = topk_w * SCALE
            flat_e = topk_idx.reshape(-1)
            tok_idx = jnp.repeat(jnp.arange(T), K)
            oh = jax.nn.one_hot(flat_e, E, dtype=jnp.int32)
            pos = jnp.take_along_axis(jnp.cumsum(oh, axis=0) - 1, flat_e[:, None], axis=1)[:, 0]
            valid = pos < C
            slot = jnp.where(valid, flat_e * C + pos, E * C)
            buf = jnp.zeros((E * C + 1, h), x.dtype).at[slot].set(x[tok_idx])
            xb = buf[:E * C].reshape(E, C, h)
            gu = jnp.einsum('ech,ehf->ecf', xb, w_gate_up)
            g, u = jnp.split(gu, 2, axis=-1)
            act = jax.nn.silu(g) * u
            yb = jnp.einsum('eci,eih->ech', act, w_down)
            yflat = jnp.concatenate([yb.reshape(E * C, h), jnp.zeros((1, h), yb.dtype)], axis=0)
            y_pairs = yflat[slot].reshape(T, K, h)
            out = jnp.einsum('tk,tkh->th', topk_w.astype(x.dtype), y_pairs)
            gu_s = x @ ws_gate_up
            gs, us = jnp.split(gu_s, 2, axis=-1)
            out = out + jax.nn.silu(gs) * us @ ws_down
            return out.reshape(b, s, h)
        return _moe_forward(hidden_states, gate_w, w_gate_up, w_down, ws_gate_up, ws_down)
    x = L0_attn_hidden_state
    x = _layernorm(x + _L0_attn_ref(x, L0_attn_Wq, L0_attn_bq, L0_attn_Wk, L0_attn_bk, L0_attn_Wv, L0_attn_bv, L0_attn_Wo, L0_attn_bo), axis=-1)
    x = _layernorm(x + _L0_ffn_ref(x, L0_ffn_gate_w, L0_ffn_w_gate_up, L0_ffn_w_down, L0_ffn_ws_gate_up, L0_ffn_ws_down), axis=-1)
    return x

_drawn_inputs = setup_inputs


def setup_inputs(seed=0):
    import zlib

    import numpy as np

    out = dict(_drawn_inputs(seed))
    spreads = {'L0_attn_bq': (0.0, 0.8),
     'L0_attn_bk': (0.0, 2.0),
     'L0_attn_bv': (0.0, 0.292),
     'L0_attn_bo': (0.0, 0.1)}
    factors = {'L0_attn_Wq': 8.0, 'L0_attn_Wk': 8.0, 'L0_attn_Wv': 7.626}
    for name, (base, spread) in spreads.items():
        noise = np.random.default_rng([zlib.crc32(name.encode()), seed]).standard_normal(out[name].shape)
        drawn = base * np.exp(spread * noise) if base else spread * noise
        out[name] = jnp.asarray(drawn.astype(out[name].dtype))
    for name, factor in factors.items():
        out[name] = (out[name] * factor).astype(out[name].dtype)
    return out
```

```python
from contextlib import ExitStack

import concourse.bass as bass
from concourse import mybir

F32 = mybir.dt.float32
BF16 = mybir.dt.bfloat16
I32 = mybir.dt.int32
U32 = mybir.dt.uint32
ALU = mybir.AluOpType
ACT = mybir.ActivationFunctionType
AX = mybir.AxisListType

P = 128
NB, SEQ, H = 2, 1024, 512
T = NB * SEQ
HC = H // P
NH, NG, HD = 32, 8, 16
REP = NH // NG
KV = NG * HD
UNITS = NB * NG
QT = SEQ // P
BLK = 512
NBLK = T // BLK
BT = BLK // P
TT = T // P
TERMS = [(0, 0), (0, 1), (1, 0), (1, 1), (0, 2), (2, 0)]
KR = HD * len(TERMS)
KM = KR + 3
STEPS = 2 * QT
S_TILES = [3, 2, 2, 2, 3, 2, 2, 2, 3, 2, 2, 2, 3, 2, 0, 0]
NS = REP * QT
E, K, G, TG = 32, 6, 8, 3
C = 96
SCALE = 16.0
I = 352
FT = [(0, 128), (128, 128), (256, 96)]
SI = 704
SFT = [(n * P, min(P, SI - n * P)) for n in range((SI + P - 1) // P)]
NSF = len(SFT)
SLOT_EXPERTS = 2
FIRST_TABLE_STEP = 4
EPS = 1e-5
XP = [2, 3, 2, 3]


def build(nc, x, Wq, bq, Wk, bk, Wv, bv, Wo, bo, gate_w, w_gate_up, w_down, ws_gate_up, ws_down, out):
    xf = x.rearrange("b s h -> (b s) h")
    of = out.rearrange("b s h -> (b s) h")
    q_parts = nc.dram_tensor("q_parts", (3, H, T), BF16).ap()
    k_parts = nc.dram_tensor("k_parts", (3, KV, T), BF16).ap()
    o_raw = nc.dram_tensor("o_raw", (UNITS, P, SEQ), F32).ap()
    x1_rows = nc.dram_tensor("x1_rows", (T, H), F32).ap()
    x1T_blocks = nc.dram_tensor("x1T_blocks", (NBLK, P, HC * BLK), F32).ap()
    total = nc.dram_tensor("total", (T + C, H), F32).ap()

    with ExitStack() as ctx:
        def sb(name, shape, dt, where=ctx):
            return where.enter_context(nc.sbuf_tensor(name, shape, dt))

        def sem(name):
            return ctx.enter_context(nc.semaphore(name))

        pair = [ctx.enter_context(nc.psum_tensor(f"pair{n}", [P, 1024], F32)) for n in range(4)]

        def bank(n):
            return pair[n // 2][:, (n % 2) * 512:(n % 2) * 512 + 512]

        ident = sb("ident", [P, P], F32)
        Wo_sb = sb("Wo_sb", [P, HC, H], F32)
        bo_bc = sb("bo_bc", [P, H], F32)
        gw_rows = sb("gw_rows", [E, H], F32)
        gwT = sb("gwT", [P, HC, E], F32)
        wsgu = sb("wsgu", [P, HC, 2 * SI], F32)
        wsd = sb("wsd", [P, NSF, H], F32)
        eps_col = sb("eps_col", [P, 1], F32)

        st1 = ExitStack()
        Wq_sb = sb("Wq_sb", [P, HC, H], F32, st1)
        Wk_sb = sb("Wk_sb", [P, HC, KV], F32, st1)
        Wv_sb = sb("Wv_sb", [P, HC, KV], F32, st1)
        bias_in = sb("bias_in", [P, HC + 1], F32, st1)
        bias_qk = sb("bias_qk", [P, HC + 1], F32, st1)
        bv_bc = sb("bv_bc", [P, KV], F32, st1)
        x_in = [sb(f"x_in{k}", [P, BT, H], F32, st1) for k in range(2)]
        xT = [sb(f"xT{k}", [P, HC, BLK], F32, st1) for k in range(2)]
        qk_full = [sb(f"qk_full{k}", [P, BLK], F32, st1) for k in range(2)]
        qk_rest = [sb(f"qk_rest{k}", [P, BLK], F32, st1) for k in range(2)]
        qk_split = [sb(f"qk_split{k}", [P, 3, BLK], BF16, st1) for k in range(2)]
        V_all = sb("V_all", [P, UNITS, QT, 32], F32, st1)
        V_unit = [sb(f"V_unit{k}", [P, QT, 32], F32, st1) for k in range(3)]
        Qa = [sb(f"Qa{k}", [KM, REP, SEQ], BF16, st1) for k in range(3)]
        Ka = [sb(f"Ka{k}", [KM, SEQ], BF16, st1) for k in range(3)]
        probs = [sb(f"probs{k}", [P, REP, BLK], F32, st1) for k in range(2)]
        rowmax = sb("rowmax", [P, NS], F32, st1)
        max_rest = sb("max_rest", [NS, P], F32, st1)
        max_split = sb("max_split", [NS, 3, P], BF16, st1)
        o_sb = [sb(f"o_sb{k}", [P, BLK], F32, st1) for k in range(2)]
        st1.close()

        st2 = ExitStack()
        logits = sb("logits", [P, TT, E], F32, st2)
        masked = sb("masked", [P, TT, E], F32, st2)
        gmax = sb("gmax", [P, TT, G], F32, st2)
        top8 = sb("top8", [P, TT, 8], F32, st2)
        r_gt = sb("r_gt", [P, TT, E], F32, st2)
        r_eq = sb("r_eq", [P, TT, E], F32, st2)
        r_cum = sb("r_cum", [P, TT, E], F32, st2)
        n_gt = sb("n_gt", [P, TT], F32, st2)
        keep_g = sb("keep_g", [P, TT, G], F32, st2)
        sel = sb("sel", [P, TT, E], F32, st2)
        sel_bf = sb("sel_bf", [P, TT, E], BF16, st2)
        seg8 = sb("seg8", [P, TT, G], F32, st2)
        seg16 = sb("seg16", [P, E, TT], F32, st2)
        seg32 = sb("seg32", [P, TT, E], F32, st2)
        zsum = sb("zsum", [P, TT], F32, st2)
        weight = sb("weight", [P, TT, E], F32, st2)
        tile_count = sb("tile_count", [P, E, TT], F32, st2)
        tile_cum = sb("tile_cum", [P, E, TT], F32, st2)
        slot_of = sb("slot_of", [P, E, TT], BF16, st2)
        before = sb("before", [P, P], BF16, st2)
        all_ones = sb("all_ones", [P, P], BF16, st2)
        iota_c = sb("iota_c", [P, TT, C], BF16, st2)
        facts = sb("facts", [P, E, TT, 6], BF16, st2)
        onehot = [sb(f"onehot{k}", [P, TT, C], BF16, st2) for k in range(2)]
        spare_row = sb("spare_row", [C, 1], F32, st2)
        table = sb("table", [C, E, 6], F32, st2)
        slot_w = sb("slot_w", [C, E], F32, st2)
        slot_src = sb("slot_src", [C, E], F32, st2)
        slot_src_i = sb("slot_src_i", [C, E], I32, st2)
        slot_dst_i = sb("slot_dst_i", [C, E], I32, st2)
        src_i = [sb(f"src_i{k}", [C, 1], I32, st2) for k in range(2)]
        dst_i = [sb(f"dst_i{k}", [C, 1], I32, st2) for k in range(2)]
        w_col = [sb(f"w_col{k}", [C, 1], F32, st2) for k in range(2)]
        wgu = [sb(f"wgu{k}", [P, HC, 2 * I], F32, st2) for k in range(2)]
        wd = [sb(f"wd{k}", [P, len(FT), H], F32, st2) for k in range(2)]
        xg = [sb(f"xg{k}", [C, H], F32, st2) for k in range(2)]
        xgT = [sb(f"xgT{k}", [P, HC, C], F32, st2) for k in range(2)]
        e_sig = [sb(f"e_sig{k}", [P, len(FT), C], F32, st2) for k in range(2)]
        e_hid = [sb(f"e_hid{k}", [P, len(FT), C], F32, st2) for k in range(2)]
        e_out = [sb(f"e_out{k}", [C, H], F32, st2) for k in range(2)]

        st3 = ExitStack()
        num = [sb(f"num{k}", [P, HC, BLK], F32, st3) for k in range(2)]
        den = sb("den", [P, HC, BLK], F32, st3)
        x_res = sb("x_res", [P, BT, H], F32, st3)
        pre1 = [sb(f"pre1_{k}", [P, H], F32, st3) for k in range(2)]
        stats1 = [sb(f"stats1_{k}", [P, 6], F32, st3) for k in range(2)]
        mv1 = [sb(f"mv1_{k}", [P, 2], F32, st3) for k in range(2)]
        std1 = [sb(f"std1_{k}", [P, 2], F32, st3) for k in range(2)]
        x1_out = [sb(f"x1_out{k}", [P, BT, H], F32, st3) for k in range(2)]
        x1T = [sb(f"x1T{k}", [P, HC, BLK], F32, st3) for k in range(2)]
        st3.close()
        st4 = ExitStack()
        sx = [sb(f"sx{k}", [P, HC, BLK], F32, st4) for k in range(2)]
        sx_rows = sb("sx_rows", [P, BT, H], F32, st4)
        s_sig = [sb(f"s_sig{k}", [P, BLK], F32, st4) for k in range(2)]
        s_hid = sb("s_hid", [P, NSF, BLK], F32, st4)
        s_sum = [sb(f"s_sum{k}", [P, BT, H], F32, st4) for k in range(2)]
        st4.close()
        st5 = ExitStack()
        f_in = [sb(f"f_in{k}", [P, BT, H], F32, st5) for k in range(2)]
        f_out = [sb(f"f_out{k}", [P, BT, H], F32, st5) for k in range(2)]
        stats2 = [sb(f"stats2_{k}", [P, 6], F32, st5) for k in range(2)]
        mv2 = [sb(f"mv2_{k}", [P, 2], F32, st5) for k in range(2)]
        std2 = [sb(f"std2_{k}", [P, 2], F32, st5) for k in range(2)]
        st5.close()
        st2.close()

        w_loaded = sem("w_loaded")
        w2_loaded = sem("w2_loaded")
        consts_made = sem("consts_made")
        ones_made = sem("ones_made")
        pool_step = sem("pool_step")
        bias_ready = sem("bias_ready")
        x_loaded = [sem(f"x_loaded{k}") for k in range(2)]
        x_turned = sem("x_turned")
        xT_act = sem("xT_act")
        xT_dve = sem("xT_dve")
        blk_projected = sem("blk_projected")
        job_done = sem("job_done")
        v_done = sem("v_done")
        v_kept = sem("v_kept")
        part1 = sem("part1")
        full_ready = sem("full_ready")
        rest_ready = sem("rest_ready")
        part2 = sem("part2")
        part3 = sem("part3")
        parts_stored = [sem(f"parts_stored{k}") for k in range(2)]
        gw_turned = sem("gw_turned")
        gw_ready = sem("gw_ready")
        qk_loaded = [sem(f"qk_loaded{k}") for k in range(3)]
        v_unit_ready = sem("v_unit_ready")
        s_ready = sem("s_ready")
        s_reduced = sem("s_reduced")
        max_turned = sem("max_turned")
        max1 = sem("max1")
        max_r = sem("max_r")
        max2 = sem("max2")
        max_ready = sem("max_ready")
        max_rows = sem("max_rows")
        st_ready = sem("st_ready")
        exp_done = sem("exp_done")
        pv_done = sem("pv_done")
        o_copied = sem("o_copied")
        o_stored = [sem(f"o_stored{k}") for k in range(2)]
        nd_loaded = [sem(f"nd_loaded{k}") for k in range(2)]
        res_loaded = sem("res_loaded")
        res_ready = sem("res_ready")
        den_inv = sem("den_inv")
        mix_in = sem("mix_in")
        y_done = sem("y_done")
        pre_done = sem("pre_done")
        stats_done = sem("stats_done")
        mv_done = sem("mv_done")
        std_done = sem("std_done")
        inv_done = sem("inv_done")
        x1_done = sem("x1_done")
        x1_turned = sem("x1_turned")
        x1T_kept = sem("x1T_kept")
        logit_done = sem("logit_done")
        logit_kept = sem("logit_kept")
        x1_stored = [sem(f"x1_stored{k}") for k in range(2)]
        x1T_stored = [sem(f"x1T_stored{k}") for k in range(2)]
        r_step = sem("r_step")
        r_consts = sem("r_consts")
        rp_step = sem("rp_step")
        r_diff = sem("r_diff")
        r_exp = sem("r_exp")
        sel_ready = sem("sel_ready")
        counts_done = sem("counts_done")
        pos_done = sem("pos_done")
        facts_ready = sem("facts_ready")
        hot_ready = sem("hot_ready")
        table_done = sem("table_done")
        table_kept = sem("table_kept")
        slots_ready = sem("slots_ready")
        sx_loaded = [sem(f"sx_loaded{k}") for k in range(2)]
        sx1_loaded = sem("sx1_loaded")
        s_gate = sem("s_gate")
        s_up = sem("s_up")
        s_silu = sem("s_silu")
        s_hidden = sem("s_hidden")
        s_down = sem("s_down")
        s_added = sem("s_added")
        s_stored = [sem(f"s_stored{k}") for k in range(2)]
        spare_zero = sem("spare_zero")
        spare_stored = sem("spare_stored")
        wgu_loaded = [sem(f"wgu_loaded{k}") for k in range(2)]
        wd_loaded = [sem(f"wd_loaded{k}") for k in range(2)]
        cols_ready = sem("cols_ready")
        gathered = [sem(f"gathered{k}") for k in range(2)]
        xg_turned = sem("xg_turned")
        xgT_ready = sem("xgT_ready")
        e_up = sem("e_up")
        e_silu = sem("e_silu")
        e_hidden = sem("e_hidden")
        e_down = sem("e_down")
        e_scaled = sem("e_scaled")
        scattered = sem("scattered")
        f_loaded = [sem(f"f_loaded{k}") for k in range(2)]
        f_stats = sem("f_stats")
        f_mv = sem("f_mv")
        f_std = sem("f_std")
        f_inv = sem("f_inv")
        f_done = sem("f_done")
        f_stored = [sem(f"f_stored{k}") for k in range(2)]

        waited = {e.engine: sem(f"waited_{n}") for n, e in (("pool", nc.gpsimd), ("dve", nc.vector), ("sp", nc.sync))}

        def settle(eng):
            eng.sem_inc(waited[eng.engine], 1)

        JOBS = HC + 1


        def project_sync(sp):
            sp.dma_start(x_in[0][:], xf[0:BLK, :].rearrange("(t p) h -> p t h", p=P)).then_inc(x_loaded[0], 16)
            for dst, src in ((Wq_sb, Wq), (Wk_sb, Wk), (Wv_sb, Wv)):
                sp.dma_start(dst[:], src.rearrange("(c p) n -> p c n", p=P)).then_inc(w_loaded, 16)
            with nc.allow_non_contiguous_dma(reason="biases as columns"):
                sp.dma_start(bias_in[:, 0:HC], bq.rearrange("(c p) -> p c", p=P)).then_inc(w_loaded, 16)
                sp.dma_start(bias_in[:, HC:HC + 1], bk.rearrange("(c p) -> p c", p=P)).then_inc(w_loaded, 16)
            sp.dma_start(bv_bc[:], bv.rearrange("(a n) -> a n", a=1).broadcast_to([P, KV])).then_inc(w_loaded, 16)
            sp.dma_start(x_in[1][:], xf[BLK:2 * BLK, :].rearrange("(t p) h -> p t h", p=P)).then_inc(x_loaded[1], 16)
            sp.dma_start(gw_rows[:], gate_w).then_inc(w2_loaded, 16)
            sp.dma_start(Wo_sb[:], Wo.rearrange("(c p) n -> p c n", p=P)).then_inc(w2_loaded, 16)
            sp.dma_start(bo_bc[:], bo.rearrange("(a n) -> a n", a=1).broadcast_to([P, H])).then_inc(w2_loaded, 16)
            sp.dma_start(wsgu[:], ws_gate_up.rearrange("(c p) n -> p c n", p=P)).then_inc(w2_loaded, 16)
            full = SI // P
            sp.dma_start(wsd[:, 0:full, :],
                         ws_down[0:full * P, :].rearrange("(c p) n -> p c n", p=P)).then_inc(w2_loaded, 16)
            sp.dma_start(wsd[0:SI - full * P, full, :], ws_down[full * P:SI, :]).then_inc(w2_loaded, 16)
            for blk in range(NBLK):
                for j in range(JOBS):
                    m = JOBS * blk + j
                    sp.wait_ge(part3, m + 1)
                    tok = slice(blk * BLK, (blk + 1) * BLK)
                    dst = q_parts[:, j * P:(j + 1) * P, tok] if j < HC else k_parts[:, :, tok]
                    sp.dma_start(dst.rearrange("s p n -> p s n"), qk_split[m % 2][:]).then_inc(parts_stored[m % 2], 16)
                if blk + 2 < NBLK:
                    sp.wait_ge(x_turned, HC * (blk + 1))
                    rows = xf[(blk + 2) * BLK:(blk + 3) * BLK, :]
                    sp.dma_start(x_in[blk % 2][:], rows.rearrange("(t p) h -> p t h", p=P)).then_inc(x_loaded[blk % 2], 16)

        def project_pool(pool):
            nc.gpsimd.memset(ident[:], 0.0).then_inc(pool_step, 1)
            pool.wait_ge(pool_step, 1)
            nc.gpsimd.affine_select(out=ident[:], in_=ident[:], compare_op=ALU.not_equal, fill=1.0, base=0,
                                    pattern=[[-1, P]], channel_multiplier=1).then_inc(consts_made, 1)
            pool.wait_ge(consts_made, 1)
            nc.gpsimd.memset(eps_col[:], EPS).then_inc(consts_made, 1)
            pool.wait_ge(consts_made, 2)
            for k in range(3):
                nc.gpsimd.memset(Ka[k][KR:KM, :], -1.0).then_inc(consts_made, 1)
                pool.wait_ge(consts_made, 3 + k)
            with pool.Fori(0, NB) as i:
                for m in range(2 * JOBS):
                    pool.wait_ge(rest_ready, 2 * JOBS * i + m + 3)
                    settle(pool)
                    nc.gpsimd.tensor_copy(qk_split[m % 2][:, 1, :], qk_rest[m % 2][:]).then_inc(part2, 1)

        def project_tensor(pe):
            pe.wait_ge(consts_made, 5)
            pe.wait_ge(w2_loaded, 96)
            for c in range(HC):
                last = nc.tensor.transpose(bank(7)[:, c * E:(c + 1) * E], gw_rows[:, c * P:(c + 1) * P], ident[0:E, 0:E])
            last.then_inc(gw_turned, 1)
            pe.wait_ge(w_loaded, 96)
            with pe.Fori(0, NB) as i:
                for k in range(2):
                    blk = 2 * i + k
                    pe.wait_ge(x_loaded[k], 16 * i + 16)
                    for c in range(HC):
                        pe.wait_ge(xT_act if c % 2 == 0 else xT_dve, 2 * blk + c // 2 + 1)
                        for t in range(BT):
                            last = nc.tensor.transpose(bank(c % 2)[:, t * P:(t + 1) * P],
                                                       x_in[k][:, t, c * P:(c + 1) * P], ident[:])
                        last.then_inc(x_turned, 1)
                    pe.wait_ge(xT_act, 2 * blk + 3)
                    pe.wait_ge(xT_dve, 2 * blk + 3)
                    for j in range(JOBS):
                        pe.wait_ge(full_ready, JOBS * blk + j + 1)
                        w = Wq_sb[:, :, j * P:(j + 1) * P] if j < HC else Wk_sb[:]
                        for c in range(HC):
                            last = nc.tensor.matmul(bank(2 + j), w[:, c, :], xT[k][:, c, :], start=(c == 0), stop=(c == HC - 1))
                        last.then_inc(job_done, 1)
                    pe.wait_ge(v_kept, blk + 1)
                    for t in range(BT):
                        for c in range(HC):
                            last = nc.tensor.matmul(bank(7)[:, t * P:(t + 1) * P], xT[k][:, c, t * P:(t + 1) * P],
                                                    Wv_sb[:, c, :], start=(c == 0), stop=(c == HC - 1))
                    last.then_inc(v_done, 1)

        def project_scalar(act):
            act.sem_inc(xT_act, 1)
            act.sem_inc(full_ready, JOBS)
            act.wait_ge(bias_ready, 2)
            with act.Fori(0, NB) as i:
                for k in range(2):
                    blk = 2 * i + k
                    for c in (0, 2):
                        act.wait_ge(x_turned, HC * blk + c + 1)
                        act.wait_ge(v_done, blk + 1)
                        nc.scalar.activation(xT[k][:, c, :], bank(0), ACT.Copy).then_inc(xT_act, 1)
                    for j in range(JOBS):
                        m = JOBS * k + j
                        act.wait_ge(job_done, JOBS * blk + j + 1)
                        act.wait_ge(rest_ready, JOBS * blk + j + 1)
                        nc.scalar.activation(qk_full[m % 2][:], bank(2 + j), ACT.Identity, bias=bias_qk[:, j:j + 1],
                                             scale=HD ** -0.5 if j < HC else 1.0).then_inc(full_ready, 1)
                        act.wait_ge(full_ready, JOBS * blk + j + JOBS + 1)
                        act.wait_ge(parts_stored[m % 2], 16 * JOBS * i + 16 * (m // 2) + 16)
                        nc.scalar.activation(qk_split[m % 2][:, 0, :], qk_full[m % 2][:], ACT.Copy).then_inc(part1, 1)

        def project_vector(dve):
            dve.sem_inc(xT_dve, 1)
            dve.sem_inc(rest_ready, 2)
            nc.vector.memset(V_all[:], 1.0).then_inc(ones_made, 1)
            dve.wait_ge(w_loaded, 96)
            nc.vector.tensor_scalar(bias_qk[:, 0:HC], bias_in[:, 0:HC], HD ** -0.5, None, ALU.mult).then_inc(bias_ready, 1)
            nc.vector.tensor_copy(bias_qk[:, HC:HC + 1], bias_in[:, HC:HC + 1]).then_inc(bias_ready, 1)
            dve.wait_ge(gw_turned, 1)
            nc.vector.tensor_copy(gwT[:], bank(7)[:, 0:HC * E].rearrange("p (c e) -> p c e", c=HC)).then_inc(gw_ready, 1)
            dve.wait_ge(gw_ready, 1)
            dve.sem_inc(v_kept, 1)
            dve.wait_ge(ones_made, 1)
            with dve.Fori(0, NB) as i:
                for k in range(2):
                    blk = 2 * i + k
                    for c in (1, 3):
                        dve.wait_ge(x_turned, HC * blk + c + 1)
                        dve.wait_ge(v_done, blk + 1)
                        nc.vector.tensor_copy(xT[k][:, c, :], bank(1)).then_inc(xT_dve, 1)
                    for j in range(JOBS):
                        m = JOBS * k + j
                        n = JOBS * blk + j
                        dve.wait_ge(part1, n + 1)
                        dve.wait_ge(full_ready, n + JOBS + 1)
                        nc.vector.tensor_tensor(qk_rest[m % 2][:], qk_full[m % 2][:], qk_split[m % 2][:, 0, :],
                                                ALU.subtract).then_inc(rest_ready, 1)
                        dve.wait_ge(rest_ready, n + 3)
                        dve.wait_ge(part2, n + 1)
                        nc.vector.tensor_tensor(qk_split[m % 2][:, 2, :], qk_rest[m % 2][:], qk_split[m % 2][:, 1, :],
                                                ALU.subtract).then_inc(part3, 1)
                    dve.wait_ge(v_done, blk + 3)
                    dst = V_all[:, bass.ds(i * NG, NG), k * BT:(k + 1) * BT, 0:HD].rearrange("p g t d -> p t g d")
                    nc.vector.tensor_tensor(dst, bank(7).rearrange("p (t g d) -> p t g d", t=BT, g=NG),
                                            bv_bc[:].rearrange("p (a g d) -> p a g d", a=1, g=NG).broadcast_to([P, BT, NG, HD]),
                                            ALU.add).then_inc(v_kept, 1)

        def load_unit(sp, u, buf):
            b, g = u // NG, u % NG
            for s, (kp, qp) in enumerate(TERMS):
                rows = slice(s * HD, (s + 1) * HD)
                sp.dma_start(Qa[buf][rows, :, :], q_parts[qp, bass.ds(g * REP * HD, REP * HD), bass.ds(b * SEQ, SEQ)]
                             .rearrange("(h d) n -> d h n", h=REP)).then_inc(qk_loaded[buf], 16)
                sp.dma_start(Ka[buf][rows, :], k_parts[kp, bass.ds(g * HD, HD), bass.ds(b * SEQ, SEQ)])\
                  .then_inc(qk_loaded[buf], 16)

        LOADS = 32 * len(TERMS)

        def by_units(eng, emit):
            emit(0, 0, 0)
            with eng.Fori(0, 4) as r:
                for j in range(3):
                    emit(3 * r + 1 + j, (1 + j) % 3, r + (1 + j) // 3)
            for u in range(13, UNITS):
                emit(u, u % 3, u // 3)

        def attend_sync(sp):
            for k in range(2):
                sp.wait_ge(parts_stored[k], 16 * (JOBS * NB + 1))
            load_unit(sp, 0, 0)
            load_unit(sp, 1, 1)

            def max_to_rows(u, buf):
                sp.wait_ge(max_ready, u + 1)
                for s in range(3):
                    sp.dma_start(Qa[buf][KR + s:KR + s + 1, :, :].rearrange("a h n -> a (h n)"),
                                 max_split[:, s, :]).then_inc(max_rows, 16)

            def store_o(u, qb):
                sp.wait_ge(o_copied, 2 * u + qb + 1)
                sp.dma_start(o_raw[u, :, qb * BLK:(qb + 1) * BLK] if isinstance(u, int) else
                             o_raw[bass.ds(u, 1), :, qb * BLK:(qb + 1) * BLK].rearrange("a p n -> (a p) n"),
                             o_sb[qb][:]).then_inc(o_stored[qb], 16)

            max_to_rows(0, 0)

            def emit(u, buf, _):
                first = isinstance(u, int) and u == 0
                tail = isinstance(u, int) and u >= UNITS - 2
                if not first:
                    store_o(u - 1, 1)
                if not tail:
                    if not first:
                        sp.wait_ge(st_ready, REP * STEPS * u)
                    load_unit(sp, u + 2, (buf + 2) % 3)
                store_o(u, 0)
                if not (isinstance(u, int) and u == UNITS - 1):
                    max_to_rows(u + 1, (buf + 1) % 3)

            by_units(sp, emit)
            store_o(UNITS - 1, 1)

        def attend_pool(pool):
            pool.wait_ge(v_kept, NBLK + 1)
            for u in range(3):
                nc.gpsimd.tensor_copy(V_unit[u][:], V_all[:, u, :, :]).then_inc(v_unit_ready, 1)
            with pool.Fori(1, 5) as r:
                for j in range(3):
                    u = 3 * r + j
                    pool.wait_ge(pv_done, STEPS * (u - 2))
                    settle(pool)
                    nc.gpsimd.tensor_copy(V_unit[j][:].rearrange("p t d -> p (t d)"),
                                          V_all[:, bass.ds(u, 1), :, :].rearrange("p a t d -> p (a t d)")).then_inc(v_unit_ready, 1)
            pool.wait_ge(pv_done, STEPS * (UNITS - 3))
            nc.gpsimd.tensor_copy(V_unit[0][:], V_all[:, UNITS - 1, :, :]).then_inc(v_unit_ready, 1)

        def score_tile(pe, u, buf, n, round_):
            first = isinstance(u, int) and u == 0
            if n == 0:
                pe.wait_ge(qk_loaded[buf], LOADS * (round_ + 1))
                if not first:
                    pe.wait_ge(max_ready, u)
            elif n == 1:
                if not first:
                    pe.wait_ge(s_reduced, NS * u)
            else:
                pe.wait_ge(s_reduced, NS * u + n - 1)
            h, qt = n // QT, n % QT
            for half in range(2):
                last = nc.tensor.matmul(pair[n % 2][:, half * 512:(half + 1) * 512], Qa[buf][0:KR, h, qt * P:(qt + 1) * P],
                                        Ka[buf][0:KR, half * 512:(half + 1) * 512], start=True, stop=True)
            last.then_inc(s_ready, 1)

        def turn_max(pe, u):
            pe.wait_ge(s_reduced, NS * u + NS)
            nc.tensor.transpose(pair[0][0:NS, 0:P], rowmax[:], ident[:]).then_inc(max_turned, 1)

        def attend_tensor(pe):
            pe.wait_ge(full_ready, JOBS * (NBLK + 1))
            pe.wait_ge(v_kept, NBLK + 1)
            for n in range(NS):
                score_tile(pe, 0, 0, n, 0)
            turn_max(pe, 0)

            def pv(u, s, buf):
                qb, kt = s // QT, s % QT
                pe.wait_ge(exp_done, REP * (STEPS * u + s + 1))
                if s == 0:
                    pe.wait_ge(v_unit_ready, u + 1)
                if kt == 0 and not (isinstance(u, int) and u == 0):
                    pe.wait_ge(o_copied, 2 * u + qb - 1)
                for h in range(REP):
                    last = nc.tensor.matmul(bank(6 + qb)[32 * h:32 * h + 32, :], V_unit[buf][:, kt, :],
                                            probs[s % 2][:, h, :], start=(kt == 0), stop=(kt == QT - 1),
                                            tile_position=(0, 32 * h))
                last.then_inc(pv_done, 1)

            def emit(u, buf, round_):
                first = isinstance(u, int) and u == 0
                final = isinstance(u, int) and u == UNITS - 1

                def st(s, h):
                    qb, kt = s // QT, s % QT
                    n = REP * s + h
                    if not (first and n < 2):
                        pe.wait_ge(exp_done, REP * STEPS * u + n - 1)
                    mm = nc.tensor.matmul(bank(4 + n % 2), Ka[buf][0:KM, kt * P:(kt + 1) * P],
                                          Qa[buf][0:KM, h, qb * BLK:(qb + 1) * BLK], start=True, stop=True)
                    mm.then_inc(st_ready, 1)

                pe.wait_ge(max_rows, 48 * u + 48)
                n = 0
                for s in range(STEPS):
                    st(s, 0)
                    st(s, 1)
                    if s > 0:
                        pv(u, s - 1, buf)
                    elif not first:
                        pv(u - 1, STEPS - 1, (buf + 2) % 3)
                    st(s, 2)
                    if not final:
                        for a in range(S_TILES[s]):
                            if a == 1:
                                st(s, 3)
                            score_tile(pe, u + 1, (buf + 1) % 3, n, (round_ + (buf + 1) // 3))
                            n += 1
                        if S_TILES[s] == 0:
                            st(s, 3)
                        if s == STEPS - 2:
                            turn_max(pe, u + 1)
                    else:
                        st(s, 3)

            by_units(pe, emit)
            pv(UNITS - 1, STEPS - 1, (UNITS - 1) % 3)

        def attend_vector(dve):
            def maxima(u):
                first = isinstance(u, int) and u == 0
                if not first:
                    dve.wait_ge(max_turned, u)
                for n in range(NS):
                    dve.wait_ge(s_ready, NS * u + n + 1)
                    nc.vector.tensor_reduce(rowmax[:, n:n + 1], pair[n % 2][:], AX.X, ALU.max).then_inc(s_reduced, 1)
                dve.wait_ge(max_turned, u + 1)
                if not first:
                    dve.wait_ge(max_rows, 48 * u)
                turned = pair[0][0:NS, 0:P]
                nc.vector.tensor_copy(max_split[:, 0, :], turned).then_inc(max1, 1)
                dve.wait_ge(max1, u + 1)
                nc.vector.tensor_tensor(max_rest[:], turned, max_split[:, 0, :], ALU.subtract).then_inc(max_r, 1)
                dve.wait_ge(max_r, u + 1)
                nc.vector.tensor_copy(max_split[:, 1, :], max_rest[:]).then_inc(max2, 1)
                dve.wait_ge(max2, u + 1)
                nc.vector.tensor_tensor(max_split[:, 2, :], max_rest[:], max_split[:, 1, :],
                                        ALU.subtract).then_inc(max_ready, 1)

            maxima(0)
            with dve.Fori(1, UNITS) as u:
                maxima(u)

        def attend_scalar(act):
            for qb in range(2):
                act.sem_inc(o_stored[qb], 16)

            def copy_o(u, qb):
                act.wait_ge(pv_done, STEPS * u + QT * (qb + 1))
                act.wait_ge(o_stored[qb], 16 * u + 16)
                nc.scalar.activation(o_sb[qb][:], bank(6 + qb), ACT.Copy).then_inc(o_copied, 1)

            def emit(u, first):
                for s in range(STEPS):
                    if not (first and s < 2):
                        act.wait_ge(pv_done, STEPS * u + s - 1)
                    for h in range(REP):
                        n = REP * s + h
                        act.wait_ge(st_ready, REP * STEPS * u + n + 1)
                        nc.scalar.activation(probs[s % 2][:, h, :], bank(4 + n % 2), ACT.Exp).then_inc(exp_done, 1)
                    if s == 1 and not first:
                        copy_o(u - 1, 1)
                    if s == QT + 1:
                        copy_o(u, 0)

            emit(0, True)
            with act.Fori(1, UNITS) as u:
                emit(u, False)
            copy_o(UNITS - 1, 1)

        def mix_sync(sp):
            for qb in range(2):
                sp.wait_ge(o_stored[qb], 16 * UNITS + 16)
            sp.wait_ge(pv_done, STEPS * UNITS)
            with sp.Fori(0, NB) as b:
                for k in range(2):
                    blk = 2 * b + k
                    sp.wait_ge(y_done, BT * blk + 1)
                    settle(sp)
                    sp.wait_ge(mix_in, blk + 1)
                    for c in range(HC):
                        for g2 in range(2):
                            u = NG * b + 2 * c + g2
                            o_unit = o_raw[bass.ds(u, 1), :, k * BLK:(k + 1) * BLK].rearrange("a (h r) n -> (a h) r n", h=REP)
                            for dst, r0 in ((num[k], 0), (den, HD)):
                                for h in range(REP):
                                    rows = slice(64 * g2 + HD * h, 64 * g2 + HD * (h + 1))
                                    sp.dma_start(dst[rows, c, :], o_unit[h, r0:r0 + HD, :]).then_inc(nd_loaded[k], 16)
                    sp.wait_ge(pre_done, BT * blk + BT)
                    sp.dma_start(x_res[:], xf[bass.ds(blk * BLK, BLK), :].rearrange("(t p) h -> p t h", p=P)).then_inc(res_loaded, 16)

        ND = 16 * HC * 2 * 2 * REP

        def mix_pool(pool):
            pool.sem_inc(mix_in, 1)
            with pool.Fori(0, NB) as b:
                for k in range(2):
                    blk = 2 * b + k
                    pool.wait_ge(res_loaded, 16 * blk + 16)
                    pool.wait_ge(w2_loaded, 96)
                    nc.gpsimd.tensor_tensor(x_res[:], x_res[:], bo_bc[:].rearrange("p (a h) -> p a h", a=1).broadcast_to([P, BT, H]),
                                            ALU.add).then_inc(res_ready, 1)
                    pool.wait_ge(nd_loaded[k], ND * b + ND)
                    pool.wait_ge(den_inv, blk + 1)
                    nc.gpsimd.tensor_tensor(num[k][:], num[k][:], den[:], ALU.mult).then_inc(mix_in, 1)

        def mix_tensor(pe):
            pe.sem_inc(y_done, 1)
            pe.wait_ge(o_copied, 2 * UNITS)
            pe.wait_ge(gw_ready, 1)

            def project_tile(blk, k, t):
                pe.wait_ge(pre_done, BT * blk + t + BT - 1)
                for c in range(HC):
                    last = nc.tensor.matmul(bank(t % 2), num[k][:, c, t * P:(t + 1) * P], Wo_sb[:, c, :],
                                            start=(c == 0), stop=(c == HC - 1))
                last.then_inc(y_done, 1)

            def turn_tile(blk, k, t):
                pe.wait_ge(x1_done, BT * blk + t + 1)
                pe.wait_ge(x1T_kept, BT * blk + t + 1)
                for c in range(HC):
                    last = nc.tensor.transpose(bank(2 + t % 2)[:, c * P:(c + 1) * P], x1_out[k][:, t, c * P:(c + 1) * P], ident[:])
                last.then_inc(x1_turned, 1)

            with pe.Fori(0, NB) as b:
                for k in range(2):
                    blk = 2 * b + k
                    pe.wait_ge(mix_in, blk + 2)
                    project_tile(blk, k, 0)
                    project_tile(blk, k, 1)
                    for t in range(BT):
                        turn_tile(blk, k, t)
                        if t + 2 < BT:
                            project_tile(blk, k, t + 2)
                    pe.wait_ge(x1T_kept, BT * blk + BT + 2)
                    pe.wait_ge(logit_kept, blk + 1)
                    for t in range(BT):
                        for c in range(HC):
                            last = nc.tensor.matmul(bank(4)[:, t * E:(t + 1) * E], x1T[k][:, c, t * P:(t + 1) * P],
                                                    gwT[:, c, :], start=(c == 0), stop=(c == HC - 1))
                    last.then_inc(logit_done, 1)

        def mix_vector(dve):
            dve.sem_inc(pre_done, BT)
            dve.sem_inc(logit_kept, 1)
            with dve.Fori(0, NB) as b:
                for k in range(2):
                    blk = 2 * b + k
                    dve.wait_ge(nd_loaded[k], ND * b + ND)
                    nc.vector.reciprocal(den[:], den[:]).then_inc(den_inv, 1)
                    dve.wait_ge(res_ready, blk + 1)
                    dve.wait_ge(x1_stored[k], 16 * b + 16)
                    for t in range(BT):
                        n = BT * blk + t
                        dve.wait_ge(y_done, n + 2)
                        nc.vector.tensor_tensor(pre1[t % 2][:], bank(t % 2), x_res[:, t, :], ALU.add).then_inc(pre_done, 1)
                        dve.wait_ge(pre_done, n + BT + 1)
                        nc.vector.bn_stats(stats1[t % 2][:], pre1[t % 2][:]).then_inc(stats_done, 1)
                        dve.wait_ge(stats_done, n + 1)
                        settle(dve)
                        nc.vector.bn_aggr(mv1[t % 2][:], stats1[t % 2][:]).then_inc(mv_done, 1)
                        dve.wait_ge(std_done, n + 1)
                        nc.vector.reciprocal(std1[t % 2][:, 1:2], std1[t % 2][:, 0:1]).then_inc(inv_done, 1)
                        dve.wait_ge(inv_done, n + 1)
                        nc.vector.tensor_scalar(x1_out[k][:, t, :], pre1[t % 2][:], mv1[t % 2][:, 0:1], std1[t % 2][:, 1:2],
                                                ALU.subtract, ALU.mult).then_inc(x1_done, 1)
                    dve.wait_ge(logit_done, blk + 1)
                    nc.vector.tensor_copy(logits[:, bass.ds(blk * BT, BT), :],
                                          bank(4)[:, 0:BT * E].rearrange("p (t e) -> p t e", t=BT)).then_inc(logit_kept, 1)

        def mix_scalar(act):
            act.sem_inc(x1T_kept, 2)
            for k in range(2):
                act.sem_inc(x1_stored[k], 16)
                act.sem_inc(x1T_stored[k], 16)
            act.wait_ge(consts_made, 5)
            with act.Fori(0, NB) as b:
                for k in range(2):
                    blk = 2 * b + k

                    def std(t):
                        n = BT * blk + t
                        act.wait_ge(mv_done, n + 1)
                        nc.scalar.activation(std1[t % 2][:, 0:1], mv1[t % 2][:, 1:2], ACT.Sqrt, bias=eps_col[:],
                                             scale=1.0).then_inc(std_done, 1)

                    def keep(t):
                        n = BT * blk + t
                        act.wait_ge(x1_turned, n + 1)
                        if t == 0:
                            act.wait_ge(x1T_stored[k], 16 * b + 16)
                        nc.scalar.activation(x1T[k][:, :, t * P:(t + 1) * P],
                                             bank(2 + t % 2).rearrange("p (c n) -> p c n", c=HC), ACT.Copy).then_inc(x1T_kept, 1)

                    std(0)
                    for t in range(BT):
                        if t + 1 < BT:
                            std(t + 1)
                        keep(t)
                    act.wait_ge(x1_done, BT * blk + BT)
                    act.dma_start(x1_rows[bass.ds(blk * BLK, BLK), :].rearrange("(t p) h -> p t h", p=P),
                                  x1_out[k][:]).then_inc(x1_stored[k], 16)
                    act.wait_ge(x1T_kept, BT * blk + BT + 2)
                    act.dma_start(x1T_blocks[bass.ds(blk, 1), :, :].rearrange("a p n -> (a p) n"),
                                  x1T[k][:].rearrange("p c n -> p (c n)")).then_inc(x1T_stored[k], 16)

        def route_pool(pool):
            pool.wait_ge(pv_done, STEPS * UNITS)
            pool.wait_ge(mix_in, NBLK + 1)
            nc.gpsimd.memset(seg8[:], 1.0).then_inc(rp_step, 1)
            nc.gpsimd.memset(seg32[:], 1.0).then_inc(rp_step, 1)
            nc.gpsimd.memset(seg16[:], 1.0).then_inc(rp_step, 1)
            nc.gpsimd.memset(all_ones[:], 1.0).then_inc(rp_step, 1)
            pool.wait_ge(rp_step, 4)
            nc.gpsimd.memset(seg8[:, :, 0:1], 0.0).then_inc(r_consts, 1)
            nc.gpsimd.memset(seg32[:, :, 0:1], 0.0).then_inc(r_consts, 1)
            nc.gpsimd.memset(seg16[:, :, 0:1], 0.0).then_inc(r_consts, 1)
            nc.gpsimd.affine_select(out=before[:], in_=all_ones[:], compare_op=ALU.is_gt, fill=0.0, base=0,
                                    pattern=[[1, P]], channel_multiplier=-1).then_inc(r_consts, 1)
            nc.gpsimd.iota(iota_c[:], pattern=[[0, TT], [1, C]], base=0, channel_multiplier=0,
                           allow_small_or_imprecise_dtypes=True).then_inc(r_consts, 1)
            nc.gpsimd.iota(facts[:, :, :, 0:1], pattern=[[0, E], [0, TT], [0, 1]], base=0, channel_multiplier=1,
                           allow_small_or_imprecise_dtypes=True).then_inc(r_consts, 1)
            nc.gpsimd.iota(facts[:, :, :, 1:2], pattern=[[0, E], [1, TT], [0, 1]], base=0, channel_multiplier=0,
                           allow_small_or_imprecise_dtypes=True).then_inc(r_consts, 1)
            nc.gpsimd.memset(facts[:, :, :, 5:6], 1.0).then_inc(r_consts, 1)
            nc.gpsimd.iota(spare_row[:], pattern=[[0, 1]], base=T, channel_multiplier=1,
                           allow_small_or_imprecise_dtypes=True).then_inc(r_consts, 1)
            nc.gpsimd.memset(e_out[0][:], 0.0).then_inc(spare_zero, 1)
            pool.wait_ge(spare_zero, 1)
            pool.dma_start(total[T:T + C, :], e_out[0][:]).then_inc(spare_stored, 16)

        def route_vector(dve):
            count = [0]

            def link(ins):
                count[0] += 1
                ins.then_inc(r_step, 1)
                dve.wait_ge(r_step, count[0])

            def bc(ap, n):
                return ap.rearrange("p (t a) -> p t a", a=1).broadcast_to([P, TT, n])

            def choose(dst, values, width, nth, seg):
                for t in range(TT):
                    last = nc.vector.max(out=top8[:, t, :], in_=values[:, t, :])
                link(last)
                thr = top8[:, :, nth - 1:nth].broadcast_to([P, TT, width])
                gt, eq, cum = r_gt[:, :, 0:width], r_eq[:, :, 0:width], r_cum[:, :, 0:width]
                if width < E:
                    flat = lambda x: x[:].rearrange("p t e -> p (t e)")[:, 0:TT * width].rearrange("p (t e) -> p t e", t=TT)
                    gt, eq, cum = flat(r_gt), flat(r_eq), flat(r_cum)
                link(nc.vector.tensor_tensor(gt, values[:], thr, ALU.is_gt))
                link(nc.vector.tensor_tensor(eq, values[:], thr, ALU.is_equal))
                link(nc.vector.tensor_reduce(n_gt[:], gt, AX.X, ALU.add))
                link(nc.vector.tensor_tensor_scan(cum.rearrange("p t e -> p (t e)"), seg[:].rearrange("p t e -> p (t e)"),
                                                  eq.rearrange("p t e -> p (t e)"), 0.0, ALU.mult, ALU.add))
                link(nc.vector.tensor_tensor(cum, cum, bc(n_gt[:], width), ALU.add))
                link(nc.vector.tensor_scalar(cum, cum, float(nth), None, ALU.is_le))
                link(nc.vector.tensor_tensor(cum, cum, eq, ALU.mult))
                link(nc.vector.tensor_tensor(dst, cum, gt, ALU.add))

            dve.wait_ge(logit_kept, NBLK + 1)
            dve.wait_ge(r_consts, 9)
            link(nc.vector.tensor_reduce(gmax[:].rearrange("p t g -> p (t g)"),
                                         logits[:].rearrange("p t (g e) -> p (t g) e", g=G), AX.X, ALU.max))
            choose(keep_g[:], gmax, G, TG, seg8)
            link(nc.vector.tensor_tensor(masked[:].rearrange("p t (g e) -> p (t g) e", g=G),
                                         logits[:].rearrange("p t (g e) -> p (t g) e", g=G),
                                         keep_g[:].rearrange("p t (g a) -> p (t g) a", a=1).broadcast_to([P, TT * G, E // G]),
                                         ALU.mult))
            choose(sel[:], masked, E, K, seg32)
            nc.vector.tensor_copy(sel_bf[:], sel[:]).then_inc(sel_ready, 1)
            link(nc.vector.tensor_tensor(masked[:], masked[:], top8[:, :, 0:1].broadcast_to([P, TT, E]), ALU.subtract))
            nc.vector.tensor_copy(r_eq[:, 0, 0:1], r_gt[:, 0, 0:1]).then_inc(r_diff, 1)
            dve.wait_ge(r_exp, 1)
            link(nc.vector.tensor_reduce(zsum[:], weight[:], AX.X, ALU.add))
            link(nc.vector.reciprocal(zsum[:], zsum[:]))
            link(nc.vector.tensor_tensor(weight[:], weight[:], bc(zsum[:], E), ALU.mult))
            link(nc.vector.scalar_tensor_tensor(out=weight[:], in0=weight[:], scalar=SCALE, in1=sel[:],
                                                op0=ALU.mult, op1=ALU.mult))
            wT = weight[:].rearrange("p t e -> p e t")
            restT = r_gt[:].rearrange("p t e -> p e t")
            link(nc.vector.tensor_copy(facts[:, :, :, 2], wT))
            link(nc.vector.tensor_tensor(restT, wT, facts[:, :, :, 2], ALU.subtract))
            link(nc.vector.tensor_copy(facts[:, :, :, 3], restT))
            link(nc.vector.tensor_tensor(facts[:, :, :, 4], restT, facts[:, :, :, 3], ALU.subtract))
            dve.wait_ge(counts_done, 1)
            cnt = bank(7).rearrange("p (t e) -> p e t", t=TT)
            link(nc.vector.tensor_copy(tile_count[:], cnt))
            link(nc.vector.tensor_tensor_scan(tile_cum[:].rearrange("p e t -> p (e t)"), seg16[:].rearrange("p e t -> p (e t)"),
                                              tile_count[:].rearrange("p e t -> p (e t)"), 0.0, ALU.mult, ALU.add))
            link(nc.vector.tensor_tensor(tile_cum[:], tile_cum[:], tile_count[:], ALU.subtract))
            dve.wait_ge(pos_done, 1)
            link(nc.vector.tensor_tensor(tile_cum[:], bank(6).rearrange("p (t e) -> p e t", t=TT), tile_cum[:], ALU.add))
            link(nc.vector.scalar_tensor_tensor(out=tile_cum[:], in0=tile_cum[:], scalar=1.0,
                                                in1=sel[:].rearrange("p t e -> p e t"), op0=ALU.add, op1=ALU.mult))
            nc.vector.tensor_scalar(slot_of[:], tile_cum[:], -1.0, None, ALU.add).then_inc(facts_ready, 1)
            dve.wait_ge(facts_ready, 1)

        def route_scalar(act):
            act.wait_ge(r_diff, 1)
            act.wait_ge(r_step, 20)
            nc.scalar.activation(weight[:], masked[:], ACT.Exp).then_inc(r_exp, 1)

        def route_tensor(pe):
            pe.wait_ge(sel_ready, 1)
            chosen = sel_bf[:].rearrange("p t e -> p (t e)")
            nc.tensor.matmul(bank(7), all_ones[:], chosen, start=True, stop=True).then_inc(counts_done, 1)
            nc.tensor.matmul(bank(6), before[:], chosen, start=True, stop=True).then_inc(pos_done, 1)
            pe.wait_ge(facts_ready, 1)

        def shared_sync(sp):
            sp.wait_ge(logit_done, NBLK)
            sp.wait_ge(x1_done, TT)
            for k in range(2):
                sp.wait_ge(x1_stored[k], 16 * (NB + 1))
                sp.wait_ge(x1T_stored[k], 16 * (NB + 1))
            for e in range(2):
                load_wgu(sp, e, e)
                load_wd(sp, e, e)
            with sp.Fori(0, NB) as b:
                for k in range(2):
                    blk = 2 * b + k
                    sp.wait_ge(s_up, NSF * blk + 1)
                    sp.dma_start(sx[k][:].rearrange("p c n -> p (c n)"),
                                 x1T_blocks[bass.ds(blk, 1), :, :].rearrange("a p n -> (a p) n")).then_inc(sx_loaded[k], 16)
                    sp.wait_ge(s_added, BT * blk + BT)
                    sp.dma_start(sx_rows[:], x1_rows[bass.ds(blk * BLK, BLK), :].rearrange("(t p) h -> p t h", p=P))\
                      .then_inc(sx1_loaded, 16)

        def shared_tensor(pe):
            pe.sem_inc(s_up, 2 * NSF)
            pe.wait_ge(x1T_kept, TT + 2)
            pe.wait_ge(pre_done, TT + BT)
            with pe.Fori(0, NB) as b:
                for k in range(2):
                    blk = 2 * b + k
                    pe.wait_ge(sx_loaded[k], 16 * b + 16)
                    for f, (f0, fn) in enumerate(SFT):
                        pe.wait_ge(s_hidden, NSF * blk + f + 1)
                        for dst, off, done in ((bank(f % 2), 0, s_gate), (bank(2 + f % 2), SI, s_up)):
                            for c in range(HC):
                                last = nc.tensor.matmul(dst[0:fn, :], wsgu[:, c, off + f0:off + f0 + fn], sx[k][:, c, :],
                                                        start=(c == 0), stop=(c == HC - 1))
                            last.then_inc(done, 1)
                        step = k * NSF + f
                        if FIRST_TABLE_STEP <= step:
                            for a in range(SLOT_EXPERTS):
                                slot_table(pe, b, SLOT_EXPERTS * (step - FIRST_TABLE_STEP) + a)
                    pe.wait_ge(s_hidden, NSF * blk + NSF + 2)
                    for t in range(BT):
                        pe.wait_ge(s_added, BT * blk + t + BT - 1)
                        for f, (f0, fn) in enumerate(SFT):
                            last = nc.tensor.matmul(bank(4 + t % 2), s_hid[0:fn, f, t * P:(t + 1) * P], wsd[0:fn, f, :],
                                                    start=(f == 0), stop=(f == NSF - 1))
                        last.then_inc(s_down, 1)

        def slot_table(pe, b, n):
            pe.wait_ge(hot_ready, (E // 2) * b + n + 1)
            if n == 0:
                pe.wait_ge(table_kept, b + 1)
            for t in range(TT):
                last = nc.tensor.matmul(bank(6)[0:C, 6 * n:6 * n + 6], onehot[n % 2][:, t, :],
                                        facts[:, bass.ds((E // 2) * b + n, 1), t:t + 1, :].rearrange("p a t s -> p (a t s)"),
                                        start=(t == 0), stop=(t == TT - 1))
            last.then_inc(table_done, 1)

        def onehots(eng, b, n):
            eng.wait_ge(table_done, (E // 2) * b + n + 1)
            col = slot_of[:, bass.ds((E // 2) * b + n, 1), :].rearrange("p a (t c) -> p (a t) c", c=1)
            nc.vector.tensor_tensor(onehot[n % 2][:], iota_c[:], col.broadcast_to([P, TT, C]), ALU.is_equal)\
              .then_inc(hot_ready, 1)

        def shared_scalar(act):
            with act.Fori(0, NB) as b:
                for k in range(2):
                    blk = 2 * b + k
                    for f, (f0, fn) in enumerate(SFT):
                        act.wait_ge(s_gate, NSF * blk + f + 1)
                        act.wait_ge(s_hidden, NSF * blk + f + 1)
                        nc.scalar.activation(s_sig[f % 2][0:fn, :], bank(f % 2)[0:fn, :], ACT.Silu).then_inc(s_silu, 1)
                    act.wait_ge(s_added, BT * blk + 2 * BT)
                    act.dma_start(total[bass.ds(blk * BLK, BLK), :].rearrange("(t p) h -> p t h", p=P),
                                  s_sum[k][:]).then_inc(s_stored[k], 16)

        def shared_vector(dve):
            dve.sem_inc(s_hidden, 2)
            dve.sem_inc(s_added, BT)
            dve.sem_inc(table_kept, 1)
            for k in range(2):
                dve.sem_inc(s_stored[k], 16)
            with dve.Fori(0, NB) as b:
                for k in range(2):
                    blk = 2 * b + k
                    for f, (f0, fn) in enumerate(SFT):
                        step = k * NSF + f
                        if FIRST_TABLE_STEP - 1 <= step < 2 * NSF - 1:
                            for a in range(SLOT_EXPERTS):
                                onehots(dve, b, SLOT_EXPERTS * (step - FIRST_TABLE_STEP + 1) + a)
                        dve.wait_ge(s_silu, NSF * blk + f + 1)
                        dve.wait_ge(s_up, NSF * blk + f + 2 * NSF + 1)
                        if f == 0:
                            dve.wait_ge(s_down, BT * blk + BT)
                        nc.vector.tensor_tensor(s_hid[0:fn, f, :], s_sig[f % 2][0:fn, :], bank(2 + f % 2)[0:fn, :],
                                                ALU.mult).then_inc(s_hidden, 1)
                    dve.wait_ge(sx1_loaded, 16 * blk + 16)
                    dve.wait_ge(s_stored[k], 16 * b + 16)
                    for t in range(BT):
                        dve.wait_ge(s_down, BT * blk + t + BT + 1)
                        nc.vector.tensor_tensor(s_sum[k][:, t, :], bank(4 + t % 2), sx_rows[:, t, :], ALU.add).then_inc(s_added, 1)
                dve.wait_ge(table_done, (E // 2) * b + E // 2 + 2)
                nc.vector.tensor_copy(table[:, bass.ds((E // 2) * b, E // 2), :],
                                      bank(6)[0:C, 0:3 * E].rearrange("p (e s) -> p e s", s=6)).then_inc(table_kept, 1)
            count = [0]

            def link(ins):
                count[0] += 1
                ins.then_inc(slots_ready, 1)
                dve.wait_ge(slots_ready, count[0])

            dve.wait_ge(table_kept, NB + 1)
            link(nc.vector.tensor_tensor(slot_w[:], table[:, :, 2], table[:, :, 3], ALU.add))
            link(nc.vector.tensor_tensor(slot_w[:], slot_w[:], table[:, :, 4], ALU.add))
            link(nc.vector.scalar_tensor_tensor(out=slot_src[:], in0=table[:, :, 1], scalar=float(P), in1=table[:, :, 0],
                                                op0=ALU.mult, op1=ALU.add))
            link(nc.vector.tensor_copy(slot_src_i[:], slot_src[:]))
            link(nc.vector.tensor_scalar(table[:, :, 5], table[:, :, 5], -1.0, 1.0, ALU.mult, ALU.add))
            link(nc.vector.scalar_tensor_tensor(out=slot_src[:], in0=table[:, :, 5], scalar=spare_row[:, 0:1], in1=slot_src[:],
                                                op0=ALU.mult, op1=ALU.add))
            link(nc.vector.tensor_copy(slot_dst_i[:], slot_src[:]))

        SLOT_STEPS = 7

        def load_wgu(sp, e, k):
            src = w_gate_up[e] if isinstance(e, int) else w_gate_up[bass.ds(e, 1), :, :].rearrange("a k n -> (a k) n")
            sp.dma_start(wgu[k][:], src.rearrange("(c p) n -> p c n", p=P)).then_inc(wgu_loaded[k], 16)

        def load_wd(sp, e, k):
            src = w_down[e] if isinstance(e, int) else w_down[bass.ds(e, 1), :, :].rearrange("a k n -> (a k) n")
            sp.dma_start(wd[k][:, 0:2, :], src[0:2 * P, :].rearrange("(c p) n -> p c n", p=P)).then_inc(wd_loaded[k], 16)
            sp.dma_start(wd[k][0:FT[2][1], 2, :], src[2 * P:I, :]).then_inc(wd_loaded[k], 16)

        def experts_sync(sp):
            with sp.Fori(1, E // 2) as r:
                for k in range(2):
                    e = 2 * r + k
                    sp.wait_ge(e_up, e - 1)
                    load_wgu(sp, e, k)
                    sp.wait_ge(e_down, e - 1)
                    load_wd(sp, e, k)

        def experts_pool(pool):
            pool.wait_ge(slots_ready, SLOT_STEPS)
            for k in range(2):
                pool.wait_ge(s_stored[k], 16 * (NB + 1))
            pool.wait_ge(spare_stored, 16)

            def fetch(e, k, before_):
                col = (lambda a: a[:, e:e + 1]) if isinstance(e, int) else (lambda a: a[:, bass.ds(e, 1)])
                if before_:
                    pool.wait_ge(e_scaled, e - 1)
                    pool.wait_ge(scattered, 16 * (e - 1))
                    pool.wait_ge(xg_turned, e - 1)
                settle(pool)
                nc.gpsimd.tensor_copy(src_i[k][:], col(slot_src_i)).then_inc(cols_ready, 1)
                nc.gpsimd.tensor_copy(dst_i[k][:], col(slot_dst_i)).then_inc(cols_ready, 1)
                nc.gpsimd.tensor_copy(w_col[k][:], col(slot_w)).then_inc(cols_ready, 1)
                pool.wait_ge(cols_ready, 3 * e + 3)
                settle(pool)
                pool.indirect_dma_start(xg[k][:], None, x1_rows, bass.IndirectOffsetOnAxis(ap=src_i[k][:, 0:1], axis=0))\
                    .then_inc(gathered[k], 16)

            def add(e, k, before_):
                pool.wait_ge(e_scaled, e + 1)
                if before_:
                    pool.wait_ge(scattered, 16 * e)
                settle(pool)
                pool.indirect_dma_start(total, bass.IndirectOffsetOnAxis(ap=dst_i[k][:, 0:1], axis=0), e_out[k][:], None,
                                        compute_op=ALU.add).then_inc(scattered, 16)

            fetch(0, 0, False)
            fetch(1, 1, False)
            add(0, 0, False)
            with pool.Fori(1, E // 2) as r:
                for k in range(2):
                    e = 2 * r + k
                    fetch(e, k, True)
                    add(e - 1, 1 - k, True)
            add(E - 1, 1, True)

        def experts_tensor(pe):
            pe.wait_ge(s_added, TT + BT)
            pe.wait_ge(s_hidden, NSF * NBLK + 2)
            pe.wait_ge(table_kept, NB + 1)

            def up(e, k, round_, warm):
                pe.wait_ge(gathered[k], 16 * (round_ + 1))
                if warm:
                    pe.wait_ge(xgT_ready, e)
                for c in range(HC):
                    last = nc.tensor.transpose(bank(0)[:, c * C:(c + 1) * C], xg[k][:, c * P:(c + 1) * P], ident[0:C, 0:C])
                last.then_inc(xg_turned, 1)
                pe.wait_ge(xgT_ready, e + 1)
                pe.wait_ge(wgu_loaded[k], 16 * (round_ + 1))
                if warm > 1:
                    pe.wait_ge(e_hidden, 2 * (e - 1))
                for b0, off in ((1 + k, 0), (3 + k, I)):
                    for f, (f0, fn) in enumerate(FT):
                        for c in range(HC):
                            last = nc.tensor.matmul(bank(b0)[0:fn, f * C:(f + 1) * C], wgu[k][:, c, off + f0:off + f0 + fn],
                                                    xgT[k][:, c, :], start=(c == 0), stop=(c == HC - 1))
                last.then_inc(e_up, 1)

            def down(e, k, round_, warm):
                pe.wait_ge(e_hidden, 2 * (e + 1))
                pe.wait_ge(wd_loaded[k], 32 * (round_ + 1))
                if warm:
                    pe.wait_ge(e_scaled, e - 1)
                for f, (f0, fn) in enumerate(FT):
                    last = nc.tensor.matmul(bank(5 + k)[0:C, :], e_hid[k][0:fn, f, :], wd[k][0:fn, f, :],
                                            start=(f == 0), stop=(f == len(FT) - 1))
                last.then_inc(e_down, 1)

            up(0, 0, 0, 0)
            up(1, 1, 0, 1)
            down(0, 0, 0, 0)
            up(2, 0, 1, 2)
            down(1, 1, 0, 0)
            with pe.Fori(1, E // 2 - 1) as r:
                for k in range(2):
                    e = 2 * r + k
                    up(e + 1, 1 - k, r + k, 2)
                    down(e, k, r, 2)
            up(E - 1, 1, E // 2 - 1, 2)
            down(E - 2, 0, E // 2 - 1, 2)
            down(E - 1, 1, E // 2 - 1, 2)

        def experts_scalar(act):
            def emit(e, k, warm):
                act.wait_ge(xg_turned, e + 1)
                if warm:
                    act.wait_ge(e_up, e - 1)
                nc.scalar.activation(xgT[k][:], bank(0)[:, 0:HC * C].rearrange("p (c n) -> p c n", c=HC), ACT.Copy)\
                  .then_inc(xgT_ready, 1)
                act.wait_ge(e_up, e + 1)
                if warm:
                    act.wait_ge(e_hidden, 2 * (e - 1))
                nc.scalar.activation(e_sig[k][:, 0:2, :], bank(1 + k)[:, 0:2 * C].rearrange("p (f n) -> p f n", f=2),
                                     ACT.Silu).then_inc(e_silu, 1)
                nc.scalar.activation(e_sig[k][0:FT[2][1], 2, :], bank(1 + k)[0:FT[2][1], 2 * C:3 * C], ACT.Silu).then_inc(e_silu, 1)

            for e in range(2):
                emit(e, e, False)
            with act.Fori(1, E // 2) as r:
                for k in range(2):
                    emit(2 * r + k, k, True)

        def experts_vector(dve):
            def emit(e, k, warm):
                dve.wait_ge(e_silu, 2 * e + 2)
                if warm:
                    dve.wait_ge(e_down, e - 1)
                nc.vector.tensor_tensor(e_hid[k][:, 0:2, :], e_sig[k][:, 0:2, :],
                                        bank(3 + k)[:, 0:2 * C].rearrange("p (f n) -> p f n", f=2), ALU.mult).then_inc(e_hidden, 1)
                nc.vector.tensor_tensor(e_hid[k][0:FT[2][1], 2, :], e_sig[k][0:FT[2][1], 2, :],
                                        bank(3 + k)[0:FT[2][1], 2 * C:3 * C], ALU.mult).then_inc(e_hidden, 1)

            def scale(e, k, warm):
                dve.wait_ge(e_down, e + 1)
                dve.wait_ge(cols_ready, 3 * e + 3)
                if warm:
                    dve.wait_ge(scattered, 16 * (e - 1))
                nc.vector.tensor_scalar(e_out[k][:], bank(5 + k)[0:C, :], w_col[k][:, 0:1], None, ALU.mult).then_inc(e_scaled, 1)

            dve.wait_ge(spare_stored, 16)
            emit(0, 0, False)
            emit(1, 1, False)
            scale(0, 0, False)
            emit(2, 0, True)
            scale(1, 1, False)
            with dve.Fori(1, E // 2 - 1) as r:
                for k in range(2):
                    e = 2 * r + k
                    emit(e + 1, 1 - k, True)
                    scale(e, k, True)
            emit(E - 1, 1, True)
            scale(E - 2, 0, True)
            scale(E - 1, 1, True)

        def finish_sync(sp):
            sp.wait_ge(scattered, 16 * E)
            sp.wait_ge(s_added, TT + BT)
            with sp.Fori(0, NB) as b:
                for k in range(2):
                    sp.wait_ge(f_done, 2 * BT * b + BT * k + BT)
                    rows = bass.ds((2 * b + k) * BLK, BLK)
                    sp.dma_start(f_in[k][:], total[rows, :].rearrange("(t p) h -> p t h", p=P)).then_inc(f_loaded[k], 16)
            for k in range(2):
                sp.wait_ge(f_stored[k], 16 * (NB + 1))

        def finish_vector(dve):
            with dve.Fori(0, NB) as b:
                for k in range(2):
                    dve.wait_ge(f_loaded[k], 16 * b + 16)
                    dve.wait_ge(f_stored[k], 16 * b + 16)

                    def stats(t):
                        n = BT * (2 * b + k) + t
                        nc.vector.bn_stats(stats2[t % 2][:], f_in[k][:, t, :]).then_inc(f_stats, 1)
                        dve.wait_ge(f_stats, n + 1)
                        settle(dve)
                        nc.vector.bn_aggr(mv2[t % 2][:], stats2[t % 2][:]).then_inc(f_mv, 1)

                    stats(0)
                    for t in range(BT):
                        n = BT * (2 * b + k) + t
                        if t + 1 < BT:
                            stats(t + 1)
                        dve.wait_ge(f_std, n + 1)
                        nc.vector.reciprocal(std2[t % 2][:, 1:2], std2[t % 2][:, 0:1]).then_inc(f_inv, 1)
                        dve.wait_ge(f_inv, n + 1)
                        nc.vector.tensor_scalar(f_out[k][:, t, :], f_in[k][:, t, :], mv2[t % 2][:, 0:1], std2[t % 2][:, 1:2],
                                                ALU.subtract, ALU.mult).then_inc(f_done, 1)

        def finish_scalar(act):
            for k in range(2):
                act.sem_inc(f_stored[k], 16)
            with act.Fori(0, NB) as b:
                for k in range(2):
                    for t in range(BT):
                        act.wait_ge(f_mv, BT * (2 * b + k) + t + 1)
                        nc.scalar.activation(std2[t % 2][:, 0:1], mv2[t % 2][:, 1:2], ACT.Sqrt, bias=eps_col[:],
                                             scale=1.0).then_inc(f_std, 1)
                    act.wait_ge(f_done, 2 * BT * b + BT * k + 3 * BT)
                    rows = bass.ds((2 * b + k) * BLK, BLK)
                    act.dma_start(of[rows, :].rearrange("(t p) h -> p t h", p=P), f_out[k][:]).then_inc(f_stored[k], 16)

        block = ctx.enter_context(nc.Block())

        @block.sync
        def _(sp):
            project_sync(sp)
            attend_sync(sp)
            mix_sync(sp)
            shared_sync(sp)
            experts_sync(sp)
            finish_sync(sp)

        @block.gpsimd
        def _(pool):
            project_pool(pool)
            attend_pool(pool)
            mix_pool(pool)
            route_pool(pool)
            experts_pool(pool)

        @block.tensor
        def _(pe):
            pe.sem_inc(v_done, 2)
            project_tensor(pe)
            attend_tensor(pe)
            mix_tensor(pe)
            route_tensor(pe)
            pe.sem_inc(s_down, BT)
            pe.sem_inc(table_done, 2)
            shared_tensor(pe)
            experts_tensor(pe)

        @block.scalar
        def _(act):
            for k in range(2):
                act.sem_inc(parts_stored[k], 16)
            project_scalar(act)
            attend_scalar(act)
            mix_scalar(act)
            route_scalar(act)
            shared_scalar(act)
            experts_scalar(act)
            finish_scalar(act)

        @block.vector
        def _(dve):
            project_vector(dve)
            attend_vector(dve)
            mix_vector(dve)
            route_vector(dve)
            shared_vector(dve)
            experts_vector(dve)
            dve.sem_inc(f_done, 2 * BT)
            finish_vector(dve)


_INS = ["L0_attn_hidden_state", "L0_attn_Wq", "L0_attn_bq", "L0_attn_Wk", "L0_attn_bk", "L0_attn_Wv", "L0_attn_bv",
        "L0_attn_Wo", "L0_attn_bo", "L0_ffn_gate_w", "L0_ffn_w_gate_up", "L0_ffn_w_down", "L0_ffn_ws_gate_up",
        "L0_ffn_ws_down"]


def kernel(**inputs):
    import numpy as np
    import concourse.bacc as bacc
    from concourse.bass_utils import run_bass_kernel_spmd as run

    nc = bacc.Bacc("TRN2", target_bir_lowering=False, num_devices=1)
    arrays, args = {}, []
    for name in _INS:
        a = np.ascontiguousarray(inputs[name])
        arrays[f"in_{name}"] = a
        args.append(nc.dram_tensor(f"in_{name}", a.shape, mybir.dt.from_np(a.dtype), kind="ExternalInput").ap())
    args.append(nc.dram_tensor("out_0", (NB, SEQ, H), F32, kind="ExternalOutput").ap())
    build(nc, *args)
    return run(nc, [arrays], core_ids=[0]).results[0]["out_0"]
```

```python
from contextlib import ExitStack

import concourse.bass as bass
from concourse import mybir

F32 = mybir.dt.float32
BF16 = mybir.dt.bfloat16
I32 = mybir.dt.int32
U32 = mybir.dt.uint32
ALU = mybir.AluOpType
ACT = mybir.ActivationFunctionType
AX = mybir.AxisListType

P = 128
NB, SEQ, H = 2, 1024, 512
T = NB * SEQ
HC = H // P
NH, NG, HD = 32, 8, 16
REP = NH // NG
KV = NG * HD
UNITS = NB * NG
QT = SEQ // P
BLK = 512
NBLK = T // BLK
BT = BLK // P
TT = T // P
TERMS = [(0, 0), (0, 1), (1, 0), (1, 1), (0, 2), (2, 0)]
KR = HD * len(TERMS)
KM = KR + 3
STEPS = 2 * QT
S_PER_STEP = 2
NS = REP * QT // 2
LEAD = 12
E, K, G, TG = 32, 6, 8, 3
C = 96
SCALE = 16.0
I = 352
FT = [(0, 128), (128, 128), (256, 96)]
SI = 704
SFT = [(n * P, min(P, SI - n * P)) for n in range((SI + P - 1) // P)]
NSF = len(SFT)
SLOT_EXPERTS = 2
FIRST_TABLE_STEP = 4
EPS = 1e-5
ROOM1, ROOM3 = 2048, 256
GR = 4


def build(nc, x, Wq, bq, Wk, bk, Wv, bv, Wo, bo, gate_w, w_gate_up, w_down, ws_gate_up, ws_down, out):
    xf = x.rearrange("b s h -> (b s) h")
    of = out.rearrange("b s h -> (b s) h")
    q_parts = nc.dram_tensor("q_parts", (3, H, T), BF16).ap()
    k_parts = nc.dram_tensor("k_parts", (3, KV, T), BF16).ap()
    o_raw = nc.dram_tensor("o_raw", (UNITS, P, SEQ), F32).ap()
    inv_den = nc.dram_tensor("inv_den", (NB * NH, SEQ), F32).ap()
    x1_rows = nc.dram_tensor("x1_rows", (T, H), F32).ap()
    x1T_blocks = nc.dram_tensor("x1T_blocks", (NBLK, P, HC * BLK), F32).ap()
    total = nc.dram_tensor("total", (T + C, H), F32).ap()

    with ExitStack() as ctx:
        def sb(name, shape, dt, where=ctx):
            return where.enter_context(nc.sbuf_tensor(name, shape, dt))

        def sem(name):
            return ctx.enter_context(nc.semaphore(name))

        pair = [ctx.enter_context(nc.psum_tensor(f"pair{n}", [P, 1024], F32)) for n in range(4)]

        def bank(n):
            return pair[n // 2][:, (n % 2) * 512:(n % 2) * 512 + 512]

        ident = sb("ident", [P, P], F32)
        Wo_sb = sb("Wo_sb", [P, HC, H], F32)
        bo_bc = sb("bo_bc", [P, H], F32)
        gw_rows = sb("gw_rows", [E, H], F32)
        gwT = sb("gwT", [P, HC, E], F32)
        wsgu = sb("wsgu", [P, HC, 2 * SI], F32)
        wsd = sb("wsd", [P, NSF, H], F32)
        eps_col = sb("eps_col", [P, 1], F32)
        den_c = [sb(f"den_c{b}", [P, NH * SEQ // P], F32) for b in range(NB)]

        st1 = ExitStack()
        V_all = sb("V_all", [P, UNITS, QT, 32], F32, st1)
        V_unit = [sb(f"V_unit{k}", [P, QT, 32], F32, st1) for k in range(3)]
        Qa = [sb(f"Qa{k}", [KM, 2, REP, BLK], BF16, st1) for k in range(3)]
        Ka = [sb(f"Ka{k}", [KM, SEQ], BF16, st1) for k in range(3)]
        probs = [sb(f"probs{k}", [P, REP, BLK], F32, st1) for k in range(2)]
        rowmax = [sb(f"rowmax{k}", [P, NS], F32, st1) for k in range(2)]
        max_full = [sb(f"max_full{k}", [NS, P], F32, st1) for k in range(2)]
        max_rest = sb("max_rest", [NS, P], F32, st1)
        max_split = [sb(f"max_split{k}", [NS, 3, P], BF16, st1) for k in range(2)]
        o_sb = [sb(f"o_sb{k}", [P, BLK], F32, st1) for k in range(2)]
        sb("room1", [P, ROOM1], F32, st1)
        Wq_sb = sb("Wq_sb", [P, HC, H], F32, st1)
        Wk_sb = sb("Wk_sb", [P, HC, KV], F32, st1)
        Wv_sb = sb("Wv_sb", [P, HC, KV], F32, st1)
        bias_in = sb("bias_in", [P, HC + 1], F32, st1)
        bias_qk = sb("bias_qk", [P, HC + 1], F32, st1)
        bv_bc = sb("bv_bc", [P, KV], F32, st1)
        x_in = [sb(f"x_in{k}", [P, BT, H], F32, st1) for k in range(2)]
        xT = [sb(f"xT{k}", [P, HC, BLK], F32, st1) for k in range(2)]
        qk_full = [sb(f"qk_full{k}", [P, BLK], F32, st1) for k in range(2)]
        qk_rest = [sb(f"qk_rest{k}", [P, BLK], F32, st1) for k in range(2)]
        qk_split = [sb(f"qk_split{k}", [P, 3, BLK], BF16, st1) for k in range(2)]
        st1.close()

        st2 = ExitStack()
        logits = sb("logits", [P, TT, E], F32, st2)
        masked = sb("masked", [P, TT, E], F32, st2)
        gmax = sb("gmax", [P, TT, G], F32, st2)
        top8 = sb("top8", [P, TT, 8], F32, st2)
        r_gt = sb("r_gt", [P, TT, E], F32, st2)
        r_eq = sb("r_eq", [P, TT, E], F32, st2)
        r_cum = sb("r_cum", [P, TT, E], F32, st2)
        n_gt = sb("n_gt", [P, TT], F32, st2)
        keep_g = sb("keep_g", [P, TT, G], F32, st2)
        sel = sb("sel", [P, TT, E], F32, st2)
        sel_bf = sb("sel_bf", [P, TT, E], BF16, st2)
        seg8 = sb("seg8", [P, TT, G], F32, st2)
        seg16 = sb("seg16", [P, E, TT], F32, st2)
        seg32 = sb("seg32", [P, TT, E], F32, st2)
        zsum = sb("zsum", [P, TT], F32, st2)
        weight = sb("weight", [P, TT, E], F32, st2)
        tile_count = sb("tile_count", [P, E, TT], F32, st2)
        tile_cum = sb("tile_cum", [P, E, TT], F32, st2)
        slot_of = sb("slot_of", [P, E, TT], BF16, st2)
        before = sb("before", [P, P], BF16, st2)
        all_ones = sb("all_ones", [P, P], BF16, st2)
        iota_c = sb("iota_c", [P, TT, C], BF16, st2)
        facts = sb("facts", [P, E, TT, 6], BF16, st2)
        onehot = [sb(f"onehot{k}", [P, TT, C], BF16, st2) for k in range(2)]
        spare_row = sb("spare_row", [C, 1], F32, st2)
        table = sb("table", [C, E, 6], F32, st2)
        slot_w = sb("slot_w", [C, E], F32, st2)
        slot_src = sb("slot_src", [C, E], F32, st2)
        slot_src_i = sb("slot_src_i", [C, E], I32, st2)
        slot_dst_i = sb("slot_dst_i", [C, E], I32, st2)
        src_i = [sb(f"src_i{k}", [C, 1], I32, st2) for k in range(GR)]
        dst_i = [sb(f"dst_i{k}", [C, 1], I32, st2) for k in range(GR)]
        w_col = [sb(f"w_col{k}", [C, 1], F32, st2) for k in range(GR)]
        zero_rows = sb("zero_rows", [C, H], F32, st2)
        st3 = ExitStack()
        pre1 = [sb(f"pre1_{k}", [P, H], F32, st3) for k in range(2)]
        stats1 = [sb(f"stats1_{k}", [P, 6], F32, st3) for k in range(2)]
        mv1 = [sb(f"mv1_{k}", [P, 2], F32, st3) for k in range(2)]
        std1 = [sb(f"std1_{k}", [P, 2], F32, st3) for k in range(2)]
        x1_out = [sb(f"x1_out{k}", [P, BT, H], F32, st3) for k in range(2)]
        x1T = [sb(f"x1T{k}", [P, HC, BLK], F32, st3) for k in range(2)]
        sb("room3", [P, ROOM3], F32, st3)
        num = [sb(f"num{k}", [P, HC, BLK], F32, st3) for k in range(2)]
        inv = [sb(f"inv{k}", [P, HC, BLK], F32, st3) for k in range(2)]
        x_res = [sb(f"x_res{k}", [P, BT, H], F32, st3) for k in range(2)]
        st3.close()
        st6 = ExitStack()
        wgu = [sb(f"wgu{k}", [P, HC, 2 * I], F32, st6) for k in range(2)]
        wd = [sb(f"wd{k}", [P, len(FT), H], F32, st6) for k in range(2)]
        xg = [sb(f"xg{k}", [C, H], F32, st6) for k in range(GR)]
        xgT = [sb(f"xgT{k}", [P, HC, C], F32, st6) for k in range(2)]
        e_sig = [sb(f"e_sig{k}", [P, len(FT), C], F32, st6) for k in range(2)]
        e_hid = [sb(f"e_hid{k}", [P, len(FT), C], F32, st6) for k in range(2)]
        e_out = [sb(f"e_out{k}", [C, H], F32, st6) for k in range(2)]

        st4 = ExitStack()
        sx = [sb(f"sx{k}", [P, HC, BLK], F32, st4) for k in range(2)]
        sx_rows = sb("sx_rows", [P, BT, H], F32, st4)
        s_sig = [sb(f"s_sig{k}", [P, BLK], F32, st4) for k in range(2)]
        s_hid = sb("s_hid", [P, NSF, BLK], F32, st4)
        s_sum = [sb(f"s_sum{k}", [P, BT, H], F32, st4) for k in range(2)]
        st4.close()
        st7 = ExitStack()
        wgu += [sb(f"wgu{k}", [P, HC, 2 * I], F32, st7) for k in range(2, GR)]
        wd += [sb(f"wd{k}", [P, len(FT), H], F32, st7) for k in range(2, GR)]
        st7.close()
        st5 = ExitStack()
        f_in = [sb(f"f_in{k}", [P, BT, H], F32, st5) for k in range(2)]
        f_out = [sb(f"f_out{k}", [P, BT, H], F32, st5) for k in range(2)]
        stats2 = [sb(f"stats2_{k}", [P, 6], F32, st5) for k in range(2)]
        mv2 = [sb(f"mv2_{k}", [P, 2], F32, st5) for k in range(2)]
        std2 = [sb(f"std2_{k}", [P, 2], F32, st5) for k in range(2)]
        st5.close()
        st6.close()
        st2.close()

        w_loaded = sem("w_loaded")
        w2_loaded = sem("w2_loaded")
        consts_made = sem("consts_made")
        ones_made = sem("ones_made")
        pool_step = sem("pool_step")
        bias_ready = sem("bias_ready")
        x_loaded = [sem(f"x_loaded{k}") for k in range(2)]
        x_turned = sem("x_turned")
        xT_act = sem("xT_act")
        xT_dve = sem("xT_dve")
        blk_projected = sem("blk_projected")
        job_done = sem("job_done")
        v_done = sem("v_done")
        v_kept = sem("v_kept")
        part1 = sem("part1")
        full_ready = sem("full_ready")
        rest_ready = sem("rest_ready")
        part2 = sem("part2")
        part3 = sem("part3")
        parts_stored = [sem(f"parts_stored{k}") for k in range(2)]
        gw_turned = sem("gw_turned")
        gw_ready = sem("gw_ready")
        qk_loaded = [sem(f"qk_loaded{k}") for k in range(3)]
        v_unit_ready = sem("v_unit_ready")
        s_ready = sem("s_ready")
        s_reduced = sem("s_reduced")
        max_turned = sem("max_turned")
        max_kept = sem("max_kept")
        max_step = sem("max_step")
        max_ready = sem("max_ready")
        max_rows = [sem(f"max_rows{k}") for k in range(2)]
        st_ready = sem("st_ready")
        exp_done = sem("exp_done")
        pv_done = sem("pv_done")
        o_copied = sem("o_copied")
        o_stored = [sem(f"o_stored{k}") for k in range(2)]
        den_loaded = sem("den_loaded")
        inv_stored = sem("inv_stored")
        nd_loaded = [sem(f"nd_loaded{k}") for k in range(2)]
        res_loaded = [sem(f"res_loaded{k}") for k in range(2)]
        res_ready = sem("res_ready")
        den_inv = sem("den_inv")
        mix_in = sem("mix_in")
        y_done = sem("y_done")
        pre_done = sem("pre_done")
        stats_done = sem("stats_done")
        mv_done = sem("mv_done")
        std_done = sem("std_done")
        inv_done = sem("inv_done")
        x1_done = sem("x1_done")
        x1_turned = sem("x1_turned")
        x1T_kept = sem("x1T_kept")
        logit_done = sem("logit_done")
        logit_kept = sem("logit_kept")
        x1_stored = [sem(f"x1_stored{k}") for k in range(2)]
        x1T_stored = [sem(f"x1T_stored{k}") for k in range(2)]
        r_step = sem("r_step")
        r_consts = sem("r_consts")
        rp_step = sem("rp_step")
        r_diff = sem("r_diff")
        r_exp = sem("r_exp")
        sel_ready = sem("sel_ready")
        counts_done = sem("counts_done")
        pos_done = sem("pos_done")
        facts_ready = sem("facts_ready")
        hot_ready = sem("hot_ready")
        table_done = sem("table_done")
        table_kept = sem("table_kept")
        slots_ready = sem("slots_ready")
        sx_loaded = [sem(f"sx_loaded{k}") for k in range(2)]
        sx1_loaded = sem("sx1_loaded")
        s_gate = sem("s_gate")
        s_up = sem("s_up")
        s_silu = sem("s_silu")
        s_hidden = sem("s_hidden")
        s_down = sem("s_down")
        s_added = sem("s_added")
        s_stored = [sem(f"s_stored{k}") for k in range(2)]
        spare_zero = sem("spare_zero")
        spare_stored = sem("spare_stored")
        wgu_loaded = [sem(f"wgu_loaded{k}") for k in range(GR)]
        wd_loaded = [sem(f"wd_loaded{k}") for k in range(GR)]
        src_ready = sem("src_ready")
        cols_ready = sem("cols_ready")
        gathered = [sem(f"gathered{k}") for k in range(GR)]
        xg_turned = sem("xg_turned")
        xgT_ready = sem("xgT_ready")
        e_up = sem("e_up")
        e_silu = sem("e_silu")
        e_hidden = sem("e_hidden")
        e_down = sem("e_down")
        e_scaled = sem("e_scaled")
        scattered = sem("scattered")
        f_loaded = [sem(f"f_loaded{k}") for k in range(2)]
        f_stats = sem("f_stats")
        f_mv = sem("f_mv")
        f_std = sem("f_std")
        f_inv = sem("f_inv")
        f_done = sem("f_done")
        f_stored = [sem(f"f_stored{k}") for k in range(2)]

        waited = {e.engine: sem(f"waited_{n}") for n, e in (("pool", nc.gpsimd), ("dve", nc.vector), ("sp", nc.sync))}

        def settle(eng):
            eng.sem_inc(waited[eng.engine], 1)

        JOBS = HC + 1


        def project_sync(sp):
            sp.dma_start(x_in[0][:], xf[0:BLK, :].rearrange("(t p) h -> p t h", p=P)).then_inc(x_loaded[0], 16)
            for dst, src in ((Wq_sb, Wq), (Wk_sb, Wk), (Wv_sb, Wv)):
                sp.dma_start(dst[:], src.rearrange("(c p) n -> p c n", p=P)).then_inc(w_loaded, 16)
            with nc.allow_non_contiguous_dma(reason="biases as columns"):
                sp.dma_start(bias_in[:, 0:HC], bq.rearrange("(c p) -> p c", p=P)).then_inc(w_loaded, 16)
                sp.dma_start(bias_in[:, HC:HC + 1], bk.rearrange("(c p) -> p c", p=P)).then_inc(w_loaded, 16)
            sp.dma_start(bv_bc[:], bv.rearrange("(a n) -> a n", a=1).broadcast_to([P, KV])).then_inc(w_loaded, 16)
            sp.dma_start(x_in[1][:], xf[BLK:2 * BLK, :].rearrange("(t p) h -> p t h", p=P)).then_inc(x_loaded[1], 16)
            sp.dma_start(gw_rows[:], gate_w).then_inc(w2_loaded, 16)
            sp.dma_start(Wo_sb[:], Wo.rearrange("(c p) n -> p c n", p=P)).then_inc(w2_loaded, 16)
            sp.dma_start(bo_bc[:], bo.rearrange("(a n) -> a n", a=1).broadcast_to([P, H])).then_inc(w2_loaded, 16)
            sp.dma_start(wsgu[:], ws_gate_up.rearrange("(c p) n -> p c n", p=P)).then_inc(w2_loaded, 16)
            full = SI // P
            sp.dma_start(wsd[:, 0:full, :],
                         ws_down[0:full * P, :].rearrange("(c p) n -> p c n", p=P)).then_inc(w2_loaded, 16)
            sp.dma_start(wsd[0:SI - full * P, full, :], ws_down[full * P:SI, :]).then_inc(w2_loaded, 16)
            for blk in range(NBLK):
                for j in range(JOBS):
                    m = JOBS * blk + j
                    sp.wait_ge(part3, m + 1)
                    tok = slice(blk * BLK, (blk + 1) * BLK)
                    dst = q_parts[:, j * P:(j + 1) * P, tok] if j < HC else k_parts[:, :, tok]
                    sp.dma_start(dst.rearrange("s p n -> p s n"), qk_split[m % 2][:]).then_inc(parts_stored[m % 2], 16)
                if blk + 2 < NBLK:
                    sp.wait_ge(x_turned, HC * (blk + 1))
                    rows = xf[(blk + 2) * BLK:(blk + 3) * BLK, :]
                    sp.dma_start(x_in[blk % 2][:], rows.rearrange("(t p) h -> p t h", p=P)).then_inc(x_loaded[blk % 2], 16)

        def project_pool(pool):
            nc.gpsimd.memset(ident[:], 0.0).then_inc(pool_step, 1)
            pool.wait_ge(pool_step, 1)
            nc.gpsimd.affine_select(out=ident[:], in_=ident[:], compare_op=ALU.not_equal, fill=1.0, base=0,
                                    pattern=[[-1, P]], channel_multiplier=1).then_inc(consts_made, 1)
            pool.wait_ge(consts_made, 1)
            nc.gpsimd.memset(eps_col[:], EPS).then_inc(consts_made, 1)
            pool.wait_ge(consts_made, 2)
            for k in range(3):
                nc.gpsimd.memset(Ka[k][KR:KM, :], -1.0).then_inc(consts_made, 1)
                pool.wait_ge(consts_made, 3 + k)
            with pool.Fori(0, NB) as i:
                for m in range(2 * JOBS):
                    pool.wait_ge(rest_ready, 2 * JOBS * i + m + 3)
                    settle(pool)
                    nc.gpsimd.tensor_copy(qk_split[m % 2][:, 1, :], qk_rest[m % 2][:]).then_inc(part2, 1)

        def project_tensor(pe):
            pe.wait_ge(consts_made, 5)
            pe.wait_ge(w2_loaded, 96)
            for c in range(HC):
                last = nc.tensor.transpose(bank(7)[:, c * E:(c + 1) * E], gw_rows[:, c * P:(c + 1) * P], ident[0:E, 0:E])
            last.then_inc(gw_turned, 1)
            pe.wait_ge(w_loaded, 96)
            with pe.Fori(0, NB) as i:
                for k in range(2):
                    blk = 2 * i + k
                    pe.wait_ge(x_loaded[k], 16 * i + 16)
                    for c in range(HC):
                        pe.wait_ge(xT_act if c % 2 == 0 else xT_dve, 2 * blk + c // 2 + 1)
                        for t in range(BT):
                            last = nc.tensor.transpose(bank(c % 2)[:, t * P:(t + 1) * P],
                                                       x_in[k][:, t, c * P:(c + 1) * P], ident[:])
                        last.then_inc(x_turned, 1)
                    pe.wait_ge(xT_act, 2 * blk + 3)
                    pe.wait_ge(xT_dve, 2 * blk + 3)
                    for j in range(JOBS):
                        pe.wait_ge(full_ready, JOBS * blk + j + 1)
                        w = Wq_sb[:, :, j * P:(j + 1) * P] if j < HC else Wk_sb[:]
                        for c in range(HC):
                            last = nc.tensor.matmul(bank(2 + j), w[:, c, :], xT[k][:, c, :], start=(c == 0), stop=(c == HC - 1))
                        last.then_inc(job_done, 1)
                    pe.wait_ge(v_kept, blk + 1)
                    for t in range(BT):
                        for c in range(HC):
                            last = nc.tensor.matmul(bank(7)[:, t * P:(t + 1) * P], xT[k][:, c, t * P:(t + 1) * P],
                                                    Wv_sb[:, c, :], start=(c == 0), stop=(c == HC - 1))
                    last.then_inc(v_done, 1)

        def project_scalar(act):
            act.sem_inc(xT_act, 1)
            act.sem_inc(full_ready, JOBS)
            act.wait_ge(bias_ready, 2)
            with act.Fori(0, NB) as i:
                for k in range(2):
                    blk = 2 * i + k
                    for c in (0, 2):
                        act.wait_ge(x_turned, HC * blk + c + 1)
                        act.wait_ge(v_done, blk + 1)
                        nc.scalar.activation(xT[k][:, c, :], bank(0), ACT.Copy).then_inc(xT_act, 1)
                    for j in range(JOBS):
                        m = JOBS * k + j
                        act.wait_ge(job_done, JOBS * blk + j + 1)
                        act.wait_ge(rest_ready, JOBS * blk + j + 1)
                        nc.scalar.activation(qk_full[m % 2][:], bank(2 + j), ACT.Identity, bias=bias_qk[:, j:j + 1],
                                             scale=HD ** -0.5 if j < HC else 1.0).then_inc(full_ready, 1)
                        act.wait_ge(full_ready, JOBS * blk + j + JOBS + 1)
                        act.wait_ge(parts_stored[m % 2], 16 * JOBS * i + 16 * (m // 2) + 16)
                        nc.scalar.activation(qk_split[m % 2][:, 0, :], qk_full[m % 2][:], ACT.Copy).then_inc(part1, 1)

        def project_vector(dve):
            dve.sem_inc(xT_dve, 1)
            dve.sem_inc(rest_ready, 2)
            nc.vector.memset(V_all[:], 1.0).then_inc(ones_made, 1)
            dve.wait_ge(w_loaded, 96)
            nc.vector.tensor_scalar(bias_qk[:, 0:HC], bias_in[:, 0:HC], HD ** -0.5, None, ALU.mult).then_inc(bias_ready, 1)
            nc.vector.tensor_copy(bias_qk[:, HC:HC + 1], bias_in[:, HC:HC + 1]).then_inc(bias_ready, 1)
            dve.wait_ge(gw_turned, 1)
            nc.vector.tensor_copy(gwT[:], bank(7)[:, 0:HC * E].rearrange("p (c e) -> p c e", c=HC)).then_inc(gw_ready, 1)
            dve.wait_ge(gw_ready, 1)
            dve.sem_inc(v_kept, 1)
            dve.wait_ge(ones_made, 1)
            with dve.Fori(0, NB) as i:
                for k in range(2):
                    blk = 2 * i + k
                    for c in (1, 3):
                        dve.wait_ge(x_turned, HC * blk + c + 1)
                        dve.wait_ge(v_done, blk + 1)
                        nc.vector.tensor_copy(xT[k][:, c, :], bank(1)).then_inc(xT_dve, 1)
                    for j in range(JOBS):
                        m = JOBS * k + j
                        n = JOBS * blk + j
                        dve.wait_ge(part1, n + 1)
                        dve.wait_ge(full_ready, n + JOBS + 1)
                        nc.vector.tensor_tensor(qk_rest[m % 2][:], qk_full[m % 2][:], qk_split[m % 2][:, 0, :],
                                                ALU.subtract).then_inc(rest_ready, 1)
                        dve.wait_ge(rest_ready, n + 3)
                        dve.wait_ge(part2, n + 1)
                        nc.vector.tensor_tensor(qk_split[m % 2][:, 2, :], qk_rest[m % 2][:], qk_split[m % 2][:, 1, :],
                                                ALU.subtract).then_inc(part3, 1)
                    dve.wait_ge(v_done, blk + 3)
                    dst = V_all[:, bass.ds(i * NG, NG), k * BT:(k + 1) * BT, 0:HD].rearrange("p g t d -> p t g d")
                    nc.vector.tensor_tensor(dst, bank(7).rearrange("p (t g d) -> p t g d", t=BT, g=NG),
                                            bv_bc[:].rearrange("p (a g d) -> p a g d", a=1, g=NG).broadcast_to([P, BT, NG, HD]),
                                            ALU.add).then_inc(v_kept, 1)

        def known(e, *which):
            return isinstance(e, int) and e in which

        def load_unit(sp, u, buf):
            b, g = u // NG, u % NG
            for s, (kp, qp) in enumerate(TERMS):
                rows = slice(s * HD, (s + 1) * HD)
                for qb in range(2):
                    sp.dma_start(Qa[buf][rows, qb, :, :],
                                 q_parts[qp, bass.ds(g * REP * HD, REP * HD), bass.ds(b * SEQ + qb * BLK, BLK)]
                                 .rearrange("(h d) n -> d h n", h=REP)).then_inc(qk_loaded[buf], 16)
                sp.dma_start(Ka[buf][rows, :], k_parts[kp, bass.ds(g * HD, HD), bass.ds(b * SEQ, SEQ)])\
                  .then_inc(qk_loaded[buf], 16)

        LOADS = 48 * len(TERMS)

        def by_units(eng, emit):
            emit(0, 0, 0)
            with eng.Fori(0, 4) as r:
                for j in range(3):
                    emit(3 * r + 1 + j, (1 + j) % 3, r + (1 + j) // 3)
            for u in range(13, UNITS):
                emit(u, u % 3, u // 3)

        def attend_sync(sp):
            for k in range(2):
                sp.wait_ge(parts_stored[k], 16 * (JOBS * NB + 1))
            load_unit(sp, 0, 0)
            load_unit(sp, 1, 1)

            def max_to_rows(u, qb, buf):
                sp.wait_ge(max_ready, 2 * u + qb + 3)
                for s in range(3):
                    sp.dma_start(Qa[buf][KR + s:KR + s + 1, qb, :, :].rearrange("a h n -> a (h n)"),
                                 max_split[qb][:, s, :]).then_inc(max_rows[qb], 16)

            def store_o(u, qb):
                sp.wait_ge(o_copied, 2 * u + qb + 1)
                sp.dma_start(o_raw[u, :, qb * BLK:(qb + 1) * BLK] if isinstance(u, int) else
                             o_raw[bass.ds(u, 1), :, qb * BLK:(qb + 1) * BLK].rearrange("a p n -> (a p) n"),
                             o_sb[qb][:]).then_inc(o_stored[qb], 16)

            max_to_rows(0, 0, 0)

            def emit(u, buf, _):
                first = known(u, 0)
                if not first:
                    store_o(u - 1, 1)
                if not known(u, UNITS - 2, UNITS - 1):
                    if not first:
                        sp.wait_ge(st_ready, REP * STEPS * u)
                    load_unit(sp, u + 2, (buf + 2) % 3)
                if known(u, UNITS - 3):
                    load_den(sp, 0)
                max_to_rows(u, 1, buf)
                store_o(u, 0)
                if known(u, UNITS - 3):
                    store_inv(sp, 0)
                    for k in range(2):
                        load_mix(sp, 0, k)
                if not known(u, UNITS - 1):
                    max_to_rows(u + 1, 0, (buf + 1) % 3)

            by_units(sp, emit)
            store_o(UNITS - 1, 1)

        def attend_pool(pool):
            pool.sem_inc(max_ready, 2)
            pool.wait_ge(v_kept, NBLK + 1)

            def split_max(u, qb):
                pool.wait_ge(max_kept, 2 * u + qb + 1)
                pool.wait_ge(max_rows[qb], 48 * u + 48)
                settle(pool)
                step = 3 * (2 * u + qb)
                nc.gpsimd.tensor_copy(max_split[qb][:, 0, :], max_full[qb][:]).then_inc(max_step, 1)
                pool.wait_ge(max_step, step + 1)
                settle(pool)
                nc.gpsimd.tensor_tensor(max_rest[:], max_full[qb][:], max_split[qb][:, 0, :], ALU.subtract).then_inc(max_step, 1)
                pool.wait_ge(max_step, step + 2)
                settle(pool)
                nc.gpsimd.tensor_copy(max_split[qb][:, 1, :], max_rest[:]).then_inc(max_step, 1)
                pool.wait_ge(max_step, step + 3)
                settle(pool)
                nc.gpsimd.tensor_tensor(max_split[qb][:, 2, :], max_rest[:], max_split[qb][:, 1, :],
                                        ALU.subtract).then_inc(max_ready, 1)

            def copy_V(u, k):
                nc.gpsimd.tensor_copy(V_unit[k][:].rearrange("p t d -> p (t d)"),
                                      V_all[:, bass.ds(u, 1), :, :].rearrange("p a t d -> p (a t d)")).then_inc(v_unit_ready, 1)

            for k in range(2):
                pool.sem_inc(max_rows[k], 48)
                copy_V(k, k)
            split_max(0, 0)

            def emit(u, buf, _):
                split_max(u, 1)
                if not known(u, UNITS - 2, UNITS - 1):
                    if not known(u, 0):
                        pool.wait_ge(pv_done, STEPS * u)
                        settle(pool)
                    copy_V(u + 2, (buf + 2) % 3)
                if known(u, UNITS - 2, UNITS - 1):
                    for i in range(5):
                        mix_piece(pool, 0, i if u == UNITS - 2 else i + 8)
                if not known(u, UNITS - 1):
                    split_max(u + 1, 0)
                if known(u, UNITS - 2):
                    for i in range(5, 8):
                        mix_piece(pool, 0, i)
                if known(u, UNITS - 1):
                    for i in range(13, 16):
                        mix_piece(pool, 0, i)

            by_units(pool, emit)

        def score_half(pe, g, buf, n, half, round_):
            qb = n // NS
            n %= NS
            if half == 0:
                if n == 0 and qb == 0:
                    pe.wait_ge(qk_loaded[buf], LOADS * (round_ + 1))
                pe.wait_ge(s_reduced, NS * g + n + 1)
                if n == 2 and not known(g, 0):
                    pe.wait_ge(max_kept, g)
            h, qt = n // (QT // 2), n % (QT // 2)
            mm = nc.tensor.matmul(pair[n % 2][:, half * 512:(half + 1) * 512], Qa[buf][0:KR, qb, h, qt * P:(qt + 1) * P],
                                  Ka[buf][0:KR, half * 512:(half + 1) * 512], start=True, stop=True)
            if half == 1:
                mm.then_inc(s_ready, 1)

        def turn_max(pe, g, qb, last=False):
            pe.wait_ge(s_reduced, NS * (g + 1) + (2 if last else 3))
            nc.tensor.transpose(pair[0][0:NS, 0:P], rowmax[qb][:], ident[:]).then_inc(max_turned, 1)

        def stream_half(pe, u, buf, round_, j):
            i = j // 2
            rest = S_PER_STEP * (STEPS // 2 + LEAD - STEPS)
            if i < rest:
                if not known(u, 0) or True:
                    score_half(pe, 2 * u + 1, buf, NS + NS - rest + i, j % 2, round_)
                return
            n = i - rest
            if j % 2 == 0 and n == 2:
                turn_max(pe, 2 * u + 1, 1)
            if j % 2 == 0 and n == NS + 2:
                turn_max(pe, 2 * u + 2, 0)
            score_half(pe, 2 * u + 2 + n // NS, (buf + 1) % 3, n, j % 2, round_ + (buf + 1) // 3)

        def attend_tensor(pe):
            pe.wait_ge(full_ready, JOBS * (NBLK + 1))
            pe.wait_ge(v_kept, NBLK + 1)
            pe.sem_inc(max_turned, 2)
            for n in range(S_PER_STEP * LEAD):
                if n == NS + 2:
                    turn_max(pe, 0, 0)
                for half in range(2):
                    score_half(pe, n // NS, 0, n, half, 0)

            def pv(u, s, buf):
                qb, kt = s // QT, s % QT
                pe.wait_ge(exp_done, REP * (STEPS * u + s + 1))
                if s == 0:
                    pe.wait_ge(v_unit_ready, u + 1)
                if kt == 0 and not (known(u, 0) and s == 0):
                    pe.wait_ge(o_copied, 2 * u + qb)
                for h in range(REP):
                    last = nc.tensor.matmul(bank(7)[32 * h:32 * h + 32, :], V_unit[buf][:, kt, :],
                                            probs[s % 2][:, h, :], start=(kt == 0), stop=(kt == QT - 1),
                                            tile_position=(0, 32 * h))
                last.then_inc(pv_done, 1)

            def emit(u, buf, round_):
                first = known(u, 0)
                final = known(u, UNITS - 1)

                def st(s, h):
                    qb, kt = s // QT, s % QT
                    n = REP * s + h
                    if not (first and n < 3):
                        pe.wait_ge(exp_done, REP * STEPS * u + n - 2)
                    if h == 0 and kt == 0:
                        pe.wait_ge(max_rows[qb], 48 * u + 96)
                    mm = nc.tensor.matmul(bank(4 + (buf + n) % 3), Ka[buf][0:KM, kt * P:(kt + 1) * P],
                                          Qa[buf][0:KM, qb, h, :], start=True, stop=True)
                    mm.then_inc(st_ready, 1)

                def stream(s, a):
                    if not final or s < STEPS // 2 + LEAD - STEPS:
                        stream_half(pe, u, buf, round_, 2 * S_PER_STEP * s + a)

                for s in range(STEPS):
                    st(s, 0)
                    stream(s, 0)
                    st(s, 1)
                    stream(s, 1)
                    if s > 0:
                        pv(u, s - 1, buf)
                    elif not first:
                        pv(u - 1, STEPS - 1, (buf + 2) % 3)
                    st(s, 2)
                    stream(s, 2)
                    st(s, 3)
                    stream(s, 3)
                    if final and s == STEPS // 2 + LEAD - STEPS:
                        turn_max(pe, 2 * u + 1, 1, last=True)

            by_units(pe, emit)
            pv(UNITS - 1, STEPS - 1, (UNITS - 1) % 3)

        def attend_vector(dve):
            def maxima(g, qb, first=False):
                dve.wait_ge(max_turned, g + 1)
                for n in range(NS):
                    if n == 2 and not first:
                        keep_max(g - 1, 1 - qb)
                    dve.wait_ge(s_ready, NS * g + n + 1)
                    nc.vector.tensor_reduce(rowmax[qb][:, n:n + 1], pair[n % 2][:], AX.X, ALU.max).then_inc(s_reduced, 1)

            def keep_max(g, qb):
                dve.wait_ge(max_turned, g + 3)
                dve.wait_ge(max_ready, g + 1)
                nc.vector.tensor_copy(max_full[qb][:], pair[0][0:NS, 0:P]).then_inc(max_kept, 1)

            dve.sem_inc(s_reduced, 2)
            maxima(0, 0, True)
            with dve.Fori(0, UNITS - 2) as u:
                maxima(2 * u + 1, 1)
                maxima(2 * u + 2, 0)
            u = UNITS - 2
            invert_den(dve, 0)
            maxima(2 * u + 1, 1)
            maxima(2 * u + 2, 0)
            maxima(2 * u + 3, 1)
            keep_max(2 * u + 3, 1)

        def attend_scalar(act):
            for qb in range(2):
                act.sem_inc(o_stored[qb], 16)

            def copy_o(u, qb):
                act.wait_ge(pv_done, STEPS * u + QT * (qb + 1))
                act.wait_ge(o_stored[qb], 16 * u + 16)
                nc.scalar.activation(o_sb[qb][:], bank(7), ACT.Copy).then_inc(o_copied, 1)

            def emit(u, buf, _):
                first = known(u, 0)
                for s in range(STEPS):
                    if not (first and s < 2):
                        act.wait_ge(pv_done, STEPS * u + s - 1)
                    for h in range(REP):
                        n = REP * s + h
                        act.wait_ge(st_ready, REP * STEPS * u + n + 1)
                        nc.scalar.activation(probs[s % 2][:, h, :], bank(4 + (buf + n) % 3), ACT.Exp).then_inc(exp_done, 1)
                        if s == 0 and h == 2 and not first:
                            copy_o(u - 1, 1)
                        if s == QT and h == 2:
                            copy_o(u, 0)

            by_units(act, emit)
            copy_o(UNITS - 1, 1)

        heads = o_raw.rearrange("u (h r) n -> (u h) r n", h=REP)

        def load_den(eng, b):
            for qb in range(2):
                eng.wait_ge(o_stored[qb], 16 * NG * (b + 1) + 16)
            eng.dma_start(den_c[b][:], heads[b * NH:(b + 1) * NH, HD, :].rearrange("h (j n) -> h j n", j=P // NH))\
               .then_inc(den_loaded, 16)

        def store_inv(eng, b):
            eng.wait_ge(den_inv, b + 1)
            eng.dma_start(inv_den[b * NH:(b + 1) * NH, :].rearrange("h (j n) -> h j n", j=P // NH), den_c[b][:])\
               .then_inc(inv_stored, 16)

        def invert_den(dve, b):
            dve.wait_ge(den_loaded, 16 * (b + 1))
            nc.vector.reciprocal(den_c[b][:], den_c[b][:]).then_inc(den_inv, 1)

        def load_mix(sp, b, k):
            if b > 0:
                sp.wait_ge(y_done, BT * (NB * (b - 1) + k) + 3 * BT)
            sp.wait_ge(inv_stored, 16 * b + 16)
            for c in range(HC):
                rows = slice(b * NH + 8 * c, b * NH + 8 * c + 8)
                tok = slice(k * BLK, (k + 1) * BLK)
                sp.dma_start(num[k][:, c, :], heads[rows, 0:HD, tok]).then_inc(nd_loaded[k], 16)
                sp.dma_start(inv[k][:, c, :], inv_den[rows, tok].rearrange("h (a n) -> h a n", a=1).broadcast_to([8, HD, BLK]))\
                  .then_inc(nd_loaded[k], 16)
            blk = NB * b + k
            if b > 0:
                sp.wait_ge(pre_done, BT * (NB * (b - 1) + k) + 3 * BT)
            sp.dma_start(x_res[k][:], xf[blk * BLK:(blk + 1) * BLK, :].rearrange("(t p) h -> p t h", p=P))\
              .then_inc(res_loaded[k], 16)

        def mix_sync(sp):
            load_den(sp, 1)
            store_inv(sp, 1)
            for k in range(2):
                load_mix(sp, 1, k)

        ND = 16 * HC * 2

        def mix_piece(pool, b, i):
            k, i = i // (HC + BT), i % (HC + BT)
            if i < HC:
                pool.wait_ge(nd_loaded[k], ND * b + ND)
                nc.gpsimd.tensor_tensor(num[k][:, i, :], num[k][:, i, :], inv[k][:, i, :], ALU.mult).then_inc(mix_in, 1)
            else:
                pool.wait_ge(res_loaded[k], 16 * b + 16)
                pool.wait_ge(w2_loaded, 96)
                nc.gpsimd.tensor_tensor(x_res[k][:, i - HC, :], x_res[k][:, i - HC, :], bo_bc[:], ALU.add).then_inc(res_ready, 1)

        def mix_pool(pool):
            for i in range(2 * (HC + BT)):
                mix_piece(pool, 1, i)

        def mix_tensor(pe):
            pe.sem_inc(y_done, 2 * BT)
            pe.wait_ge(o_copied, 2 * UNITS)
            pe.wait_ge(gw_ready, 1)

            def project_tile(blk, k, t):
                pe.wait_ge(pre_done, BT * blk + t + 2 * BT - 1)
                for c in range(HC):
                    last = nc.tensor.matmul(bank(t % 2), num[k][:, c, t * P:(t + 1) * P], Wo_sb[:, c, :],
                                            start=(c == 0), stop=(c == HC - 1))
                last.then_inc(y_done, 1)

            def turn_tile(blk, k, t):
                pe.wait_ge(x1_done, BT * blk + t + 1)
                pe.wait_ge(x1T_kept, BT * blk + t + 1)
                for c in range(HC):
                    last = nc.tensor.transpose(bank(2 + t % 2)[:, c * P:(c + 1) * P], x1_out[k][:, t, c * P:(c + 1) * P], ident[:])
                last.then_inc(x1_turned, 1)

            with pe.Fori(0, NB) as b:
                for k in range(2):
                    blk = 2 * b + k
                    pe.wait_ge(mix_in, HC * blk + HC)
                    project_tile(blk, k, 0)
                    project_tile(blk, k, 1)
                    for t in range(BT):
                        turn_tile(blk, k, t)
                        if t + 2 < BT:
                            project_tile(blk, k, t + 2)
                    pe.wait_ge(x1T_kept, BT * blk + BT + 2)
                    pe.wait_ge(logit_kept, blk + 1)
                    for t in range(BT):
                        for c in range(HC):
                            last = nc.tensor.matmul(bank(4)[:, t * E:(t + 1) * E], x1T[k][:, c, t * P:(t + 1) * P],
                                                    gwT[:, c, :], start=(c == 0), stop=(c == HC - 1))
                    last.then_inc(logit_done, 1)

        def mix_vector(dve):
            invert_den(dve, 1)
            dve.sem_inc(pre_done, 2 * BT)
            dve.sem_inc(logit_kept, 1)
            with dve.Fori(0, NB) as b:
                for k in range(2):
                    blk = 2 * b + k
                    dve.wait_ge(res_ready, BT * blk + BT)
                    dve.wait_ge(x1_stored[k], 16 * b + 16)
                    for t in range(BT):
                        n = BT * blk + t
                        dve.wait_ge(y_done, n + 2 * BT + 1)
                        nc.vector.tensor_tensor(pre1[t % 2][:], bank(t % 2), x_res[k][:, t, :], ALU.add).then_inc(pre_done, 1)
                        dve.wait_ge(pre_done, n + 2 * BT + 1)
                        nc.vector.bn_stats(stats1[t % 2][:], pre1[t % 2][:]).then_inc(stats_done, 1)
                        dve.wait_ge(stats_done, n + 1)
                        settle(dve)
                        nc.vector.bn_aggr(mv1[t % 2][:], stats1[t % 2][:]).then_inc(mv_done, 1)
                        dve.wait_ge(std_done, n + 1)
                        nc.vector.reciprocal(std1[t % 2][:, 1:2], std1[t % 2][:, 0:1]).then_inc(inv_done, 1)
                        dve.wait_ge(inv_done, n + 1)
                        nc.vector.tensor_scalar(x1_out[k][:, t, :], pre1[t % 2][:], mv1[t % 2][:, 0:1], std1[t % 2][:, 1:2],
                                                ALU.subtract, ALU.mult).then_inc(x1_done, 1)
                    dve.wait_ge(logit_done, blk + 1)
                    nc.vector.tensor_copy(logits[:, bass.ds(blk * BT, BT), :],
                                          bank(4)[:, 0:BT * E].rearrange("p (t e) -> p t e", t=BT)).then_inc(logit_kept, 1)

        def mix_scalar(act):
            act.sem_inc(x1T_kept, 2)
            for k in range(2):
                act.sem_inc(x1_stored[k], 16)
                act.sem_inc(x1T_stored[k], 16)
            act.wait_ge(consts_made, 5)
            with act.Fori(0, NB) as b:
                for k in range(2):
                    blk = 2 * b + k

                    def std(t):
                        n = BT * blk + t
                        act.wait_ge(mv_done, n + 1)
                        nc.scalar.activation(std1[t % 2][:, 0:1], mv1[t % 2][:, 1:2], ACT.Sqrt, bias=eps_col[:],
                                             scale=1.0).then_inc(std_done, 1)

                    def keep(t):
                        n = BT * blk + t
                        act.wait_ge(x1_turned, n + 1)
                        if t == 0:
                            act.wait_ge(x1T_stored[k], 16 * b + 16)
                        nc.scalar.activation(x1T[k][:, :, t * P:(t + 1) * P],
                                             bank(2 + t % 2).rearrange("p (c n) -> p c n", c=HC), ACT.Copy).then_inc(x1T_kept, 1)

                    std(0)
                    for t in range(BT):
                        if t + 1 < BT:
                            std(t + 1)
                        keep(t)
                    act.wait_ge(x1_done, BT * blk + BT)
                    act.dma_start(x1_rows[bass.ds(blk * BLK, BLK), :].rearrange("(t p) h -> p t h", p=P),
                                  x1_out[k][:]).then_inc(x1_stored[k], 16)
                    act.wait_ge(x1T_kept, BT * blk + BT + 2)
                    act.dma_start(x1T_blocks[bass.ds(blk, 1), :, :].rearrange("a p n -> (a p) n"),
                                  x1T[k][:].rearrange("p c n -> p (c n)")).then_inc(x1T_stored[k], 16)

        def route_pool(pool):
            pool.wait_ge(pv_done, STEPS * UNITS)
            pool.wait_ge(mix_in, HC * NBLK)
            nc.gpsimd.memset(seg8[:], 1.0).then_inc(rp_step, 1)
            nc.gpsimd.memset(seg32[:], 1.0).then_inc(rp_step, 1)
            nc.gpsimd.memset(seg16[:], 1.0).then_inc(rp_step, 1)
            nc.gpsimd.memset(all_ones[:], 1.0).then_inc(rp_step, 1)
            pool.wait_ge(rp_step, 4)
            nc.gpsimd.memset(seg8[:, :, 0:1], 0.0).then_inc(r_consts, 1)
            nc.gpsimd.memset(seg32[:, :, 0:1], 0.0).then_inc(r_consts, 1)
            nc.gpsimd.memset(seg16[:, :, 0:1], 0.0).then_inc(r_consts, 1)
            nc.gpsimd.affine_select(out=before[:], in_=all_ones[:], compare_op=ALU.is_gt, fill=0.0, base=0,
                                    pattern=[[1, P]], channel_multiplier=-1).then_inc(r_consts, 1)
            nc.gpsimd.iota(iota_c[:], pattern=[[0, TT], [1, C]], base=0, channel_multiplier=0,
                           allow_small_or_imprecise_dtypes=True).then_inc(r_consts, 1)
            nc.gpsimd.iota(facts[:, :, :, 0:1], pattern=[[0, E], [0, TT], [0, 1]], base=0, channel_multiplier=1,
                           allow_small_or_imprecise_dtypes=True).then_inc(r_consts, 1)
            nc.gpsimd.iota(facts[:, :, :, 1:2], pattern=[[0, E], [1, TT], [0, 1]], base=0, channel_multiplier=0,
                           allow_small_or_imprecise_dtypes=True).then_inc(r_consts, 1)
            nc.gpsimd.memset(facts[:, :, :, 5:6], 1.0).then_inc(r_consts, 1)
            nc.gpsimd.iota(spare_row[:], pattern=[[0, 1]], base=T, channel_multiplier=1,
                           allow_small_or_imprecise_dtypes=True).then_inc(r_consts, 1)
            nc.gpsimd.memset(zero_rows[:], 0.0).then_inc(spare_zero, 1)
            pool.wait_ge(spare_zero, 1)
            pool.dma_start(total[T:T + C, :], zero_rows[:]).then_inc(spare_stored, 16)

        def route_vector(dve):
            count = [0]

            def link(ins):
                count[0] += 1
                ins.then_inc(r_step, 1)
                dve.wait_ge(r_step, count[0])

            def bc(ap, n):
                return ap.rearrange("p (t a) -> p t a", a=1).broadcast_to([P, TT, n])

            def choose(dst, values, width, nth, seg):
                for t in range(TT):
                    last = nc.vector.max(out=top8[:, t, :], in_=values[:, t, :])
                link(last)
                thr = top8[:, :, nth - 1:nth].broadcast_to([P, TT, width])
                gt, eq, cum = r_gt[:, :, 0:width], r_eq[:, :, 0:width], r_cum[:, :, 0:width]
                if width < E:
                    flat = lambda x: x[:].rearrange("p t e -> p (t e)")[:, 0:TT * width].rearrange("p (t e) -> p t e", t=TT)
                    gt, eq, cum = flat(r_gt), flat(r_eq), flat(r_cum)
                link(nc.vector.tensor_tensor(gt, values[:], thr, ALU.is_gt))
                link(nc.vector.tensor_tensor(eq, values[:], thr, ALU.is_equal))
                link(nc.vector.tensor_reduce(n_gt[:], gt, AX.X, ALU.add))
                link(nc.vector.tensor_tensor_scan(cum.rearrange("p t e -> p (t e)"), seg[:].rearrange("p t e -> p (t e)"),
                                                  eq.rearrange("p t e -> p (t e)"), 0.0, ALU.mult, ALU.add))
                link(nc.vector.tensor_tensor(cum, cum, bc(n_gt[:], width), ALU.add))
                link(nc.vector.tensor_scalar(cum, cum, float(nth), None, ALU.is_le))
                link(nc.vector.tensor_tensor(cum, cum, eq, ALU.mult))
                link(nc.vector.tensor_tensor(dst, cum, gt, ALU.add))

            dve.wait_ge(logit_kept, NBLK + 1)
            dve.wait_ge(r_consts, 9)
            link(nc.vector.tensor_reduce(gmax[:].rearrange("p t g -> p (t g)"),
                                         logits[:].rearrange("p t (g e) -> p (t g) e", g=G), AX.X, ALU.max))
            choose(keep_g[:], gmax, G, TG, seg8)
            link(nc.vector.tensor_tensor(masked[:].rearrange("p t (g e) -> p (t g) e", g=G),
                                         logits[:].rearrange("p t (g e) -> p (t g) e", g=G),
                                         keep_g[:].rearrange("p t (g a) -> p (t g) a", a=1).broadcast_to([P, TT * G, E // G]),
                                         ALU.mult))
            choose(sel[:], masked, E, K, seg32)
            nc.vector.tensor_copy(sel_bf[:], sel[:]).then_inc(sel_ready, 1)
            link(nc.vector.tensor_tensor(masked[:], masked[:], top8[:, :, 0:1].broadcast_to([P, TT, E]), ALU.subtract))
            nc.vector.tensor_copy(r_eq[:, 0, 0:1], r_gt[:, 0, 0:1]).then_inc(r_diff, 1)
            dve.wait_ge(r_exp, 1)
            link(nc.vector.tensor_reduce(zsum[:], weight[:], AX.X, ALU.add))
            link(nc.vector.reciprocal(zsum[:], zsum[:]))
            link(nc.vector.tensor_tensor(weight[:], weight[:], bc(zsum[:], E), ALU.mult))
            link(nc.vector.scalar_tensor_tensor(out=weight[:], in0=weight[:], scalar=SCALE, in1=sel[:],
                                                op0=ALU.mult, op1=ALU.mult))
            wT = weight[:].rearrange("p t e -> p e t")
            restT = r_gt[:].rearrange("p t e -> p e t")
            link(nc.vector.tensor_copy(facts[:, :, :, 2], wT))
            link(nc.vector.tensor_tensor(restT, wT, facts[:, :, :, 2], ALU.subtract))
            link(nc.vector.tensor_copy(facts[:, :, :, 3], restT))
            link(nc.vector.tensor_tensor(facts[:, :, :, 4], restT, facts[:, :, :, 3], ALU.subtract))
            dve.wait_ge(counts_done, 1)
            cnt = bank(7).rearrange("p (t e) -> p e t", t=TT)
            link(nc.vector.tensor_copy(tile_count[:], cnt))
            link(nc.vector.tensor_tensor_scan(tile_cum[:].rearrange("p e t -> p (e t)"), seg16[:].rearrange("p e t -> p (e t)"),
                                              tile_count[:].rearrange("p e t -> p (e t)"), 0.0, ALU.mult, ALU.add))
            link(nc.vector.tensor_tensor(tile_cum[:], tile_cum[:], tile_count[:], ALU.subtract))
            dve.wait_ge(pos_done, 1)
            link(nc.vector.tensor_tensor(tile_cum[:], bank(6).rearrange("p (t e) -> p e t", t=TT), tile_cum[:], ALU.add))
            link(nc.vector.scalar_tensor_tensor(out=tile_cum[:], in0=tile_cum[:], scalar=1.0,
                                                in1=sel[:].rearrange("p t e -> p e t"), op0=ALU.add, op1=ALU.mult))
            nc.vector.tensor_scalar(slot_of[:], tile_cum[:], -1.0, None, ALU.add).then_inc(facts_ready, 1)
            dve.wait_ge(facts_ready, 1)

        def route_scalar(act):
            act.wait_ge(r_diff, 1)
            act.wait_ge(r_step, 20)
            nc.scalar.activation(weight[:], masked[:], ACT.Exp).then_inc(r_exp, 1)

        def route_tensor(pe):
            pe.wait_ge(sel_ready, 1)
            chosen = sel_bf[:].rearrange("p t e -> p (t e)")
            nc.tensor.matmul(bank(7), all_ones[:], chosen, start=True, stop=True).then_inc(counts_done, 1)
            nc.tensor.matmul(bank(6), before[:], chosen, start=True, stop=True).then_inc(pos_done, 1)
            pe.wait_ge(facts_ready, 1)

        def shared_sync(sp):
            sp.wait_ge(logit_done, NBLK)
            sp.wait_ge(x1_done, TT)
            for k in range(2):
                sp.wait_ge(x1_stored[k], 16 * (NB + 1))
                sp.wait_ge(x1T_stored[k], 16 * (NB + 1))
            for e in range(2):
                load_wgu(sp, e, e)
                load_wd(sp, e, e)
            with sp.Fori(0, NB) as b:
                for k in range(2):
                    blk = 2 * b + k
                    sp.wait_ge(s_up, NSF * blk + 1)
                    sp.dma_start(sx[k][:].rearrange("p c n -> p (c n)"),
                                 x1T_blocks[bass.ds(blk, 1), :, :].rearrange("a p n -> (a p) n")).then_inc(sx_loaded[k], 16)
                    sp.wait_ge(s_added, BT * blk + BT)
                    sp.dma_start(sx_rows[:], x1_rows[bass.ds(blk * BLK, BLK), :].rearrange("(t p) h -> p t h", p=P))\
                      .then_inc(sx1_loaded, 16)

        def shared_tensor(pe):
            pe.sem_inc(s_up, 2 * NSF)
            pe.wait_ge(x1T_kept, TT + 2)
            pe.wait_ge(pre_done, TT + 2 * BT)
            with pe.Fori(0, NB) as b:
                for k in range(2):
                    blk = 2 * b + k
                    pe.wait_ge(sx_loaded[k], 16 * b + 16)
                    for f, (f0, fn) in enumerate(SFT):
                        pe.wait_ge(s_hidden, NSF * blk + f + 1)
                        for dst, off, done in ((bank(f % 2), 0, s_gate), (bank(2 + f % 2), SI, s_up)):
                            for c in range(HC):
                                last = nc.tensor.matmul(dst[0:fn, :], wsgu[:, c, off + f0:off + f0 + fn], sx[k][:, c, :],
                                                        start=(c == 0), stop=(c == HC - 1))
                            last.then_inc(done, 1)
                        step = k * NSF + f
                        if FIRST_TABLE_STEP <= step:
                            for a in range(SLOT_EXPERTS):
                                slot_table(pe, b, SLOT_EXPERTS * (step - FIRST_TABLE_STEP) + a)
                    pe.wait_ge(s_hidden, NSF * blk + NSF + 2)
                    for t in range(BT):
                        pe.wait_ge(s_added, BT * blk + t + BT - 1)
                        for f, (f0, fn) in enumerate(SFT):
                            last = nc.tensor.matmul(bank(4 + t % 2), s_hid[0:fn, f, t * P:(t + 1) * P], wsd[0:fn, f, :],
                                                    start=(f == 0), stop=(f == NSF - 1))
                        last.then_inc(s_down, 1)

        def slot_table(pe, b, n):
            pe.wait_ge(hot_ready, (E // 2) * b + n + 1)
            if n == 0:
                pe.wait_ge(table_kept, b + 1)
            for t in range(TT):
                last = nc.tensor.matmul(bank(6)[0:C, 6 * n:6 * n + 6], onehot[n % 2][:, t, :],
                                        facts[:, bass.ds((E // 2) * b + n, 1), t:t + 1, :].rearrange("p a t s -> p (a t s)"),
                                        start=(t == 0), stop=(t == TT - 1))
            last.then_inc(table_done, 1)

        def onehots(eng, b, n):
            eng.wait_ge(table_done, (E // 2) * b + n + 1)
            col = slot_of[:, bass.ds((E // 2) * b + n, 1), :].rearrange("p a (t c) -> p (a t) c", c=1)
            nc.vector.tensor_tensor(onehot[n % 2][:], iota_c[:], col.broadcast_to([P, TT, C]), ALU.is_equal)\
              .then_inc(hot_ready, 1)

        def shared_scalar(act):
            with act.Fori(0, NB) as b:
                for k in range(2):
                    blk = 2 * b + k
                    for f, (f0, fn) in enumerate(SFT):
                        act.wait_ge(s_gate, NSF * blk + f + 1)
                        act.wait_ge(s_hidden, NSF * blk + f + 1)
                        nc.scalar.activation(s_sig[f % 2][0:fn, :], bank(f % 2)[0:fn, :], ACT.Silu).then_inc(s_silu, 1)
                    act.wait_ge(s_added, BT * blk + 2 * BT)
                    act.dma_start(total[bass.ds(blk * BLK, BLK), :].rearrange("(t p) h -> p t h", p=P),
                                  s_sum[k][:]).then_inc(s_stored[k], 16)

        def shared_vector(dve):
            dve.sem_inc(s_hidden, 2)
            dve.sem_inc(s_added, BT)
            dve.sem_inc(table_kept, 1)
            for k in range(2):
                dve.sem_inc(s_stored[k], 16)
            with dve.Fori(0, NB) as b:
                for k in range(2):
                    blk = 2 * b + k
                    for f, (f0, fn) in enumerate(SFT):
                        step = k * NSF + f
                        if FIRST_TABLE_STEP - 1 <= step < 2 * NSF - 1:
                            for a in range(SLOT_EXPERTS):
                                onehots(dve, b, SLOT_EXPERTS * (step - FIRST_TABLE_STEP + 1) + a)
                        dve.wait_ge(s_silu, NSF * blk + f + 1)
                        dve.wait_ge(s_up, NSF * blk + f + 2 * NSF + 1)
                        if f == 0:
                            dve.wait_ge(s_down, BT * blk + BT)
                        nc.vector.tensor_tensor(s_hid[0:fn, f, :], s_sig[f % 2][0:fn, :], bank(2 + f % 2)[0:fn, :],
                                                ALU.mult).then_inc(s_hidden, 1)
                    dve.wait_ge(sx1_loaded, 16 * blk + 16)
                    dve.wait_ge(s_stored[k], 16 * b + 16)
                    for t in range(BT):
                        dve.wait_ge(s_down, BT * blk + t + BT + 1)
                        nc.vector.tensor_tensor(s_sum[k][:, t, :], bank(4 + t % 2), sx_rows[:, t, :], ALU.add).then_inc(s_added, 1)
                dve.wait_ge(table_done, (E // 2) * b + E // 2 + 2)
                nc.vector.tensor_copy(table[:, bass.ds((E // 2) * b, E // 2), :],
                                      bank(6)[0:C, 0:3 * E].rearrange("p (e s) -> p e s", s=6)).then_inc(table_kept, 1)
            count = [0]

            def link(ins):
                count[0] += 1
                ins.then_inc(slots_ready, 1)
                dve.wait_ge(slots_ready, count[0])

            dve.wait_ge(table_kept, NB + 1)
            link(nc.vector.tensor_tensor(slot_w[:], table[:, :, 2], table[:, :, 3], ALU.add))
            link(nc.vector.tensor_tensor(slot_w[:], slot_w[:], table[:, :, 4], ALU.add))
            link(nc.vector.scalar_tensor_tensor(out=slot_src[:], in0=table[:, :, 1], scalar=float(P), in1=table[:, :, 0],
                                                op0=ALU.mult, op1=ALU.add))
            link(nc.vector.tensor_copy(slot_src_i[:], slot_src[:]))
            link(nc.vector.tensor_scalar(table[:, :, 5], table[:, :, 5], -1.0, 1.0, ALU.mult, ALU.add))
            link(nc.vector.scalar_tensor_tensor(out=slot_src[:], in0=table[:, :, 5], scalar=spare_row[:, 0:1], in1=slot_src[:],
                                                op0=ALU.mult, op1=ALU.add))
            link(nc.vector.tensor_copy(slot_dst_i[:], slot_src[:]))

        SLOT_STEPS = 7

        def load_wgu(sp, e, k):
            src = w_gate_up[e] if isinstance(e, int) else w_gate_up[bass.ds(e, 1), :, :].rearrange("a k n -> (a k) n")
            sp.dma_start(wgu[k][:], src.rearrange("(c p) n -> p c n", p=P)).then_inc(wgu_loaded[k], 16)

        def load_wd(sp, e, k):
            src = w_down[e] if isinstance(e, int) else w_down[bass.ds(e, 1), :, :].rearrange("a k n -> (a k) n")
            sp.dma_start(wd[k][:, 0:2, :], src[0:2 * P, :].rearrange("(c p) n -> p c n", p=P)).then_inc(wd_loaded[k], 16)
            sp.dma_start(wd[k][0:FT[2][1], 2, :], src[2 * P:I, :]).then_inc(wd_loaded[k], 16)

        def by_rounds(eng, emit):
            rounds = E // GR
            for k in range(GR):
                emit(k, k, 0)
            with eng.Fori(1, rounds - 1) as r:
                for k in range(GR):
                    emit(GR * r + k, k, r)
            for k in range(GR):
                emit(E - GR + k, k, rounds - 1)

        def experts_sync(sp):
            def emit(e, k, r):
                if known(e, 0, 1):
                    return
                if not known(e, 2, 3):
                    sp.wait_ge(e_up, e - GR + 1)
                load_wgu(sp, e, k)
                if not known(e, 2, 3):
                    sp.wait_ge(e_down, e - GR + 1)
                load_wd(sp, e, k)

            sp.wait_ge(s_up, NSF * (NBLK + 2))
            sp.wait_ge(s_hidden, NSF * NBLK + 2)
            sp.wait_ge(s_down, TT + BT)
            sp.wait_ge(s_added, TT + BT)
            for k in range(2):
                sp.wait_ge(s_stored[k], 16 * (NB + 1))
            by_rounds(sp, emit)

        def experts_pool(pool):
            pool.wait_ge(slots_ready, SLOT_STEPS)

            def col(a, e):
                return a[:, e:e + 1] if isinstance(e, int) else a[:, bass.ds(e, 1)]

            def gather(e, k):
                if not known(e, *range(GR)):
                    pool.wait_ge(xg_turned, e - GR + 1)
                settle(pool)
                nc.gpsimd.tensor_copy(src_i[k][:], col(slot_src_i, e)).then_inc(src_ready, 1)
                pool.wait_ge(src_ready, e + 1)
                settle(pool)
                pool.indirect_dma_start(xg[k][:], None, x1_rows, bass.IndirectOffsetOnAxis(ap=src_i[k][:, 0:1], axis=0))\
                    .then_inc(gathered[k], 16)

            def columns(e, k):
                if not known(e, *range(GR)):
                    pool.wait_ge(e_scaled, e - GR + 1)
                    pool.wait_ge(scattered, 16 * (e - GR + 1))
                settle(pool)
                nc.gpsimd.tensor_copy(dst_i[k][:], col(slot_dst_i, e)).then_inc(cols_ready, 1)
                nc.gpsimd.tensor_copy(w_col[k][:], col(slot_w, e)).then_inc(cols_ready, 1)

            def add(e, k):
                pool.wait_ge(e_scaled, e + 1)
                pool.wait_ge(cols_ready, 2 * e + 2)
                if not known(e, 0):
                    pool.wait_ge(scattered, 16 * e)
                settle(pool)
                pool.indirect_dma_start(total, bass.IndirectOffsetOnAxis(ap=dst_i[k][:, 0:1], axis=0), e_out[k % 2][:], None,
                                        compute_op=ALU.add).then_inc(scattered, 16)

            def emit(e, k, r):
                if not known(e, *range(E - GR, E)):
                    gather(e + GR, k)
                add(e, k)
                if not known(e, 0, *range(E - GR + 1, E)):
                    columns(e + GR - 1, (k - 1) % GR)

            for e in range(GR):
                gather(e, e)
                columns(e, e)
            for k in range(2):
                pool.wait_ge(s_stored[k], 16 * (NB + 1))
            pool.wait_ge(spare_stored, 16)
            by_rounds(pool, emit)

        def experts_tensor(pe):
            pe.wait_ge(s_added, TT + BT)
            pe.wait_ge(s_hidden, NSF * NBLK + 2)
            pe.wait_ge(table_kept, NB + 1)

            def turn(e, k, r):
                pe.wait_ge(gathered[k], 16 * (r + 1))
                if not known(e, 0):
                    pe.wait_ge(xgT_ready, e)
                for c in range(HC):
                    last = nc.tensor.transpose(bank(0)[:, c * C:(c + 1) * C], xg[k][:, c * P:(c + 1) * P], ident[0:C, 0:C])
                last.then_inc(xg_turned, 1)

            def up(e, k, r):
                pe.wait_ge(xgT_ready, e + 1)
                pe.wait_ge(wgu_loaded[k], 16 * (r + 1))
                if not known(e, 0, 1):
                    pe.wait_ge(e_hidden, 2 * (e - 1))
                for b0, off in ((1 + k % 2, 0), (3 + k % 2, I)):
                    for f, (f0, fn) in enumerate(FT):
                        for c in range(HC):
                            last = nc.tensor.matmul(bank(b0)[0:fn, f * C:(f + 1) * C], wgu[k][:, c, off + f0:off + f0 + fn],
                                                    xgT[k % 2][:, c, :], start=(c == 0), stop=(c == HC - 1))
                last.then_inc(e_up, 1)

            def down(e, k, r):
                pe.wait_ge(e_hidden, 2 * (e + 1))
                pe.wait_ge(wd_loaded[k], 32 * (r + 1))
                if not known(e, 0, 1):
                    pe.wait_ge(e_scaled, e - 1)
                for f, (f0, fn) in enumerate(FT):
                    last = nc.tensor.matmul(bank(5 + k % 2)[0:C, :], e_hid[k % 2][0:fn, f, :], wd[k][0:fn, f, :],
                                            start=(f == 0), stop=(f == len(FT) - 1))
                last.then_inc(e_down, 1)

            def ahead(step, e, k, r, n):
                step(e + n, (k + n) % GR, r + (k + n) // GR)

            def emit(e, k, r):
                if not known(e, E - 1):
                    ahead(up, e, k, r, 1)
                if not known(e, E - 2, E - 1):
                    ahead(turn, e, k, r, 2)
                down(e, k, r)

            turn(0, 0, 0)
            up(0, 0, 0)
            turn(1, 1, 0)
            by_rounds(pe, emit)

        def experts_scalar(act):
            def copy_T(e, k, r):
                act.wait_ge(xg_turned, e + 1)
                if not known(e, 0, 1):
                    act.wait_ge(e_up, e - 1)
                nc.scalar.activation(xgT[k % 2][:], bank(0)[:, 0:HC * C].rearrange("p (c n) -> p c n", c=HC), ACT.Copy)\
                  .then_inc(xgT_ready, 1)

            def silu(e, k, r):
                act.wait_ge(e_up, e + 1)
                if not known(e, 0, 1):
                    act.wait_ge(e_hidden, 2 * (e - 1))
                nc.scalar.activation(e_sig[k % 2][:, 0:2, :], bank(1 + k % 2)[:, 0:2 * C].rearrange("p (f n) -> p f n", f=2),
                                     ACT.Silu).then_inc(e_silu, 1)
                nc.scalar.activation(e_sig[k % 2][0:FT[2][1], 2, :], bank(1 + k % 2)[0:FT[2][1], 2 * C:3 * C],
                                     ACT.Silu).then_inc(e_silu, 1)

            def emit(e, k, r):
                silu(e, k, r)
                if not known(e, E - 1):
                    copy_T(e + 1, (k + 1) % GR, r)

            copy_T(0, 0, 0)
            by_rounds(act, emit)

        def experts_vector(dve):
            def hidden(e, k, r):
                dve.wait_ge(e_silu, 2 * e + 2)
                if not known(e, 0, 1):
                    dve.wait_ge(e_down, e - 1)
                nc.vector.tensor_tensor(e_hid[k % 2][:, 0:2, :], e_sig[k % 2][:, 0:2, :],
                                        bank(3 + k % 2)[:, 0:2 * C].rearrange("p (f n) -> p f n", f=2),
                                        ALU.mult).then_inc(e_hidden, 1)
                nc.vector.tensor_tensor(e_hid[k % 2][0:FT[2][1], 2, :], e_sig[k % 2][0:FT[2][1], 2, :],
                                        bank(3 + k % 2)[0:FT[2][1], 2 * C:3 * C], ALU.mult).then_inc(e_hidden, 1)

            def scale(e, k, r):
                dve.wait_ge(e_down, e + 1)
                dve.wait_ge(cols_ready, 2 * e + 2)
                if not known(e, 0, 1):
                    dve.wait_ge(scattered, 16 * (e - 1))
                nc.vector.tensor_scalar(e_out[k % 2][:], bank(5 + k % 2)[0:C, :], w_col[k][:, 0:1], None,
                                        ALU.mult).then_inc(e_scaled, 1)

            def emit(e, k, r):
                if not known(e, E - 1):
                    hidden(e + 1, (k + 1) % GR, r)
                scale(e, k, r)

            hidden(0, 0, 0)
            by_rounds(dve, emit)

        def finish_sync(sp):
            sp.wait_ge(scattered, 16 * E)
            sp.wait_ge(s_added, TT + BT)
            with sp.Fori(0, NB) as b:
                for k in range(2):
                    sp.wait_ge(f_done, 2 * BT * b + BT * k + BT)
                    rows = bass.ds((2 * b + k) * BLK, BLK)
                    sp.dma_start(f_in[k][:], total[rows, :].rearrange("(t p) h -> p t h", p=P)).then_inc(f_loaded[k], 16)
            for k in range(2):
                sp.wait_ge(f_stored[k], 16 * (NB + 1))

        def finish_vector(dve):
            with dve.Fori(0, NB) as b:
                for k in range(2):
                    dve.wait_ge(f_loaded[k], 16 * b + 16)
                    dve.wait_ge(f_stored[k], 16 * b + 16)

                    def stats(t):
                        n = BT * (2 * b + k) + t
                        nc.vector.bn_stats(stats2[t % 2][:], f_in[k][:, t, :]).then_inc(f_stats, 1)
                        dve.wait_ge(f_stats, n + 1)
                        settle(dve)
                        nc.vector.bn_aggr(mv2[t % 2][:], stats2[t % 2][:]).then_inc(f_mv, 1)

                    stats(0)
                    for t in range(BT):
                        n = BT * (2 * b + k) + t
                        if t + 1 < BT:
                            stats(t + 1)
                        dve.wait_ge(f_std, n + 1)
                        nc.vector.reciprocal(std2[t % 2][:, 1:2], std2[t % 2][:, 0:1]).then_inc(f_inv, 1)
                        dve.wait_ge(f_inv, n + 1)
                        nc.vector.tensor_scalar(f_out[k][:, t, :], f_in[k][:, t, :], mv2[t % 2][:, 0:1], std2[t % 2][:, 1:2],
                                                ALU.subtract, ALU.mult).then_inc(f_done, 1)

        def finish_scalar(act):
            for k in range(2):
                act.sem_inc(f_stored[k], 16)
            with act.Fori(0, NB) as b:
                for k in range(2):
                    for t in range(BT):
                        act.wait_ge(f_mv, BT * (2 * b + k) + t + 1)
                        nc.scalar.activation(std2[t % 2][:, 0:1], mv2[t % 2][:, 1:2], ACT.Sqrt, bias=eps_col[:],
                                             scale=1.0).then_inc(f_std, 1)
                    act.wait_ge(f_done, 2 * BT * b + BT * k + 3 * BT)
                    rows = bass.ds((2 * b + k) * BLK, BLK)
                    act.dma_start(of[rows, :].rearrange("(t p) h -> p t h", p=P), f_out[k][:]).then_inc(f_stored[k], 16)

        block = ctx.enter_context(nc.Block())

        @block.sync
        def _(sp):
            project_sync(sp)
            attend_sync(sp)
            mix_sync(sp)
            shared_sync(sp)
            experts_sync(sp)
            finish_sync(sp)

        @block.gpsimd
        def _(pool):
            project_pool(pool)
            attend_pool(pool)
            mix_pool(pool)
            route_pool(pool)
            experts_pool(pool)

        @block.tensor
        def _(pe):
            pe.sem_inc(v_done, 2)
            project_tensor(pe)
            attend_tensor(pe)
            mix_tensor(pe)
            route_tensor(pe)
            pe.sem_inc(s_down, BT)
            pe.sem_inc(table_done, 2)
            shared_tensor(pe)
            experts_tensor(pe)

        @block.scalar
        def _(act):
            for k in range(2):
                act.sem_inc(parts_stored[k], 16)
            project_scalar(act)
            attend_scalar(act)
            mix_scalar(act)
            route_scalar(act)
            shared_scalar(act)
            experts_scalar(act)
            finish_scalar(act)

        @block.vector
        def _(dve):
            project_vector(dve)
            attend_vector(dve)
            mix_vector(dve)
            route_vector(dve)
            shared_vector(dve)
            experts_vector(dve)
            dve.sem_inc(f_done, 2 * BT)
            finish_vector(dve)


_INS = ["L0_attn_hidden_state", "L0_attn_Wq", "L0_attn_bq", "L0_attn_Wk", "L0_attn_bk", "L0_attn_Wv", "L0_attn_bv",
        "L0_attn_Wo", "L0_attn_bo", "L0_ffn_gate_w", "L0_ffn_w_gate_up", "L0_ffn_w_down", "L0_ffn_ws_gate_up",
        "L0_ffn_ws_down"]


def kernel(**inputs):
    import numpy as np
    import concourse.bacc as bacc
    from concourse.bass_utils import run_bass_kernel_spmd as run

    nc = bacc.Bacc("TRN2", target_bir_lowering=False, num_devices=1)
    arrays, args = {}, []
    for name in _INS:
        a = np.ascontiguousarray(inputs[name])
        arrays[f"in_{name}"] = a
        args.append(nc.dram_tensor(f"in_{name}", a.shape, mybir.dt.from_np(a.dtype), kind="ExternalInput").ap())
    args.append(nc.dram_tensor("out_0", (NB, SEQ, H), F32, kind="ExternalOutput").ap())
    build(nc, *args)
    return run(nc, [arrays], core_ids=[0]).results[0]["out_0"]
```

```python
from contextlib import ExitStack

import concourse.bass as bass
from concourse import mybir

F32 = mybir.dt.float32
BF16 = mybir.dt.bfloat16
I32 = mybir.dt.int32
U32 = mybir.dt.uint32
ALU = mybir.AluOpType
ACT = mybir.ActivationFunctionType
AX = mybir.AxisListType

P = 128
NB, SEQ, H = 2, 1024, 512
T = NB * SEQ
HC = H // P
NH, NG, HD = 32, 8, 16
REP = NH // NG
KV = NG * HD
UNITS = NB * NG
QT = SEQ // P
BLK = 512
NBLK = T // BLK
BT = BLK // P
TT = T // P
TERMS = [(0, 0), (0, 1), (1, 0), (1, 1), (0, 2), (2, 0)]
KR = HD * len(TERMS)
KM = KR + 3
STEPS = 2 * QT
S_PER_STEP = 2
NS = REP * QT // 2
LEAD = 12
E, K, G, TG = 32, 6, 8, 3
C = 96
SCALE = 16.0
I = 352
FT = [(0, 128), (128, 128), (256, 96)]
SI = 704
SFT = [(n * P, min(P, SI - n * P)) for n in range((SI + P - 1) // P)]
NSF = len(SFT)
SLOT_EXPERTS = 2
FIRST_TABLE_STEP = 4
FP, FR = 2, 4
EPS = 1e-5
ROOM1, ROOM3 = 2048, 256
GR = 4


def build(nc, x, Wq, bq, Wk, bk, Wv, bv, Wo, bo, gate_w, w_gate_up, w_down, ws_gate_up, ws_down, out):
    xf = x.rearrange("b s h -> (b s) h")
    of = out.rearrange("b s h -> (b s) h")
    q_parts = nc.dram_tensor("q_parts", (3, H, T), BF16).ap()
    k_parts = nc.dram_tensor("k_parts", (3, KV, T), BF16).ap()
    o_raw = nc.dram_tensor("o_raw", (UNITS, P, SEQ), F32).ap()
    inv_den = nc.dram_tensor("inv_den", (NB * NH, SEQ), F32).ap()
    x1_rows = nc.dram_tensor("x1_rows", (T, H), F32).ap()
    x1T_blocks = nc.dram_tensor("x1T_blocks", (NBLK, P, HC * BLK), F32).ap()
    total = nc.dram_tensor("total", (T + C, H), F32).ap()

    with ExitStack() as ctx:
        def sb(name, shape, dt, where=ctx):
            return where.enter_context(nc.sbuf_tensor(name, shape, dt))

        def sem(name):
            return ctx.enter_context(nc.semaphore(name))

        pair = [ctx.enter_context(nc.psum_tensor(f"pair{n}", [P, 1024], F32)) for n in range(4)]

        def bank(n):
            return pair[n // 2][:, (n % 2) * 512:(n % 2) * 512 + 512]

        ident = sb("ident", [P, P], F32)
        Wo_sb = sb("Wo_sb", [P, HC, H], F32)
        bo_bc = sb("bo_bc", [P, H], F32)
        gw_rows = sb("gw_rows", [E, H], F32)
        gwT = sb("gwT", [P, HC, E], F32)
        wsgu = sb("wsgu", [P, HC, 2 * SI], F32)
        wsd = sb("wsd", [P, NSF, H], F32)
        eps_col = sb("eps_col", [P, 1], F32)
        den_c = [sb(f"den_c{b}", [P, NH * SEQ // P], F32) for b in range(NB)]

        st1 = ExitStack()
        V_all = sb("V_all", [P, UNITS, QT, 32], F32, st1)
        V_unit = [sb(f"V_unit{k}", [P, QT, 32], F32, st1) for k in range(3)]
        Qa = [sb(f"Qa{k}", [KM, 2, REP, BLK], BF16, st1) for k in range(3)]
        Ka = [sb(f"Ka{k}", [KM, SEQ], BF16, st1) for k in range(3)]
        probs = [sb(f"probs{k}", [P, REP, BLK], F32, st1) for k in range(2)]
        rowmax = [sb(f"rowmax{k}", [P, NS], F32, st1) for k in range(2)]
        max_full = [sb(f"max_full{k}", [NS, P], F32, st1) for k in range(2)]
        max_rest = sb("max_rest", [NS, P], F32, st1)
        max_split = [sb(f"max_split{k}", [NS, 3, P], BF16, st1) for k in range(2)]
        o_sb = [sb(f"o_sb{k}", [P, BLK], F32, st1) for k in range(2)]
        sb("room1", [P, ROOM1], F32, st1)
        Wq_sb = sb("Wq_sb", [P, HC, H], F32, st1)
        Wk_sb = sb("Wk_sb", [P, HC, KV], F32, st1)
        Wv_sb = sb("Wv_sb", [P, HC, KV], F32, st1)
        bias_in = sb("bias_in", [P, HC + 1], F32, st1)
        bias_qk = sb("bias_qk", [P, HC + 1], F32, st1)
        bv_bc = sb("bv_bc", [P, KV], F32, st1)
        x_in = [sb(f"x_in{k}", [P, BT, H], F32, st1) for k in range(2)]
        xT = [sb(f"xT{k}", [P, HC, BLK], F32, st1) for k in range(2)]
        qk_full = [sb(f"qk_full{k}", [P, BLK], F32, st1) for k in range(2)]
        qk_rest = [sb(f"qk_rest{k}", [P, BLK], F32, st1) for k in range(2)]
        qk_split = [sb(f"qk_split{k}", [P, 3, BLK], BF16, st1) for k in range(2)]
        st1.close()

        st2 = ExitStack()
        logits = sb("logits", [P, TT, E], F32, st2)
        masked = sb("masked", [P, TT, E], F32, st2)
        gmax = sb("gmax", [P, TT, G], F32, st2)
        top8 = sb("top8", [P, TT, 8], F32, st2)
        r_gt = sb("r_gt", [P, TT, E], F32, st2)
        r_eq = sb("r_eq", [P, TT, E], F32, st2)
        r_cum = sb("r_cum", [P, TT, E], F32, st2)
        n_gt = sb("n_gt", [P, TT], F32, st2)
        keep_g = sb("keep_g", [P, TT, G], F32, st2)
        sel = sb("sel", [P, TT, E], F32, st2)
        sel_bf = sb("sel_bf", [P, TT, E], BF16, st2)
        seg8 = sb("seg8", [P, TT, G], F32, st2)
        seg16 = sb("seg16", [P, E, TT], F32, st2)
        seg32 = sb("seg32", [P, TT, E], F32, st2)
        zsum = sb("zsum", [P, TT], F32, st2)
        weight = sb("weight", [P, TT, E], F32, st2)
        tile_count = sb("tile_count", [P, E, TT], F32, st2)
        tile_cum = sb("tile_cum", [P, E, TT], F32, st2)
        slot_of = sb("slot_of", [P, E, TT], BF16, st2)
        before = sb("before", [P, P], BF16, st2)
        all_ones = sb("all_ones", [P, P], BF16, st2)
        iota_c = sb("iota_c", [P, TT, C], BF16, st2)
        facts = sb("facts", [P, E, TT, 6], BF16, st2)
        onehot = [sb(f"onehot{k}", [P, TT, C], BF16, st2) for k in range(2)]
        spare_row = sb("spare_row", [C, 1], F32, st2)
        table = sb("table", [C, E, 6], F32, st2)
        slot_w = sb("slot_w", [C, E], F32, st2)
        slot_src = sb("slot_src", [C, E], F32, st2)
        slot_src_i = sb("slot_src_i", [C, E], I32, st2)
        slot_dst_i = sb("slot_dst_i", [C, E], I32, st2)
        src_i = [sb(f"src_i{k}", [C, 1], I32, st2) for k in range(GR)]
        dst_i = [sb(f"dst_i{k}", [C, 1], I32, st2) for k in range(GR)]
        w_col = [sb(f"w_col{k}", [C, 1], F32, st2) for k in range(GR)]
        zero_rows = sb("zero_rows", [C, H], F32, st2)
        st3 = ExitStack()
        pre1 = [sb(f"pre1_{k}", [P, H], F32, st3) for k in range(2)]
        stats1 = [sb(f"stats1_{k}", [P, 6], F32, st3) for k in range(2)]
        mv1 = [sb(f"mv1_{k}", [P, 2], F32, st3) for k in range(2)]
        std1 = [sb(f"std1_{k}", [P, 2], F32, st3) for k in range(2)]
        x1_out = [sb(f"x1_out{k}", [P, BT, H], F32, st3) for k in range(2)]
        x1T = [sb(f"x1T{k}", [P, HC, BLK], F32, st3) for k in range(2)]
        sb("room3", [P, ROOM3], F32, st3)
        num = [sb(f"num{k}", [P, HC, BLK], F32, st3) for k in range(2)]
        inv = [sb(f"inv{k}", [P, HC, BLK], F32, st3) for k in range(2)]
        x_res = [sb(f"x_res{k}", [P, BT, H], F32, st3) for k in range(2)]
        st3.close()
        st6 = ExitStack()
        wgu = [sb(f"wgu{k}", [P, HC, 2 * I], F32, st6) for k in range(2)]
        wd = [sb(f"wd{k}", [P, len(FT), H], F32, st6) for k in range(2)]
        xg = [sb(f"xg{k}", [C, H], F32, st6) for k in range(GR)]
        xgT = [sb(f"xgT{k}", [P, HC, C], F32, st6) for k in range(2)]
        e_sig = [sb(f"e_sig{k}", [P, len(FT), C], F32, st6) for k in range(2)]
        e_hid = [sb(f"e_hid{k}", [P, len(FT), C], F32, st6) for k in range(2)]
        e_out = [sb(f"e_out{k}", [C, H], F32, st6) for k in range(2)]

        st4 = ExitStack()
        sx = [sb(f"sx{k}", [P, HC, BLK], F32, st4) for k in range(2)]
        sx_rows = sb("sx_rows", [P, BT, H], F32, st4)
        s_sig = [sb(f"s_sig{k}", [P, BLK], F32, st4) for k in range(2)]
        s_hid = sb("s_hid", [P, NSF, BLK], F32, st4)
        s_sum = [sb(f"s_sum{k}", [P, BT, H], F32, st4) for k in range(2)]
        st4.close()
        st7 = ExitStack()
        wgu += [sb(f"wgu{k}", [P, HC, 2 * I], F32, st7) for k in range(2, GR)]
        wd += [sb(f"wd{k}", [P, len(FT), H], F32, st7) for k in range(2, GR)]
        st7.close()
        st5 = ExitStack()
        f_in = [sb(f"f_in{k}", [P, FP, H], F32, st5) for k in range(FR)]
        f_out = [sb(f"f_out{k}", [P, FP, H], F32, st5) for k in range(FR)]
        stats2 = [sb(f"stats2_{k}", [P, FP, 6], F32, st5) for k in range(2)]
        mv2 = [sb(f"mv2_{k}", [P, FP, 2], F32, st5) for k in range(2)]
        std2 = [sb(f"std2_{k}", [P, FP, 1], F32, st5) for k in range(2)]
        inv2 = [sb(f"inv2_{k}", [P, FP, 1], F32, st5) for k in range(2)]
        shift2 = [sb(f"shift2_{k}", [P, FP, 1], F32, st5) for k in range(2)]
        st5.close()
        st6.close()
        st2.close()

        w_loaded = sem("w_loaded")
        w2_loaded = sem("w2_loaded")
        consts_made = sem("consts_made")
        ones_made = sem("ones_made")
        pool_step = sem("pool_step")
        bias_ready = sem("bias_ready")
        x_loaded = [sem(f"x_loaded{k}") for k in range(2)]
        x_turned = sem("x_turned")
        xT_act = sem("xT_act")
        xT_dve = sem("xT_dve")
        blk_projected = sem("blk_projected")
        job_done = sem("job_done")
        v_done = sem("v_done")
        v_kept = sem("v_kept")
        part1 = sem("part1")
        full_ready = sem("full_ready")
        rest_ready = sem("rest_ready")
        part2 = sem("part2")
        part3 = sem("part3")
        parts_stored = [sem(f"parts_stored{k}") for k in range(2)]
        gw_loaded = sem("gw_loaded")
        gw_turned = sem("gw_turned")
        gw_ready = sem("gw_ready")
        qk_loaded = [sem(f"qk_loaded{k}") for k in range(3)]
        v_unit_ready = sem("v_unit_ready")
        s_ready = sem("s_ready")
        s_reduced = sem("s_reduced")
        max_turned = sem("max_turned")
        max_kept = sem("max_kept")
        max_step = sem("max_step")
        max_ready = sem("max_ready")
        max_rows = [sem(f"max_rows{k}") for k in range(2)]
        st_ready = sem("st_ready")
        exp_done = sem("exp_done")
        pv_done = sem("pv_done")
        o_copied = sem("o_copied")
        o_stored = [sem(f"o_stored{k}") for k in range(2)]
        den_loaded = sem("den_loaded")
        inv_stored = sem("inv_stored")
        nd_loaded = [sem(f"nd_loaded{k}") for k in range(2)]
        res_loaded = [sem(f"res_loaded{k}") for k in range(2)]
        res_ready = sem("res_ready")
        den_inv = sem("den_inv")
        mix_in = sem("mix_in")
        y_done = sem("y_done")
        pre_done = sem("pre_done")
        stats_done = sem("stats_done")
        mv_done = sem("mv_done")
        std_done = sem("std_done")
        inv_done = sem("inv_done")
        x1_done = sem("x1_done")
        x1_turned = sem("x1_turned")
        x1T_kept = sem("x1T_kept")
        logit_done = sem("logit_done")
        logit_kept = sem("logit_kept")
        x1_stored = [sem(f"x1_stored{k}") for k in range(2)]
        x1T_stored = [sem(f"x1T_stored{k}") for k in range(2)]
        r_step = sem("r_step")
        r_consts = sem("r_consts")
        rp_step = sem("rp_step")
        r_diff = sem("r_diff")
        r_exp = sem("r_exp")
        sel_ready = sem("sel_ready")
        counts_done = sem("counts_done")
        pos_done = sem("pos_done")
        facts_ready = sem("facts_ready")
        hot_ready = sem("hot_ready")
        table_done = sem("table_done")
        table_kept = sem("table_kept")
        slots_ready = sem("slots_ready")
        sx_loaded = [sem(f"sx_loaded{k}") for k in range(2)]
        sx1_loaded = sem("sx1_loaded")
        s_gate = sem("s_gate")
        s_up = sem("s_up")
        s_silu = sem("s_silu")
        s_hidden = sem("s_hidden")
        s_down = sem("s_down")
        s_added = sem("s_added")
        s_stored = [sem(f"s_stored{k}") for k in range(2)]
        spare_zero = sem("spare_zero")
        spare_stored = sem("spare_stored")
        wgu_loaded = [sem(f"wgu_loaded{k}") for k in range(GR)]
        wd_loaded = [sem(f"wd_loaded{k}") for k in range(GR)]
        src_ready = sem("src_ready")
        cols_ready = sem("cols_ready")
        gathered = [sem(f"gathered{k}") for k in range(GR)]
        xg_turned = sem("xg_turned")
        xgT_ready = sem("xgT_ready")
        e_up = sem("e_up")
        e_silu = sem("e_silu")
        e_hidden = sem("e_hidden")
        e_down = sem("e_down")
        e_scaled = sem("e_scaled")
        scattered = sem("scattered")
        f_loaded = [sem(f"f_loaded{k}") for k in range(FR)]
        f_stats = sem("f_stats")
        f_mv = sem("f_mv")
        f_std = sem("f_std")
        f_inv = sem("f_inv")
        f_shift = sem("f_shift")
        f_even = sem("f_even")
        f_odd = sem("f_odd")
        f_stored = [sem(f"f_stored{k}") for k in range(FR)]

        waited = {e.engine: sem(f"waited_{n}") for n, e in (("pool", nc.gpsimd), ("dve", nc.vector), ("sp", nc.sync))}

        def settle(eng):
            eng.sem_inc(waited[eng.engine], 1)

        JOBS = HC + 1
        EARLY = NBLK // NB
        EARLY_TILES = S_PER_STEP * LEAD
        SKIPPED = (NBLK - EARLY) * (2 * JOBS + BT) - EARLY_TILES

        def early_tile(blk, j, a):
            i = (blk - EARLY) * (2 * JOBS + BT) + 2 * j + a - SKIPPED
            return i if i >= 0 else None

        def job_bank(blk, j):
            return bank(2 + j) if blk < EARLY else bank(4 + (JOBS * (blk - EARLY) + j) % 3)


        def project_sync(sp):
            sp.dma_start(x_in[0][:], xf[0:BLK, :].rearrange("(t p) h -> p t h", p=P)).then_inc(x_loaded[0], 16)
            for dst, src in ((Wq_sb, Wq), (Wk_sb, Wk), (Wv_sb, Wv)):
                sp.dma_start(dst[:], src.rearrange("(c p) n -> p c n", p=P)).then_inc(w_loaded, 16)
            with nc.allow_non_contiguous_dma(reason="biases as columns"):
                sp.dma_start(bias_in[:, 0:HC], bq.rearrange("(c p) -> p c", p=P)).then_inc(w_loaded, 16)
                sp.dma_start(bias_in[:, HC:HC + 1], bk.rearrange("(c p) -> p c", p=P)).then_inc(w_loaded, 16)
            sp.dma_start(bv_bc[:], bv.rearrange("(a n) -> a n", a=1).broadcast_to([P, KV])).then_inc(w_loaded, 16)
            sp.dma_start(x_in[1][:], xf[BLK:2 * BLK, :].rearrange("(t p) h -> p t h", p=P)).then_inc(x_loaded[1], 16)
            sp.dma_start(gw_rows[:], gate_w).then_inc(gw_loaded, 16)
            for blk in range(NBLK):
                if 1 <= blk < NBLK - 1:
                    sp.wait_ge(x_turned, HC * blk)
                    rows = xf[(blk + 1) * BLK:(blk + 2) * BLK, :]
                    sp.dma_start(x_in[(blk + 1) % 2][:], rows.rearrange("(t p) h -> p t h", p=P))\
                      .then_inc(x_loaded[(blk + 1) % 2], 16)
                if blk == EARLY:
                    for k in range(2):
                        sp.wait_ge(parts_stored[k], 16 * (JOBS + 1))
                    load_unit(sp, 0, 0)
                for j in range(JOBS):
                    m = JOBS * blk + j
                    sp.wait_ge(part3, m + 1)
                    tok = slice(blk * BLK, (blk + 1) * BLK)
                    dst = q_parts[:, j * P:(j + 1) * P, tok] if j < HC else k_parts[:, :, tok]
                    sp.dma_start(dst.rearrange("s p n -> p s n"), qk_split[m % 2][:]).then_inc(parts_stored[m % 2], 16)
                if blk == EARLY:
                    load_unit(sp, 1, 1)

        def project_pool(pool):
            pool.sem_inc(max_ready, 2)
            nc.gpsimd.memset(ident[:], 0.0).then_inc(pool_step, 1)
            pool.wait_ge(pool_step, 1)
            nc.gpsimd.affine_select(out=ident[:], in_=ident[:], compare_op=ALU.not_equal, fill=1.0, base=0,
                                    pattern=[[-1, P]], channel_multiplier=1).then_inc(consts_made, 1)
            pool.wait_ge(consts_made, 1)
            nc.gpsimd.memset(eps_col[:], EPS).then_inc(consts_made, 1)
            pool.wait_ge(consts_made, 2)
            for k in range(3):
                nc.gpsimd.memset(Ka[k][KR:KM, :], -1.0).then_inc(consts_made, 1)
                pool.wait_ge(consts_made, 3 + k)
            with pool.Fori(0, NB) as i:
                for m in range(2 * JOBS):
                    pool.wait_ge(rest_ready, 2 * JOBS * i + m + 3)
                    settle(pool)
                    nc.gpsimd.tensor_copy(qk_split[m % 2][:, 1, :], qk_rest[m % 2][:]).then_inc(part2, 1)

        def project_tensor(pe):
            pe.wait_ge(consts_made, 5)

            def turn(blk, c):
                k = blk % 2
                if c == 0:
                    pe.wait_ge(x_loaded[k], 16 * (blk // 2) + 16)
                pe.wait_ge(xT_act if c % 2 == 0 else xT_dve, 2 * blk + c // 2 + 1)
                for t in range(BT):
                    last = nc.tensor.transpose(bank(c % 2)[:, t * P:(t + 1) * P], x_in[k][:, t, c * P:(c + 1) * P], ident[:])
                last.then_inc(x_turned, 1)

            def early(blk, j, a):
                i = early_tile(blk, j, a)
                if i is None:
                    return
                g, n = i // NS, i % NS
                if i == 0:
                    pe.wait_ge(qk_loaded[0], LOADS)
                pe.wait_ge(s_reduced, i + 2)
                if i == NS + 1:
                    nc.tensor.transpose(pair[1][0:NS, 0:P], rowmax[0][:], ident[:]).then_inc(max_turned, 1)
                    pe.wait_ge(max_kept, 1)
                h, qt = n // (QT // 2), n % (QT // 2)
                for half in range(2):
                    last = nc.tensor.matmul(pair[1][:, half * 512:(half + 1) * 512], Qa[0][0:KR, g, h, qt * P:(qt + 1) * P],
                                            Ka[0][0:KR, half * 512:(half + 1) * 512], start=True, stop=True)
                last.then_inc(s_ready, 1)

            for c in range(HC):
                turn(0, c)
            pe.wait_ge(w_loaded, 96)
            for blk in range(NBLK):
                k = blk % 2
                pe.wait_ge(xT_act, 2 * blk + 3)
                pe.wait_ge(xT_dve, 2 * blk + 3)
                for j in range(JOBS):
                    pe.wait_ge(full_ready, JOBS * blk + j + (1 if blk < EARLY else JOBS - 2))
                    w = Wq_sb[:, :, j * P:(j + 1) * P] if j < HC else Wk_sb[:]
                    for c in range(HC):
                        last = nc.tensor.matmul(job_bank(blk, j), w[:, c, :], xT[k][:, c, :], start=(c == 0), stop=(c == HC - 1))
                        if c == HC // 2 - 1:
                            early(blk, j, 0)
                    last.then_inc(job_done, 1)
                    early(blk, j, 1)
                    if j < HC and blk + 1 < NBLK:
                        turn(blk + 1, j)
                pe.wait_ge(v_kept, blk + 1)
                for t in range(BT):
                    for c in range(HC):
                        last = nc.tensor.matmul(bank(7)[:, t * P:(t + 1) * P], xT[k][:, c, t * P:(t + 1) * P],
                                                Wv_sb[:, c, :], start=(c == 0), stop=(c == HC - 1))
                    if t == BT - 1:
                        last.then_inc(v_done, 1)
                    early(blk, JOBS, t)

        def project_scalar(act):
            act.sem_inc(xT_act, 1)
            act.sem_inc(full_ready, JOBS)
            act.wait_ge(bias_ready, 2)

            def keep(blk, c):
                act.wait_ge(x_turned, HC * blk + c + 1)
                act.wait_ge(v_done, blk + 1)
                nc.scalar.activation(xT[blk % 2][:, c, :], bank(0), ACT.Copy).then_inc(xT_act, 1)

            for c in (0, 2):
                keep(0, c)
            for blk in range(NBLK):
                for j in range(JOBS):
                    n = JOBS * blk + j
                    m = n % 2
                    act.wait_ge(job_done, n + 1)
                    act.wait_ge(rest_ready, n + 1)
                    nc.scalar.activation(qk_full[m][:], job_bank(blk, j), ACT.Identity, bias=bias_qk[:, j:j + 1],
                                         scale=HD ** -0.5 if j < HC else 1.0).then_inc(full_ready, 1)
                    if j in (0, 2) and blk + 1 < NBLK:
                        keep(blk + 1, j)
                    act.wait_ge(full_ready, n + JOBS + 1)
                    act.wait_ge(parts_stored[m], 16 * (n // 2) + 16)
                    nc.scalar.activation(qk_split[m][:, 0, :], qk_full[m][:], ACT.Copy).then_inc(part1, 1)

        def project_vector(dve):
            dve.sem_inc(xT_dve, 1)
            dve.sem_inc(s_reduced, 2)
            dve.sem_inc(rest_ready, 2)
            nc.vector.memset(V_all[:], 1.0).then_inc(ones_made, 1)
            dve.wait_ge(w_loaded, 96)
            nc.vector.tensor_scalar(bias_qk[:, 0:HC], bias_in[:, 0:HC], HD ** -0.5, None, ALU.mult).then_inc(bias_ready, 1)
            nc.vector.tensor_copy(bias_qk[:, HC:HC + 1], bias_in[:, HC:HC + 1]).then_inc(bias_ready, 1)
            dve.sem_inc(v_kept, 1)
            dve.wait_ge(ones_made, 1)

            def keep(blk, c):
                dve.wait_ge(x_turned, HC * blk + c + 1)
                dve.wait_ge(v_done, blk + 1)
                nc.vector.tensor_copy(xT[blk % 2][:, c, :], bank(1)).then_inc(xT_dve, 1)

            def early(blk, j, a):
                i = early_tile(blk, j, a)
                if i is not None:
                    if i == NS + 1:
                        keep_max(dve, 0, 0, pair[1])
                    reduce_tile(dve, i // NS, i // NS, i % NS, pair[1])

            for c in (1, 3):
                keep(0, c)
            for blk in range(NBLK):
                for a in range(2):
                    early(blk, 0, a)
                for j in range(JOBS):
                    n = JOBS * blk + j
                    m = n % 2
                    dve.wait_ge(part1, n + 1)
                    dve.wait_ge(full_ready, n + JOBS + 1)
                    nc.vector.tensor_tensor(qk_rest[m][:], qk_full[m][:], qk_split[m][:, 0, :],
                                            ALU.subtract).then_inc(rest_ready, 1)
                    if j in (1, 3) and blk + 1 < NBLK:
                        keep(blk + 1, j)
                    early(blk, j + 1, 0)
                    dve.wait_ge(rest_ready, n + 3)
                    dve.wait_ge(part2, n + 1)
                    nc.vector.tensor_tensor(qk_split[m][:, 2, :], qk_rest[m][:], qk_split[m][:, 1, :],
                                            ALU.subtract).then_inc(part3, 1)
                    early(blk, j + 1, 1)
                for a in range(2, BT):
                    early(blk, JOBS, a)
                dve.wait_ge(v_done, blk + 3)
                b, t0 = blk // 2, blk % 2 * BT
                dst = V_all[:, b * NG:(b + 1) * NG, t0:t0 + BT, 0:HD].rearrange("p g t d -> p t g d")
                nc.vector.tensor_tensor(dst, bank(7).rearrange("p (t g d) -> p t g d", t=BT, g=NG),
                                        bv_bc[:].rearrange("p (a g d) -> p a g d", a=1, g=NG).broadcast_to([P, BT, NG, HD]),
                                        ALU.add).then_inc(v_kept, 1)
            dve.wait_ge(gw_turned, 1)
            nc.vector.tensor_copy(gwT[:], bank(7)[:, 0:HC * E].rearrange("p (c e) -> p c e", c=HC)).then_inc(gw_ready, 1)

        def known(e, *which):
            return isinstance(e, int) and e in which

        def load_unit(sp, u, buf):
            b, g = u // NG, u % NG
            for s, (kp, qp) in enumerate(TERMS):
                rows = slice(s * HD, (s + 1) * HD)
                for qb in range(2):
                    sp.dma_start(Qa[buf][rows, qb, :, :],
                                 q_parts[qp, bass.ds(g * REP * HD, REP * HD), bass.ds(b * SEQ + qb * BLK, BLK)]
                                 .rearrange("(h d) n -> d h n", h=REP)).then_inc(qk_loaded[buf], 16)
                sp.dma_start(Ka[buf][rows, :], k_parts[kp, bass.ds(g * HD, HD), bass.ds(b * SEQ, SEQ)])\
                  .then_inc(qk_loaded[buf], 16)

        LOADS = 48 * len(TERMS)

        def by_units(eng, emit):
            emit(0, 0, 0)
            with eng.Fori(0, 4) as r:
                for j in range(3):
                    emit(3 * r + 1 + j, (1 + j) % 3, r + (1 + j) // 3)
            for u in range(13, UNITS):
                emit(u, u % 3, u // 3)

        def attend_sync(sp):
            for k in range(2):
                sp.wait_ge(parts_stored[k], 16 * (JOBS * NB + 1))

            def max_to_rows(u, qb, buf):
                sp.wait_ge(max_ready, 2 * u + qb + 3)
                for s in range(3):
                    sp.dma_start(Qa[buf][KR + s:KR + s + 1, qb, :, :].rearrange("a h n -> a (h n)"),
                                 max_split[qb][:, s, :]).then_inc(max_rows[qb], 16)

            def store_o(u, qb):
                sp.wait_ge(o_copied, 2 * u + qb + 1)
                sp.dma_start(o_raw[u, :, qb * BLK:(qb + 1) * BLK] if isinstance(u, int) else
                             o_raw[bass.ds(u, 1), :, qb * BLK:(qb + 1) * BLK].rearrange("a p n -> (a p) n"),
                             o_sb[qb][:]).then_inc(o_stored[qb], 16)

            max_to_rows(0, 0, 0)
            sp.dma_start(Wo_sb[:], Wo.rearrange("(c p) n -> p c n", p=P)).then_inc(w2_loaded, 16)
            sp.dma_start(bo_bc[:], bo.rearrange("(a n) -> a n", a=1).broadcast_to([P, H])).then_inc(w2_loaded, 16)
            sp.dma_start(wsgu[:], ws_gate_up.rearrange("(c p) n -> p c n", p=P)).then_inc(w2_loaded, 16)
            full = SI // P
            sp.dma_start(wsd[:, 0:full, :],
                         ws_down[0:full * P, :].rearrange("(c p) n -> p c n", p=P)).then_inc(w2_loaded, 16)
            sp.dma_start(wsd[0:SI - full * P, full, :], ws_down[full * P:SI, :]).then_inc(w2_loaded, 16)


            def emit(u, buf, _):
                first = known(u, 0)
                if not first:
                    store_o(u - 1, 1)
                if not known(u, UNITS - 2, UNITS - 1):
                    if not first:
                        sp.wait_ge(st_ready, REP * STEPS * u)
                    load_unit(sp, u + 2, (buf + 2) % 3)
                if known(u, UNITS - 3):
                    load_den(sp, 0)
                max_to_rows(u, 1, buf)
                store_o(u, 0)
                if not known(u, UNITS - 1):
                    max_to_rows(u + 1, 0, (buf + 1) % 3)
                if known(u, UNITS - 3):
                    store_inv(sp, 0)
                    for k in range(2):
                        load_mix(sp, 0, k)

            by_units(sp, emit)
            store_o(UNITS - 1, 1)

        def attend_pool(pool):

            def split_max(u, qb):
                pool.wait_ge(max_kept, 2 * u + qb + 1)
                pool.wait_ge(max_rows[qb], 48 * u + 48)
                settle(pool)
                step = 3 * (2 * u + qb)
                nc.gpsimd.tensor_copy(max_split[qb][:, 0, :], max_full[qb][:]).then_inc(max_step, 1)
                pool.wait_ge(max_step, step + 1)
                settle(pool)
                nc.gpsimd.tensor_tensor(max_rest[:], max_full[qb][:], max_split[qb][:, 0, :], ALU.subtract).then_inc(max_step, 1)
                pool.wait_ge(max_step, step + 2)
                settle(pool)
                nc.gpsimd.tensor_copy(max_split[qb][:, 1, :], max_rest[:]).then_inc(max_step, 1)
                pool.wait_ge(max_step, step + 3)
                settle(pool)
                nc.gpsimd.tensor_tensor(max_split[qb][:, 2, :], max_rest[:], max_split[qb][:, 1, :],
                                        ALU.subtract).then_inc(max_ready, 1)

            def copy_V(u, k):
                nc.gpsimd.tensor_copy(V_unit[k][:].rearrange("p t d -> p (t d)"),
                                      V_all[:, bass.ds(u, 1), :, :].rearrange("p a t d -> p (a t d)")).then_inc(v_unit_ready, 1)

            for k in range(2):
                pool.sem_inc(max_rows[k], 48)
            split_max(0, 0)
            pool.wait_ge(v_kept, NBLK + 1)
            for k in range(2):
                copy_V(k, k)

            def emit(u, buf, _):
                split_max(u, 1)
                if not known(u, UNITS - 2, UNITS - 1):
                    if not known(u, 0):
                        pool.wait_ge(pv_done, STEPS * u)
                        settle(pool)
                    copy_V(u + 2, (buf + 2) % 3)
                if known(u, UNITS - 2, UNITS - 1):
                    for i in range(5):
                        mix_piece(pool, 0, i if u == UNITS - 2 else i + 8)
                if not known(u, UNITS - 1):
                    split_max(u + 1, 0)
                if known(u, UNITS - 2):
                    for i in range(5, 8):
                        mix_piece(pool, 0, i)
                if known(u, UNITS - 1):
                    for i in range(13, 16):
                        mix_piece(pool, 0, i)

            by_units(pool, emit)

        def score_half(pe, g, buf, n, half, round_):
            qb = n // NS
            n %= NS
            if half == 0:
                if n == 0 and qb == 0:
                    pe.wait_ge(qk_loaded[buf], LOADS * (round_ + 1))
                pe.wait_ge(s_reduced, NS * g + n + 1)
                if n == 2 and not known(g, 0):
                    pe.wait_ge(max_kept, g)
            h, qt = n // (QT // 2), n % (QT // 2)
            mm = nc.tensor.matmul(pair[n % 2][:, half * 512:(half + 1) * 512], Qa[buf][0:KR, qb, h, qt * P:(qt + 1) * P],
                                  Ka[buf][0:KR, half * 512:(half + 1) * 512], start=True, stop=True)
            if half == 1:
                mm.then_inc(s_ready, 1)

        def turn_max(pe, g, qb, last=False):
            pe.wait_ge(s_reduced, NS * (g + 1) + (2 if last else 3))
            nc.tensor.transpose(pair[0][0:NS, 0:P], rowmax[qb][:], ident[:]).then_inc(max_turned, 1)

        def stream_half(pe, u, buf, round_, j):
            i = j // 2
            rest = S_PER_STEP * (STEPS // 2 + LEAD - STEPS)
            if i < rest:
                score_half(pe, 2 * u + 1, buf, NS + NS - rest + i, j % 2, round_)
                return
            n = i - rest
            if j % 2 == 0 and n == 2:
                turn_max(pe, 2 * u + 1, 1)
            if j % 2 == 0 and n == NS + 2:
                turn_max(pe, 2 * u + 2, 0)
            score_half(pe, 2 * u + 2 + n // NS, (buf + 1) % 3, n, j % 2, round_ + (buf + 1) // 3)

        def attend_tensor(pe):
            pe.wait_ge(v_kept, NBLK + 1)
            pe.wait_ge(gw_loaded, 16)
            for c in range(HC):
                last = nc.tensor.transpose(bank(7)[:, c * E:(c + 1) * E], gw_rows[:, c * P:(c + 1) * P], ident[0:E, 0:E])
            last.then_inc(gw_turned, 1)
            pe.wait_ge(full_ready, JOBS * (NBLK + 1))
            pe.wait_ge(xT_act, 2 * NBLK + 1)
            pe.wait_ge(xT_dve, 2 * NBLK + 1)
            pe.wait_ge(gw_ready, 1)

            def pv(u, s, buf):
                qb, kt = s // QT, s % QT
                pe.wait_ge(exp_done, REP * (STEPS * u + s + 1))
                if s == 0:
                    pe.wait_ge(v_unit_ready, u + 1)
                if kt == 0 and not (known(u, 0) and s == 0):
                    pe.wait_ge(o_copied, 2 * u + qb)
                for h in range(REP):
                    last = nc.tensor.matmul(bank(7)[32 * h:32 * h + 32, :], V_unit[buf][:, kt, :],
                                            probs[s % 2][:, h, :], start=(kt == 0), stop=(kt == QT - 1),
                                            tile_position=(0, 32 * h))
                last.then_inc(pv_done, 1)

            def emit(u, buf, round_):
                first = known(u, 0)
                final = known(u, UNITS - 1)

                def st(s, h):
                    qb, kt = s // QT, s % QT
                    n = REP * s + h
                    if not (first and n < 3):
                        pe.wait_ge(exp_done, REP * STEPS * u + n - 2)
                    if h == 0 and kt == 0:
                        pe.wait_ge(max_rows[qb], 48 * u + 96)
                    mm = nc.tensor.matmul(bank(4 + (buf + n) % 3), Ka[buf][0:KM, kt * P:(kt + 1) * P],
                                          Qa[buf][0:KM, qb, h, :], start=True, stop=True)
                    mm.then_inc(st_ready, 1)

                def stream(s, a):
                    if not final or s < STEPS // 2 + LEAD - STEPS:
                        stream_half(pe, u, buf, round_, 2 * S_PER_STEP * s + a)

                for s in range(STEPS):
                    st(s, 0)
                    stream(s, 0)
                    st(s, 1)
                    stream(s, 1)
                    if s > 0:
                        pv(u, s - 1, buf)
                    elif not first:
                        pv(u - 1, STEPS - 1, (buf + 2) % 3)
                    st(s, 2)
                    stream(s, 2)
                    st(s, 3)
                    stream(s, 3)
                    if final and s == STEPS // 2 + LEAD - STEPS:
                        turn_max(pe, 2 * u + 1, 1, last=True)

            by_units(pe, emit)
            pv(UNITS - 1, STEPS - 1, (UNITS - 1) % 3)

        def attend_vector(dve):
            def maxima(g, qb, n0=0):
                if n0 == 0:
                    dve.wait_ge(max_turned, g + 1)
                for n in range(n0, NS):
                    if n == 1:
                        keep_max(dve, g - 1, 1 - qb, pair[0])
                    reduce_tile(dve, g, qb, n, pair[n % 2])

            maxima(1, 1, EARLY_TILES - NS)
            maxima(2, 0)
            with dve.Fori(1, UNITS - 2) as u:
                maxima(2 * u + 1, 1)
                maxima(2 * u + 2, 0)
            invert_den(dve, 0)
            for g in range(2 * UNITS - 3, 2 * UNITS):
                maxima(g, g % 2)
            keep_max(dve, 2 * UNITS - 1, 1, pair[0])

        def reduce_tile(dve, g, qb, n, tile):
            dve.wait_ge(s_ready, NS * g + n + 1)
            nc.vector.tensor_reduce(rowmax[qb][:, n:n + 1], tile[:], AX.X, ALU.max).then_inc(s_reduced, 1)

        def keep_max(dve, g, qb, tile):
            dve.wait_ge(max_turned, g + 3)
            dve.wait_ge(max_ready, g + 1)
            nc.vector.tensor_copy(max_full[qb][:], tile[0:NS, 0:P]).then_inc(max_kept, 1)

        def attend_scalar(act):
            for qb in range(2):
                act.sem_inc(o_stored[qb], 16)

            def copy_o(u, qb):
                act.wait_ge(pv_done, STEPS * u + QT * (qb + 1))
                act.wait_ge(o_stored[qb], 16 * u + 16)
                nc.scalar.activation(o_sb[qb][:], bank(7), ACT.Copy).then_inc(o_copied, 1)

            def emit(u, buf, _):
                first = known(u, 0)
                for s in range(STEPS):
                    if not (first and s < 2):
                        act.wait_ge(pv_done, STEPS * u + s - 1)
                    for h in range(REP):
                        n = REP * s + h
                        act.wait_ge(st_ready, REP * STEPS * u + n + 1)
                        nc.scalar.activation(probs[s % 2][:, h, :], bank(4 + (buf + n) % 3), ACT.Exp).then_inc(exp_done, 1)
                        if s == 0 and h == 2 and not first:
                            copy_o(u - 1, 1)
                        if s == QT and h == 2:
                            copy_o(u, 0)

            by_units(act, emit)
            copy_o(UNITS - 1, 1)

        heads = o_raw.rearrange("u (h r) n -> (u h) r n", h=REP)

        def load_den(eng, b):
            for qb in range(2):
                eng.wait_ge(o_stored[qb], 16 * NG * (b + 1) + 16)
            eng.dma_start(den_c[b][:], heads[b * NH:(b + 1) * NH, HD, :].rearrange("h (j n) -> h j n", j=P // NH))\
               .then_inc(den_loaded, 16)

        def store_inv(eng, b):
            eng.wait_ge(den_inv, b + 1)
            eng.dma_start(inv_den[b * NH:(b + 1) * NH, :].rearrange("h (j n) -> h j n", j=P // NH), den_c[b][:])\
               .then_inc(inv_stored, 16)

        def invert_den(dve, b):
            dve.wait_ge(den_loaded, 16 * (b + 1))
            nc.vector.reciprocal(den_c[b][:], den_c[b][:]).then_inc(den_inv, 1)

        def load_mix(sp, b, k):
            if b > 0:
                sp.wait_ge(y_done, BT * (NB * (b - 1) + k) + 3 * BT)
            sp.wait_ge(inv_stored, 16 * b + 16)
            for c in range(HC):
                rows = slice(b * NH + 8 * c, b * NH + 8 * c + 8)
                tok = slice(k * BLK, (k + 1) * BLK)
                sp.dma_start(num[k][:, c, :], heads[rows, 0:HD, tok]).then_inc(nd_loaded[k], 16)
                sp.dma_start(inv[k][:, c, :], inv_den[rows, tok].rearrange("h (a n) -> h a n", a=1).broadcast_to([8, HD, BLK]))\
                  .then_inc(nd_loaded[k], 16)
            blk = NB * b + k
            if b > 0:
                sp.wait_ge(pre_done, BT * (NB * (b - 1) + k) + 3 * BT)
            sp.dma_start(x_res[k][:], xf[blk * BLK:(blk + 1) * BLK, :].rearrange("(t p) h -> p t h", p=P))\
              .then_inc(res_loaded[k], 16)

        def mix_sync(sp):
            load_den(sp, 1)
            store_inv(sp, 1)
            for k in range(2):
                load_mix(sp, 1, k)

        ND = 16 * HC * 2

        def mix_piece(pool, b, i):
            k, i = i // (HC + BT), i % (HC + BT)
            if i < HC:
                pool.wait_ge(nd_loaded[k], ND * b + ND)
                nc.gpsimd.tensor_tensor(num[k][:, i, :], num[k][:, i, :], inv[k][:, i, :], ALU.mult).then_inc(mix_in, 1)
            else:
                pool.wait_ge(res_loaded[k], 16 * b + 16)
                pool.wait_ge(w2_loaded, 80)
                nc.gpsimd.tensor_tensor(x_res[k][:, i - HC, :], x_res[k][:, i - HC, :], bo_bc[:], ALU.add).then_inc(res_ready, 1)

        def mix_pool(pool):
            for i in range(2 * (HC + BT)):
                mix_piece(pool, 1, i)

        def mix_tensor(pe):
            pe.sem_inc(y_done, 2 * BT)
            pe.wait_ge(o_copied, 2 * UNITS)
            pe.wait_ge(gw_ready, 1)

            def project_tile(blk, k, t):
                pe.wait_ge(pre_done, BT * blk + t + 2 * BT - 1)
                for c in range(HC):
                    last = nc.tensor.matmul(bank(t % 2), num[k][:, c, t * P:(t + 1) * P], Wo_sb[:, c, :],
                                            start=(c == 0), stop=(c == HC - 1))
                last.then_inc(y_done, 1)

            def turn_tile(blk, k, t):
                pe.wait_ge(x1_done, BT * blk + t + 1)
                pe.wait_ge(x1T_kept, BT * blk + t + 1)
                for c in range(HC):
                    last = nc.tensor.transpose(bank(2 + t % 2)[:, c * P:(c + 1) * P], x1_out[k][:, t, c * P:(c + 1) * P], ident[:])
                last.then_inc(x1_turned, 1)

            def logit_tile(b, t):
                pe.wait_ge(x1T_kept, 2 * BT * b + t + 3)
                if t == 0:
                    pe.wait_ge(logit_kept, b + 1)
                for c in range(HC):
                    last = nc.tensor.matmul(bank(4)[:, t * E:(t + 1) * E], x1T[t // BT][:, c, t % BT * P:(t % BT + 1) * P],
                                            gwT[:, c, :], start=(c == 0), stop=(c == HC - 1))
                if t == 2 * BT - 1:
                    last.then_inc(logit_done, 1)

            with pe.Fori(0, NB) as b:
                def project_next(t):
                    blk = 2 * b + t // BT
                    if t % BT == 0:
                        pe.wait_ge(mix_in, HC * blk + HC)
                    project_tile(blk, t // BT, t % BT)

                project_next(0)
                project_next(1)
                for t in range(2 * BT):
                    if t + 2 < 2 * BT:
                        project_next(t + 2)
                    turn_tile(2 * b + t // BT, t // BT, t % BT)
                    if t > 0:
                        logit_tile(b, t - 1)
                logit_tile(b, 2 * BT - 1)

        def mix_vector(dve):
            dve.sem_inc(pre_done, 2 * BT)
            dve.sem_inc(logit_kept, 1)
            invert_den(dve, 1)
            with dve.Fori(0, NB) as b:
                for k in range(2):
                    blk = 2 * b + k
                    dve.wait_ge(res_ready, BT * blk + BT)
                    dve.wait_ge(x1_stored[k], 16 * b + 16)
                    for t in range(BT):
                        n = BT * blk + t
                        dve.wait_ge(y_done, n + 2 * BT + 1)
                        nc.vector.tensor_tensor(pre1[t % 2][:], bank(t % 2), x_res[k][:, t, :], ALU.add).then_inc(pre_done, 1)
                        dve.wait_ge(pre_done, n + 2 * BT + 1)
                        nc.vector.bn_stats(stats1[t % 2][:], pre1[t % 2][:]).then_inc(stats_done, 1)
                        dve.wait_ge(stats_done, n + 1)
                        settle(dve)
                        nc.vector.bn_aggr(mv1[t % 2][:], stats1[t % 2][:]).then_inc(mv_done, 1)
                        dve.wait_ge(std_done, n + 1)
                        nc.vector.reciprocal(std1[t % 2][:, 1:2], std1[t % 2][:, 0:1]).then_inc(inv_done, 1)
                        dve.wait_ge(inv_done, n + 1)
                        nc.vector.tensor_scalar(x1_out[k][:, t, :], pre1[t % 2][:], mv1[t % 2][:, 0:1], std1[t % 2][:, 1:2],
                                                ALU.subtract, ALU.mult).then_inc(x1_done, 1)
                dve.wait_ge(logit_done, b + 1)
                nc.vector.tensor_copy(logits[:, bass.ds(2 * BT * b, 2 * BT), :],
                                      bank(4)[:, 0:2 * BT * E].rearrange("p (t e) -> p t e", t=2 * BT)).then_inc(logit_kept, 1)

        def mix_scalar(act):
            act.sem_inc(x1T_kept, 2)
            for k in range(2):
                act.sem_inc(x1_stored[k], 16)
                act.sem_inc(x1T_stored[k], 16)
            act.wait_ge(consts_made, 5)
            with act.Fori(0, NB) as b:
                for k in range(2):
                    blk = 2 * b + k

                    def std(t):
                        n = BT * blk + t
                        act.wait_ge(mv_done, n + 1)
                        nc.scalar.activation(std1[t % 2][:, 0:1], mv1[t % 2][:, 1:2], ACT.Sqrt, bias=eps_col[:],
                                             scale=1.0).then_inc(std_done, 1)

                    def keep(t):
                        n = BT * blk + t
                        act.wait_ge(x1_turned, n + 1)
                        if t == 0:
                            act.wait_ge(x1T_stored[k], 16 * b + 16)
                        nc.scalar.activation(x1T[k][:, :, t * P:(t + 1) * P],
                                             bank(2 + t % 2).rearrange("p (c n) -> p c n", c=HC), ACT.Copy).then_inc(x1T_kept, 1)

                    std(0)
                    for t in range(BT):
                        if t + 1 < BT:
                            std(t + 1)
                        keep(t)
                    act.wait_ge(x1_done, BT * blk + BT)
                    act.dma_start(x1_rows[bass.ds(blk * BLK, BLK), :].rearrange("(t p) h -> p t h", p=P),
                                  x1_out[k][:]).then_inc(x1_stored[k], 16)
                    act.wait_ge(x1T_kept, BT * blk + BT + 2)
                    act.dma_start(x1T_blocks[bass.ds(blk, 1), :, :].rearrange("a p n -> (a p) n"),
                                  x1T[k][:].rearrange("p c n -> p (c n)")).then_inc(x1T_stored[k], 16)

        def route_pool(pool):
            pool.wait_ge(pv_done, STEPS * UNITS)
            pool.wait_ge(mix_in, HC * NBLK)
            nc.gpsimd.memset(seg8[:], 1.0).then_inc(rp_step, 1)
            nc.gpsimd.memset(seg32[:], 1.0).then_inc(rp_step, 1)
            nc.gpsimd.memset(seg16[:], 1.0).then_inc(rp_step, 1)
            nc.gpsimd.memset(all_ones[:], 1.0).then_inc(rp_step, 1)
            pool.wait_ge(rp_step, 4)
            nc.gpsimd.memset(seg8[:, :, 0:1], 0.0).then_inc(r_consts, 1)
            nc.gpsimd.memset(seg32[:, :, 0:1], 0.0).then_inc(r_consts, 1)
            nc.gpsimd.memset(seg16[:, :, 0:1], 0.0).then_inc(r_consts, 1)
            nc.gpsimd.affine_select(out=before[:], in_=all_ones[:], compare_op=ALU.is_gt, fill=0.0, base=0,
                                    pattern=[[1, P]], channel_multiplier=-1).then_inc(r_consts, 1)
            nc.gpsimd.iota(iota_c[:], pattern=[[0, TT], [1, C]], base=0, channel_multiplier=0,
                           allow_small_or_imprecise_dtypes=True).then_inc(r_consts, 1)
            nc.gpsimd.iota(facts[:, :, :, 0:1], pattern=[[0, E], [0, TT], [0, 1]], base=0, channel_multiplier=1,
                           allow_small_or_imprecise_dtypes=True).then_inc(r_consts, 1)
            nc.gpsimd.iota(facts[:, :, :, 1:2], pattern=[[0, E], [1, TT], [0, 1]], base=0, channel_multiplier=0,
                           allow_small_or_imprecise_dtypes=True).then_inc(r_consts, 1)
            nc.gpsimd.memset(facts[:, :, :, 5:6], 1.0).then_inc(r_consts, 1)
            nc.gpsimd.iota(spare_row[:], pattern=[[0, 1]], base=T, channel_multiplier=1,
                           allow_small_or_imprecise_dtypes=True).then_inc(r_consts, 1)
            nc.gpsimd.memset(zero_rows[:], 0.0).then_inc(spare_zero, 1)
            pool.wait_ge(spare_zero, 1)
            pool.dma_start(total[T:T + C, :], zero_rows[:]).then_inc(spare_stored, 16)

        def route_vector(dve):
            count = [0]

            def link(ins):
                count[0] += 1
                ins.then_inc(r_step, 1)
                dve.wait_ge(r_step, count[0])

            def bc(ap, n):
                return ap.rearrange("p (t a) -> p t a", a=1).broadcast_to([P, TT, n])

            def choose(dst, values, width, nth, seg):
                for t in range(TT):
                    last = nc.vector.max(out=top8[:, t, :], in_=values[:, t, :])
                link(last)
                thr = top8[:, :, nth - 1:nth].broadcast_to([P, TT, width])
                gt, eq, cum = r_gt[:, :, 0:width], r_eq[:, :, 0:width], r_cum[:, :, 0:width]
                if width < E:
                    flat = lambda x: x[:].rearrange("p t e -> p (t e)")[:, 0:TT * width].rearrange("p (t e) -> p t e", t=TT)
                    gt, eq, cum = flat(r_gt), flat(r_eq), flat(r_cum)
                link(nc.vector.tensor_tensor(gt, values[:], thr, ALU.is_gt))
                link(nc.vector.tensor_tensor(eq, values[:], thr, ALU.is_equal))
                link(nc.vector.tensor_reduce(n_gt[:], gt, AX.X, ALU.add))
                link(nc.vector.tensor_tensor_scan(cum.rearrange("p t e -> p (t e)"), seg[:].rearrange("p t e -> p (t e)"),
                                                  eq.rearrange("p t e -> p (t e)"), 0.0, ALU.mult, ALU.add))
                link(nc.vector.tensor_tensor(cum, cum, bc(n_gt[:], width), ALU.add))
                link(nc.vector.tensor_scalar(cum, cum, float(nth), None, ALU.is_le))
                link(nc.vector.tensor_tensor(cum, cum, eq, ALU.mult))
                link(nc.vector.tensor_tensor(dst, cum, gt, ALU.add))

            dve.wait_ge(logit_kept, NB + 1)
            dve.wait_ge(r_consts, 9)
            link(nc.vector.tensor_reduce(gmax[:].rearrange("p t g -> p (t g)"),
                                         logits[:].rearrange("p t (g e) -> p (t g) e", g=G), AX.X, ALU.max))
            choose(keep_g[:], gmax, G, TG, seg8)
            link(nc.vector.tensor_tensor(masked[:].rearrange("p t (g e) -> p (t g) e", g=G),
                                         logits[:].rearrange("p t (g e) -> p (t g) e", g=G),
                                         keep_g[:].rearrange("p t (g a) -> p (t g) a", a=1).broadcast_to([P, TT * G, E // G]),
                                         ALU.mult))
            choose(sel[:], masked, E, K, seg32)
            nc.vector.tensor_copy(sel_bf[:], sel[:]).then_inc(sel_ready, 1)
            link(nc.vector.tensor_tensor(masked[:], masked[:], top8[:, :, 0:1].broadcast_to([P, TT, E]), ALU.subtract))
            nc.vector.tensor_copy(r_eq[:, 0, 0:1], r_gt[:, 0, 0:1]).then_inc(r_diff, 1)
            shared_hidden(dve, 0, 0)
            dve.wait_ge(r_exp, 1)
            link(nc.vector.tensor_reduce(zsum[:], weight[:], AX.X, ALU.add))
            link(nc.vector.reciprocal(zsum[:], zsum[:]))
            link(nc.vector.tensor_tensor(weight[:], weight[:], bc(zsum[:], E), ALU.mult))
            link(nc.vector.scalar_tensor_tensor(out=weight[:], in0=weight[:], scalar=SCALE, in1=sel[:],
                                                op0=ALU.mult, op1=ALU.mult))
            wT = weight[:].rearrange("p t e -> p e t")
            restT = r_gt[:].rearrange("p t e -> p e t")
            link(nc.vector.tensor_copy(facts[:, :, :, 2], wT))
            link(nc.vector.tensor_tensor(restT, wT, facts[:, :, :, 2], ALU.subtract))
            link(nc.vector.tensor_copy(facts[:, :, :, 3], restT))
            link(nc.vector.tensor_tensor(facts[:, :, :, 4], restT, facts[:, :, :, 3], ALU.subtract))
            dve.wait_ge(counts_done, 1)
            cnt = bank(7).rearrange("p (t e) -> p e t", t=TT)
            link(nc.vector.tensor_copy(tile_count[:], cnt))
            link(nc.vector.tensor_tensor_scan(tile_cum[:].rearrange("p e t -> p (e t)"), seg16[:].rearrange("p e t -> p (e t)"),
                                              tile_count[:].rearrange("p e t -> p (e t)"), 0.0, ALU.mult, ALU.add))
            link(nc.vector.tensor_tensor(tile_cum[:], tile_cum[:], tile_count[:], ALU.subtract))
            dve.wait_ge(pos_done, 1)
            link(nc.vector.tensor_tensor(tile_cum[:], bank(6).rearrange("p (t e) -> p e t", t=TT), tile_cum[:], ALU.add))
            link(nc.vector.scalar_tensor_tensor(out=tile_cum[:], in0=tile_cum[:], scalar=1.0,
                                                in1=sel[:].rearrange("p t e -> p e t"), op0=ALU.add, op1=ALU.mult))
            nc.vector.tensor_scalar(slot_of[:], tile_cum[:], -1.0, None, ALU.add).then_inc(facts_ready, 1)
            dve.wait_ge(facts_ready, 1)

        def route_scalar(act):
            shared_silu(act, 0, 0)
            act.wait_ge(r_diff, 1)
            act.wait_ge(r_step, 20)
            nc.scalar.activation(weight[:], masked[:], ACT.Exp).then_inc(r_exp, 1)

        def route_tensor(pe):
            pe.wait_ge(sel_ready, 1)
            chosen = sel_bf[:].rearrange("p t e -> p (t e)")
            nc.tensor.matmul(bank(7), all_ones[:], chosen, start=True, stop=True).then_inc(counts_done, 1)
            nc.tensor.matmul(bank(6), before[:], chosen, start=True, stop=True).then_inc(pos_done, 1)

        def shared_sync(sp):
            def load_T(blk):
                sp.wait_ge(s_up, NSF * blk + 1)
                sp.wait_ge(x1T_stored[blk % 2], 16 * (blk // 2) + 32)
                sp.dma_start(sx[blk % 2][:].rearrange("p c n -> p (c n)"), x1T_blocks[blk]).then_inc(sx_loaded[blk % 2], 16)

            def load_rows(blk):
                sp.wait_ge(s_added, BT * blk + BT)
                sp.dma_start(sx_rows[:], x1_rows[blk * BLK:(blk + 1) * BLK, :].rearrange("(t p) h -> p t h", p=P))\
                  .then_inc(sx1_loaded, 16)

            sp.wait_ge(mix_in, HC * NBLK)
            sp.wait_ge(pre_done, BT * (NBLK + 1))
            load_T(0)
            load_T(1)
            sp.wait_ge(logit_done, NB)
            sp.wait_ge(x1_done, TT)
            for k in range(2):
                sp.wait_ge(x1_stored[k], 16 * (NB + 1))
                sp.wait_ge(x1T_stored[k], 16 * (NB + 1))
            load_rows(0)
            for e in range(2):
                load_wgu(sp, e, e)
                load_wd(sp, e, e)
            for blk in range(1, NBLK):
                if blk > 1:
                    load_T(blk)
                load_rows(blk)

        def shared_tensor(pe):
            pe.wait_ge(x1T_kept, TT + 2)
            pe.wait_ge(pre_done, TT + 2 * BT)

            def gate_up(blk, f):
                k = blk % 2
                f0, fn = SFT[f]
                if f == 0:
                    pe.wait_ge(sx_loaded[k], 16 * (blk // 2) + 16)
                pe.wait_ge(s_hidden, NSF * blk + f + 1)
                for dst, off, done in ((bank(f % 2), 0, s_gate), (bank(2 + f % 2), SI, s_up)):
                    for c in range(HC):
                        last = nc.tensor.matmul(dst[0:fn, :], wsgu[:, c, off + f0:off + f0 + fn], sx[k][:, c, :],
                                                start=(c == 0), stop=(c == HC - 1))
                    last.then_inc(done, 1)
                if blk == 0 and f == 1:
                    route_tensor(pe)
                for e in table_experts(NSF * blk + f):
                    slot_table(pe, e)

            for blk in range(NBLK):
                for f in range(0 if blk == 0 else 1, NSF):
                    gate_up(blk, f)
                if blk + 1 < NBLK:
                    gate_up(blk + 1, 0)
                pe.wait_ge(s_hidden, NSF * blk + NSF + 2)
                for t in range(BT):
                    pe.wait_ge(s_added, BT * blk + t + BT - 1)
                    for f, (f0, fn) in enumerate(SFT):
                        last = nc.tensor.matmul(bank(4 + t % 2), s_hid[0:fn, f, t * P:(t + 1) * P], wsd[0:fn, f, :],
                                                start=(f == 0), stop=(f == NSF - 1))
                    last.then_inc(s_down, 1)

        def table_experts(step):
            n = SLOT_EXPERTS * (step - FIRST_TABLE_STEP)
            return range(n, n + SLOT_EXPERTS) if 0 <= n < E else ()

        TABLES_MADE = FIRST_TABLE_STEP + E // SLOT_EXPERTS

        def slot_table(pe, e):
            pe.wait_ge(hot_ready, e + 1)
            for t in range(TT):
                last = nc.tensor.matmul(bank(6)[0:C, 6 * e:6 * e + 6], onehot[e % 2][:, t, :], facts[:, e, t, :],
                                        start=(t == 0), stop=(t == TT - 1))
            last.then_inc(table_done, 1)

        def onehots(dve, e):
            dve.wait_ge(table_done, e + 1)
            col = slot_of[:, e, :].rearrange("p (t c) -> p t c", c=1)
            nc.vector.tensor_tensor(onehot[e % 2][:], iota_c[:], col.broadcast_to([P, TT, C]), ALU.is_equal)\
              .then_inc(hot_ready, 1)

        def shared_silu(act, blk, f):
            fn = SFT[f][1]
            act.wait_ge(s_gate, NSF * blk + f + 1)
            act.wait_ge(s_hidden, NSF * blk + f + 1)
            nc.scalar.activation(s_sig[f % 2][0:fn, :], bank(f % 2)[0:fn, :], ACT.Silu).then_inc(s_silu, 1)

        def shared_scalar(act):
            for blk in range(NBLK):
                for f in range(NSF):
                    if blk > 0 or f > 0:
                        shared_silu(act, blk, f)
                act.wait_ge(s_added, BT * blk + 2 * BT)
                act.dma_start(total[blk * BLK:(blk + 1) * BLK, :].rearrange("(t p) h -> p t h", p=P),
                              s_sum[blk % 2][:]).then_inc(s_stored[blk % 2], 16)

        def shared_hidden(dve, blk, f):
            fn = SFT[f][1]
            dve.wait_ge(s_silu, NSF * blk + f + 1)
            dve.wait_ge(s_up, NSF * blk + f + 2 * NSF + 1)
            if f == 0:
                dve.wait_ge(s_down, BT * blk + BT)
            nc.vector.tensor_tensor(s_hid[0:fn, f, :], s_sig[f % 2][0:fn, :], bank(2 + f % 2)[0:fn, :],
                                    ALU.mult).then_inc(s_hidden, 1)

        def shared_vector(dve):
            for blk in range(NBLK):
                k = blk % 2
                for f in range(NSF):
                    step = NSF * blk + f
                    if step == TABLES_MADE + 1:
                        slot_rows(dve)
                    for e in table_experts(step + 1) if f < NSF - 1 else ():
                        onehots(dve, e)
                    if step > 0:
                        shared_hidden(dve, blk, f)
                    if f == NSF - 1:
                        for e in table_experts(step + 1):
                            onehots(dve, e)
                dve.wait_ge(sx1_loaded, 16 * blk + 16)
                dve.wait_ge(s_stored[k], 16 * (blk // 2) + 16)
                for t in range(BT):
                    dve.wait_ge(s_down, BT * blk + t + BT + 1)
                    nc.vector.tensor_tensor(s_sum[k][:, t, :], bank(4 + t % 2), sx_rows[:, t, :], ALU.add).then_inc(s_added, 1)

        def slot_rows(dve):
            dve.wait_ge(table_done, E + 2)
            nc.vector.tensor_copy(table[:], bank(6)[0:C, 0:6 * E].rearrange("p (e s) -> p e s", s=6)).then_inc(table_kept, 1)
            count = [0]

            def link(ins):
                count[0] += 1
                ins.then_inc(slots_ready, 1)
                dve.wait_ge(slots_ready, count[0])

            dve.wait_ge(table_kept, 1)
            link(nc.vector.tensor_tensor(slot_w[:], table[:, :, 2], table[:, :, 3], ALU.add))
            link(nc.vector.tensor_tensor(slot_w[:], slot_w[:], table[:, :, 4], ALU.add))
            link(nc.vector.scalar_tensor_tensor(out=slot_src[:], in0=table[:, :, 1], scalar=float(P), in1=table[:, :, 0],
                                                op0=ALU.mult, op1=ALU.add))
            link(nc.vector.tensor_copy(slot_src_i[:], slot_src[:]))
            link(nc.vector.tensor_scalar(table[:, :, 5], table[:, :, 5], -1.0, 1.0, ALU.mult, ALU.add))
            link(nc.vector.scalar_tensor_tensor(out=slot_src[:], in0=table[:, :, 5], scalar=spare_row[:, 0:1], in1=slot_src[:],
                                                op0=ALU.mult, op1=ALU.add))
            link(nc.vector.tensor_copy(slot_dst_i[:], slot_src[:]))

        SLOT_STEPS = 7

        def load_wgu(sp, e, k):
            src = w_gate_up[e] if isinstance(e, int) else w_gate_up[bass.ds(e, 1), :, :].rearrange("a k n -> (a k) n")
            sp.dma_start(wgu[k][:], src.rearrange("(c p) n -> p c n", p=P)).then_inc(wgu_loaded[k], 16)

        def load_wd(sp, e, k):
            src = w_down[e] if isinstance(e, int) else w_down[bass.ds(e, 1), :, :].rearrange("a k n -> (a k) n")
            sp.dma_start(wd[k][:, 0:2, :], src[0:2 * P, :].rearrange("(c p) n -> p c n", p=P)).then_inc(wd_loaded[k], 16)
            sp.dma_start(wd[k][0:FT[2][1], 2, :], src[2 * P:I, :]).then_inc(wd_loaded[k], 16)

        def by_rounds(eng, emit):
            rounds = E // GR
            for k in range(GR):
                emit(k, k, 0)
            with eng.Fori(1, rounds - 1) as r:
                for k in range(GR):
                    emit(GR * r + k, k, r)
            for k in range(GR):
                emit(E - GR + k, k, rounds - 1)

        def experts_sync(sp):
            def emit(e, k, r):
                if known(e, 0, 1):
                    return
                if not known(e, 2, 3):
                    sp.wait_ge(e_up, e - GR + 1)
                load_wgu(sp, e, k)
                if not known(e, 2, 3):
                    sp.wait_ge(e_down, e - GR + 1)
                load_wd(sp, e, k)

            sp.wait_ge(s_up, NSF * (NBLK + 2))
            sp.wait_ge(s_hidden, NSF * NBLK + 2)
            sp.wait_ge(s_down, TT + BT)
            sp.wait_ge(s_added, TT + BT)
            for k in range(2):
                sp.wait_ge(s_stored[k], 16 * (NB + 1))
            by_rounds(sp, emit)

        def experts_pool(pool):
            pool.wait_ge(slots_ready, SLOT_STEPS)
            for k in range(2):
                pool.wait_ge(x1_stored[k], 16 * (NB + 1))

            def col(a, e):
                return a[:, e:e + 1] if isinstance(e, int) else a[:, bass.ds(e, 1)]

            def gather(e, k):
                if not known(e, *range(GR)):
                    pool.wait_ge(xg_turned, e - GR + 1)
                settle(pool)
                nc.gpsimd.tensor_copy(src_i[k][:], col(slot_src_i, e)).then_inc(src_ready, 1)
                pool.wait_ge(src_ready, e + 1)
                settle(pool)
                pool.indirect_dma_start(xg[k][:], None, x1_rows, bass.IndirectOffsetOnAxis(ap=src_i[k][:, 0:1], axis=0))\
                    .then_inc(gathered[k], 16)

            def columns(e, k):
                if not known(e, *range(GR)):
                    pool.wait_ge(e_scaled, e - GR + 1)
                    pool.wait_ge(scattered, 16 * (e - GR + 1))
                settle(pool)
                nc.gpsimd.tensor_copy(dst_i[k][:], col(slot_dst_i, e)).then_inc(cols_ready, 1)
                nc.gpsimd.tensor_copy(w_col[k][:], col(slot_w, e)).then_inc(cols_ready, 1)

            def add(e, k):
                pool.wait_ge(e_scaled, e + 1)
                pool.wait_ge(cols_ready, 2 * e + 2)
                if not known(e, 0):
                    pool.wait_ge(scattered, 16 * e)
                settle(pool)
                pool.indirect_dma_start(total, bass.IndirectOffsetOnAxis(ap=dst_i[k][:, 0:1], axis=0), e_out[k % 2][:], None,
                                        compute_op=ALU.add).then_inc(scattered, 16)

            def emit(e, k, r):
                if not known(e, *range(E - GR, E)):
                    gather(e + GR, k)
                add(e, k)
                if not known(e, 0, *range(E - GR + 1, E)):
                    columns(e + GR - 1, (k - 1) % GR)

            for e in range(GR):
                gather(e, e)
                columns(e, e)
            for k in range(2):
                pool.wait_ge(s_stored[k], 16 * (NB + 1))
            pool.wait_ge(spare_stored, 16)
            by_rounds(pool, emit)

        def experts_tensor(pe):
            pe.wait_ge(s_added, TT + BT)
            pe.wait_ge(s_hidden, NSF * NBLK + 2)
            pe.wait_ge(table_kept, 1)

            def turn(e, k, r):
                pe.wait_ge(gathered[k], 16 * (r + 1))
                if not known(e, 0):
                    pe.wait_ge(xgT_ready, e)
                for c in range(HC):
                    last = nc.tensor.transpose(bank(0)[:, c * C:(c + 1) * C], xg[k][:, c * P:(c + 1) * P], ident[0:C, 0:C])
                last.then_inc(xg_turned, 1)

            def up(e, k, r):
                pe.wait_ge(xgT_ready, e + 1)
                pe.wait_ge(wgu_loaded[k], 16 * (r + 1))
                if not known(e, 0, 1):
                    pe.wait_ge(e_hidden, 2 * (e - 1))
                for b0, off in ((1 + k % 2, 0), (3 + k % 2, I)):
                    for f, (f0, fn) in enumerate(FT):
                        for c in range(HC):
                            last = nc.tensor.matmul(bank(b0)[0:fn, f * C:(f + 1) * C], wgu[k][:, c, off + f0:off + f0 + fn],
                                                    xgT[k % 2][:, c, :], start=(c == 0), stop=(c == HC - 1))
                last.then_inc(e_up, 1)

            def down(e, k, r):
                pe.wait_ge(e_hidden, 2 * (e + 1))
                pe.wait_ge(wd_loaded[k], 32 * (r + 1))
                if not known(e, 0, 1):
                    pe.wait_ge(e_scaled, e - 1)
                for f, (f0, fn) in enumerate(FT):
                    last = nc.tensor.matmul(bank(5 + k % 2)[0:C, :], e_hid[k % 2][0:fn, f, :], wd[k][0:fn, f, :],
                                            start=(f == 0), stop=(f == len(FT) - 1))
                last.then_inc(e_down, 1)

            def ahead(step, e, k, r, n):
                step(e + n, (k + n) % GR, r + (k + n) // GR)

            def emit(e, k, r):
                if not known(e, E - 1):
                    ahead(up, e, k, r, 1)
                if not known(e, E - 2, E - 1):
                    ahead(turn, e, k, r, 2)
                down(e, k, r)

            turn(0, 0, 0)
            up(0, 0, 0)
            turn(1, 1, 0)
            by_rounds(pe, emit)

        def experts_scalar(act):
            def copy_T(e, k, r):
                act.wait_ge(xg_turned, e + 1)
                if not known(e, 0, 1):
                    act.wait_ge(e_up, e - 1)
                nc.scalar.activation(xgT[k % 2][:], bank(0)[:, 0:HC * C].rearrange("p (c n) -> p c n", c=HC), ACT.Copy)\
                  .then_inc(xgT_ready, 1)

            def silu(e, k, r):
                act.wait_ge(e_up, e + 1)
                if not known(e, 0, 1):
                    act.wait_ge(e_hidden, 2 * (e - 1))
                nc.scalar.activation(e_sig[k % 2][:, 0:2, :], bank(1 + k % 2)[:, 0:2 * C].rearrange("p (f n) -> p f n", f=2),
                                     ACT.Silu).then_inc(e_silu, 1)
                nc.scalar.activation(e_sig[k % 2][0:FT[2][1], 2, :], bank(1 + k % 2)[0:FT[2][1], 2 * C:3 * C],
                                     ACT.Silu).then_inc(e_silu, 1)

            def emit(e, k, r):
                silu(e, k, r)
                if not known(e, E - 1):
                    copy_T(e + 1, (k + 1) % GR, r)

            copy_T(0, 0, 0)
            by_rounds(act, emit)

        def experts_vector(dve):
            def hidden(e, k, r):
                dve.wait_ge(e_silu, 2 * e + 2)
                if not known(e, 0, 1):
                    dve.wait_ge(e_down, e - 1)
                nc.vector.tensor_tensor(e_hid[k % 2][:, 0:2, :], e_sig[k % 2][:, 0:2, :],
                                        bank(3 + k % 2)[:, 0:2 * C].rearrange("p (f n) -> p f n", f=2),
                                        ALU.mult).then_inc(e_hidden, 1)
                nc.vector.tensor_tensor(e_hid[k % 2][0:FT[2][1], 2, :], e_sig[k % 2][0:FT[2][1], 2, :],
                                        bank(3 + k % 2)[0:FT[2][1], 2 * C:3 * C], ALU.mult).then_inc(e_hidden, 1)

            def scale(e, k, r):
                dve.wait_ge(e_down, e + 1)
                dve.wait_ge(cols_ready, 2 * e + 2)
                if not known(e, 0, 1):
                    dve.wait_ge(scattered, 16 * (e - 1))
                nc.vector.tensor_scalar(e_out[k % 2][:], bank(5 + k % 2)[0:C, :], w_col[k][:, 0:1], None,
                                        ALU.mult).then_inc(e_scaled, 1)

            def emit(e, k, r):
                if not known(e, E - 1):
                    hidden(e + 1, (k + 1) % GR, r)
                scale(e, k, r)

            hidden(0, 0, 0)
            by_rounds(dve, emit)

        def piece_rows(a, n):
            return a[bass.ds(n * (FP * P), FP * P), :].rearrange("(t p) h -> p t h", p=P)

        def finish_sync(sp):
            sp.wait_ge(scattered, 16 * E)
            sp.wait_ge(s_added, TT + BT)
            with sp.Fori(0, NB) as b:
                for k in range(FR):
                    n = FR * b + k
                    sp.wait_ge(f_even, n + 1)
                    sp.wait_ge(f_odd, n + 1)
                    sp.dma_start(f_in[k][:], piece_rows(total, n)).then_inc(f_loaded[k], 16)
            for k in range(FR):
                sp.wait_ge(f_stored[k], 16 * (NB + 1))

        def finish_vector(dve):
            with dve.Fori(0, NB) as b:
                def stats(k):
                    n = FR * b + k
                    dve.wait_ge(f_loaded[k], 16 * b + 16)
                    for t in range(FP):
                        nc.vector.bn_stats(stats2[k % 2][:, t, :], f_in[k][:, t, :]).then_inc(f_stats, 1)
                    dve.wait_ge(f_stats, FP * n + FP)
                    settle(dve)
                    for t in range(FP):
                        nc.vector.bn_aggr(mv2[k % 2][:, t, :], stats2[k % 2][:, t, :]).then_inc(f_mv, 1)

                stats(0)
                for k in range(FR):
                    n = FR * b + k
                    if k + 1 < FR:
                        stats(k + 1)
                    dve.wait_ge(f_std, n + 1)
                    dve.wait_ge(f_odd, n + FR - 1)
                    nc.vector.reciprocal(inv2[k % 2][:], std2[k % 2][:]).then_inc(f_inv, 1)
                    dve.wait_ge(f_inv, n + 1)
                    nc.vector.scalar_tensor_tensor(out=shift2[k % 2][:], in0=mv2[k % 2][:, :, 0:1], scalar=-1.0, in1=inv2[k % 2][:],
                                                   op0=ALU.mult, op1=ALU.mult).then_inc(f_shift, 1)
                    dve.wait_ge(f_stored[k], 16 * b + 16)
                    nc.vector.tensor_scalar(f_out[k][:, 0, :], f_in[k][:, 0, :], mv2[k % 2][:, 0, 0:1], inv2[k % 2][:, 0, :],
                                            ALU.subtract, ALU.mult).then_inc(f_even, 1)

        def finish_scalar(act):
            act.sem_inc(f_odd, FR)
            for k in range(FR):
                act.sem_inc(f_stored[k], 16)
            with act.Fori(0, NB) as b:
                def deviation(k):
                    n = FR * b + k
                    act.wait_ge(f_mv, FP * n + FP)
                    nc.scalar.activation(std2[k % 2][:], mv2[k % 2][:, :, 1:2], ACT.Sqrt, bias=eps_col[:], scale=1.0)\
                        .then_inc(f_std, 1)

                deviation(0)
                for k in range(FR):
                    n = FR * b + k
                    if k + 1 < FR:
                        deviation(k + 1)
                    act.wait_ge(f_shift, n + 1)
                    act.wait_ge(f_stored[k], 16 * b + 16)
                    nc.scalar.activation(f_out[k][:, 1, :], f_in[k][:, 1, :], ACT.Identity, bias=shift2[k % 2][:, 1, :],
                                         scale=inv2[k % 2][:, 1, :]).then_inc(f_odd, 1)
                    act.wait_ge(f_even, n + FR + 1)
                    act.wait_ge(f_odd, n + FR + 1)
                    act.dma_start(piece_rows(of, n), f_out[k][:]).then_inc(f_stored[k], 16)

        block = ctx.enter_context(nc.Block())

        @block.sync
        def _(sp):
            project_sync(sp)
            attend_sync(sp)
            mix_sync(sp)
            shared_sync(sp)
            experts_sync(sp)
            finish_sync(sp)

        @block.gpsimd
        def _(pool):
            project_pool(pool)
            attend_pool(pool)
            mix_pool(pool)
            route_pool(pool)
            experts_pool(pool)

        @block.tensor
        def _(pe):
            pe.sem_inc(v_done, 2)
            pe.sem_inc(max_turned, 2)
            project_tensor(pe)
            attend_tensor(pe)
            pe.sem_inc(s_up, 2 * NSF)
            pe.sem_inc(s_down, BT)
            pe.sem_inc(table_done, 2)
            mix_tensor(pe)
            shared_tensor(pe)
            experts_tensor(pe)

        @block.scalar
        def _(act):
            for k in range(2):
                act.sem_inc(parts_stored[k], 16)
            project_scalar(act)
            attend_scalar(act)
            mix_scalar(act)
            route_scalar(act)
            shared_scalar(act)
            experts_scalar(act)
            finish_scalar(act)

        @block.vector
        def _(dve):
            project_vector(dve)
            attend_vector(dve)
            mix_vector(dve)
            dve.sem_inc(s_hidden, 2)
            dve.sem_inc(s_added, BT)
            for k in range(2):
                dve.sem_inc(s_stored[k], 16)
            route_vector(dve)
            shared_vector(dve)
            experts_vector(dve)
            dve.sem_inc(f_even, FR)
            finish_vector(dve)


_INS = ["L0_attn_hidden_state", "L0_attn_Wq", "L0_attn_bq", "L0_attn_Wk", "L0_attn_bk", "L0_attn_Wv", "L0_attn_bv",
        "L0_attn_Wo", "L0_attn_bo", "L0_ffn_gate_w", "L0_ffn_w_gate_up", "L0_ffn_w_down", "L0_ffn_ws_gate_up",
        "L0_ffn_ws_down"]


def kernel(**inputs):
    import numpy as np
    import concourse.bacc as bacc
    from concourse.bass_utils import run_bass_kernel_spmd as run

    nc = bacc.Bacc("TRN2", target_bir_lowering=False, num_devices=1)
    arrays, args = {}, []
    for name in _INS:
        a = np.ascontiguousarray(inputs[name])
        arrays[f"in_{name}"] = a
        args.append(nc.dram_tensor(f"in_{name}", a.shape, mybir.dt.from_np(a.dtype), kind="ExternalInput").ap())
    args.append(nc.dram_tensor("out_0", (NB, SEQ, H), F32, kind="ExternalOutput").ap())
    build(nc, *args)
    return run(nc, [arrays], core_ids=[0]).results[0]["out_0"]
```
